# Optimizing a Trainium2 kernel written in Bass

```python
import numpy as np
import jax
import jax.numpy as jnp

def _softmax(x, axis=-1):
    return jax.nn.softmax(x, axis=axis)

def _gelu(x):
    return jax.nn.gelu(x, approximate=True)

def _silu(x):
    return jax.nn.silu(x)

def _sigmoid(x):
    return jax.nn.sigmoid(x)

def _layernorm(x, axis=-1, eps=1e-05):
    m = jnp.mean(x, axis=axis, keepdims=True)
    v = jnp.var(x, axis=axis, keepdims=True)
    return (x - m) / jnp.sqrt(v + eps)

def _scatter_add(tgt, idx, src, axis=0):
    return tgt.at[idx].add(src)

def _segment_sum(src, seg, n):
    return jax.ops.segment_sum(src, seg, n)
kernel_name = 'mk_decoder_postln_d1_seqx_r2_21c912'

def setup_inputs(seed: int=0):
    np.random.seed(seed)
    _w = jnp.asarray

    def _rec_inputs():
        import jax
        import jax.numpy as jnp
        _rk = jax.random.key(seed)
        x = 0.0002417 + 0.9998 * jax.random.normal(jax.random.fold_in(_rk, 1), (4, 2048, 512), jnp.float32)
        _lenS = 2048 - jax.random.randint(jax.random.fold_in(_rk, 7), (4,), 0, max(1, 2048 // 4) + 1, jnp.int32)
        _lenS2 = 154 - jax.random.randint(jax.random.fold_in(_rk, 8), (4,), 0, max(1, 154 // 4) + 1, jnp.int32)
        _ctx_1024P = jax.random.normal(jax.random.fold_in(_rk, 11), (4, 16, 512), jnp.float32)
        _ctx_1024c = jax.random.dirichlet(jax.random.fold_in(_rk, 511), 0.3 * jnp.ones((16,), jnp.float32), (4, 154))
        _ctx_1024t = jnp.einsum('bsk,bkd->bsd', _ctx_1024c, _ctx_1024P)
        _ctx_1024t = _ctx_1024t * jax.lax.rsqrt(jnp.mean(jnp.square(_ctx_1024t)) + 1e-12) * 0.953939
        ctx_1024 = 7.22013e-05 + 1.00017 * (_ctx_1024t + 0.3 * jax.random.normal(jax.random.fold_in(_rk, 611), (4, 154, 512), jnp.float32))
        _validS = jnp.arange(2048)[None, :] < _lenS[:, None]
        _validS2 = jnp.arange(154)[None, :] < _lenS2[:, None]
        _causal = jnp.tril(jnp.ones((2048, 2048), dtype=bool))
        mask_Bx1x1xS2_ik0 = jnp.where(jnp.broadcast_to(_validS2[:, None, None, :], (4, 1, 1, 154)), 0, 1).astype(jnp.int32)
        return (x, ctx_1024, mask_Bx1x1xS2_ik0)
    x, ctx_1024, mask_Bx1x1xS2_ik0 = _rec_inputs()

    def _L0_attn_setup():
        import jax, jax.numpy as jnp
        import numpy as np
        B, S, D = (4, 1024, 512)
        SCALE = 1.0 / np.sqrt(D)
        key = jax.random.key(seed)
        k1, k2, k3 = jax.random.split(key, 3)
        x = jax.random.normal(k1, (B, S, D), dtype=jnp.float32)
        bound = 1.0 / np.sqrt(D)
        W_qk = jax.random.uniform(k2, (D, D), minval=-bound, maxval=bound, dtype=jnp.float32)
        W_v = jax.random.uniform(k3, (D, D), minval=-bound, maxval=bound, dtype=jnp.float32)
        alibi_slope = jnp.full((1,), 0.5, dtype=jnp.float32)
        return {'x': x, 'W_qk': W_qk, 'W_v': W_v, 'alibi_slope': alibi_slope}
    _L0_attn_all = _L0_attn_setup()
    _L0_attn_in = {k: v for k, v in _L0_attn_all.items() if k in ('W_qk', 'W_v', 'alibi_slope')}
    del _L0_attn_all

    def _L0_xattn_setup():
        import jax, jax.numpy as jnp
        import numpy as np
        HEADS = 16
        NEG = -1e+20
        key = jax.random.key(seed)
        ks = jax.random.split(key, 8)
        N, S, E = (4, 1024, 512)
        inp = {'values': jax.random.normal(ks[0], (N, S, E), jnp.float32), 'keys': jax.random.normal(ks[1], (N, S, E), jnp.float32), 'query': jax.random.normal(ks[2], (N, S, E), jnp.float32), 'mask': jax.random.randint(ks[3], (N, 1, 1, S), 0, 2, jnp.int32), 'Wv': jax.random.normal(ks[4], (E, E), jnp.float32) * E ** (-0.5), 'Wk': jax.random.normal(ks[5], (E, E), jnp.float32) * E ** (-0.5), 'Wq': jax.random.normal(ks[6], (E, E), jnp.float32) * E ** (-0.5), 'Wo': jax.random.normal(ks[7], (E, E), jnp.float32) * E ** (-0.5)}
        return inp
    _L0_xattn_all = _L0_xattn_setup()
    _L0_xattn_in = {k: v for k, v in _L0_xattn_all.items() if k in ('Wv', 'Wk', 'Wq', 'Wo')}
    del _L0_xattn_all

    def _L0_ffn_setup():
        import jax, jax.numpy as jnp
        import numpy as np
        B, S, H, DV = (4, 2048, 512, 512)
        E, INNER, P, K = (8, 32, 8, 2)

        def _ln(v, g, b, eps=1e-05):
            m = jnp.mean(v, axis=-1, keepdims=True)
            var = jnp.var(v, axis=-1, keepdims=True)
            return (v - m) * jax.lax.rsqrt(var + eps) * g + b
        key = jax.random.key(seed)
        ks = jax.random.split(key, 8)
        sc = lambda d: 1.0 / np.sqrt(d)
        return {'x': jax.random.normal(ks[0], (B, S, H), jnp.float32), 'Wv': jax.random.normal(ks[1], (DV, H), jnp.float32) * sc(H), 'bv': jnp.zeros((DV,), jnp.float32), 'Wg': jax.random.normal(ks[2], (E, DV), jnp.float32) * sc(DV), 'bg': jnp.zeros((E,), jnp.float32), 'Wp': jax.random.normal(ks[3], (E, P, DV), jnp.float32) * sc(DV), 'alpha': jnp.zeros((), jnp.float32), 'g_r': jnp.ones((E,), jnp.float32), 'b_r': jnp.zeros((E,), jnp.float32), 'g_c': jnp.ones((E,), jnp.float32), 'b_c': jnp.zeros((E,), jnp.float32), 'W1': jax.random.normal(ks[4], (E, INNER, DV), jnp.float32) * sc(DV), 'b1': jnp.zeros((E, INNER), jnp.float32), 'W2': jax.random.normal(ks[5], (E, DV, INNER), jnp.float32) * sc(INNER), 'b2': jnp.zeros((E, DV), jnp.float32)}
    _L0_ffn_all = _L0_ffn_setup()
    _L0_ffn_in = {k: v for k, v in _L0_ffn_all.items() if k in ('Wv', 'bv', 'Wg', 'bg', 'Wp', 'alpha', 'g_r', 'b_r', 'g_c', 'b_c', 'W1', 'b1', 'W2', 'b2')}
    del _L0_ffn_all
    return {'x': x, 'ctx_1024': ctx_1024, 'mask_Bx1x1xS2_ik0': mask_Bx1x1xS2_ik0, 'L0_attn_W_qk': _L0_attn_in['W_qk'], 'L0_attn_W_v': _L0_attn_in['W_v'], 'L0_attn_alibi_slope': _L0_attn_in['alibi_slope'], 'L0_xattn_Wv': _L0_xattn_in['Wv'], 'L0_xattn_Wk': _L0_xattn_in['Wk'], 'L0_xattn_Wq': _L0_xattn_in['Wq'], 'L0_xattn_Wo': _L0_xattn_in['Wo'], 'L0_ffn_Wv': _L0_ffn_in['Wv'], 'L0_ffn_bv': _L0_ffn_in['bv'], 'L0_ffn_Wg': _L0_ffn_in['Wg'], 'L0_ffn_bg': _L0_ffn_in['bg'], 'L0_ffn_Wp': _L0_ffn_in['Wp'], 'L0_ffn_alpha': _L0_ffn_in['alpha'], 'L0_ffn_g_r': _L0_ffn_in['g_r'], 'L0_ffn_b_r': _L0_ffn_in['b_r'], 'L0_ffn_g_c': _L0_ffn_in['g_c'], 'L0_ffn_b_c': _L0_ffn_in['b_c'], 'L0_ffn_W1': _L0_ffn_in['W1'], 'L0_ffn_b1': _L0_ffn_in['b1'], 'L0_ffn_W2': _L0_ffn_in['W2'], 'L0_ffn_b2': _L0_ffn_in['b2']}

def reference(x, ctx_1024, mask_Bx1x1xS2_ik0, L0_attn_W_qk, L0_attn_W_v, L0_attn_alibi_slope, L0_xattn_Wv, L0_xattn_Wk, L0_xattn_Wq, L0_xattn_Wo, L0_ffn_Wv, L0_ffn_bv, L0_ffn_Wg, L0_ffn_bg, L0_ffn_Wp, L0_ffn_alpha, L0_ffn_g_r, L0_ffn_b_r, L0_ffn_g_c, L0_ffn_b_c, L0_ffn_W1, L0_ffn_b1, L0_ffn_W2, L0_ffn_b2):
    import jax
    import jax.numpy as jnp

    def _L0_attn_ref(x, W_qk, W_v, alibi_slope):
        import jax, jax.numpy as jnp
        import numpy as np
        B, S, D = (4, 1024, 512)
        SCALE = 1.0 / np.sqrt(D)
        seq_len = x.shape[1]
        scores = jnp.einsum('bqe,bke->bqk', x @ W_qk, x) * SCALE
        kpos = jnp.arange(seq_len, dtype=x.dtype)[None, :]
        qpos = jnp.arange(seq_len, dtype=x.dtype)[:, None]
        scores = scores + (kpos - qpos) * alibi_slope[0]
        causal = qpos >= kpos
        scores = jnp.where(causal, scores, -jnp.inf)
        attn = jax.nn.softmax(scores, axis=-1)
        v = x @ W_v.T
        return jnp.einsum('bqk,bkd->bqd', attn, v)

    def _L0_xattn_ref(values, keys, query, mask, Wv, Wk, Wq, Wo):
        import jax, jax.numpy as jnp
        import numpy as np
        HEADS = 16
        NEG = -1e+20
        N, Sq, E = query.shape
        H = HEADS
        D = E // H
        v = (values @ Wv.T).reshape(N, -1, H, D)
        k = (keys @ Wk.T).reshape(N, -1, H, D)
        q = (query @ Wq.T).reshape(N, Sq, H, D)
        scores = jnp.einsum('nqhd,nkhd->nhqk', q, k)
        scores = jnp.where(mask == 0, jnp.float32(NEG), scores)
        attn = jax.nn.softmax(scores / jnp.sqrt(jnp.float32(D)), axis=-1)
        out = jnp.einsum('nhqk,nkhd->nqhd', attn, v).reshape(N, Sq, E)
        return out @ Wo.T

    def _L0_ffn_ref(x, Wv, bv, Wg, bg, Wp, alpha, g_r, b_r, g_c, b_c, W1, b1, W2, b2):
        import jax, jax.numpy as jnp
        import numpy as np
        B, S, H, DV = (4, 2048, 512, 512)
        E, INNER, P, K = (8, 32, 8, 2)

        def _ln(v, g, b, eps=1e-05):
            m = jnp.mean(v, axis=-1, keepdims=True)
            var = jnp.var(v, axis=-1, keepdims=True)
            return (v - m) * jax.lax.rsqrt(var + eps) * g + b
        V = jnp.einsum('bsh,dh->bsd', x, Wv) + bv
        Vf = V.reshape(-1, DV)
        r = Vf @ Wg.T + bg
        pv = jnp.einsum('epd,nd->nep', Wp, Vf)
        c = jnp.sqrt(jnp.sum(pv * pv, axis=-1)) / np.sqrt(P)
        s = _ln(r, g_r, b_r) + jax.nn.sigmoid(alpha) * _ln(c, g_c, b_c)
        topv, sel = jax.lax.top_k(s, K)
        w = jax.nn.softmax(topv, axis=-1)
        delta = jnp.zeros_like(Vf)
        for e in range(E):
            h = jax.nn.silu(Vf @ W1[e].T + b1[e])
            out = h @ W2[e].T + b2[e]
            we = jnp.sum(jnp.where(sel == e, w, 0.0), axis=-1)
            delta = delta + out * we[:, None]
        return (Vf + delta).reshape(V.shape)
    x = _layernorm(x + _L0_attn_ref(x, L0_attn_W_qk, L0_attn_W_v, L0_attn_alibi_slope), axis=-1)
    x = _layernorm(x + _L0_xattn_ref(ctx_1024, ctx_1024, x, mask_Bx1x1xS2_ik0, L0_xattn_Wv, L0_xattn_Wk, L0_xattn_Wq, L0_xattn_Wo), axis=-1)
    x = _layernorm(x + _L0_ffn_ref(x, L0_ffn_Wv, L0_ffn_bv, L0_ffn_Wg, L0_ffn_bg, L0_ffn_Wp, L0_ffn_alpha, L0_ffn_g_r, L0_ffn_b_r, L0_ffn_g_c, L0_ffn_b_c, L0_ffn_W1, L0_ffn_b1, L0_ffn_W2, L0_ffn_b2), axis=-1)
    return x

_drawn_inputs = setup_inputs


def setup_inputs(seed=0):
    import zlib

    import numpy as np

    out = dict(_drawn_inputs(seed))
    spreads = {'L0_ffn_bv': (0.0, 0.1),
     'L0_ffn_bg': (0.0, 0.1),
     'L0_ffn_g_r': (1.0, 0.2),
     'L0_ffn_b_r': (0.0, 0.1),
     'L0_ffn_g_c': (1.0, 0.2),
     'L0_ffn_b_c': (0.0, 0.1),
     'L0_ffn_b1': (0.0, 0.1),
     'L0_ffn_b2': (0.0, 0.1)}
    factors = {}
    for name, (base, spread) in spreads.items():
        noise = np.random.default_rng([zlib.crc32(name.encode()), seed]).standard_normal(out[name].shape)
        drawn = base * np.exp(spread * noise) if base else spread * noise
        out[name] = jnp.asarray(drawn.astype(out[name].dtype))
    for name, factor in factors.items():
        out[name] = (out[name] * factor).astype(out[name].dtype)
    return out
```

```python
from contextlib import ExitStack

import concourse.bass as bass
from concourse import mybir

P = 128
B, S, D = 4, 2048, 512
C = D // P
NT = S // P
CTX = 154
CREM = CTX - P
HEADS, DH = 16, 32
E, INNER, PV = 8, 32, 8
EPS = 1e-5
GW = E + E * PV + E * INNER
HP = 3 * P
VB = DH + 1
HALF = 8
NEG = -1.0e20
FROM_ONE = 1
CUT = -3.0e38

F32 = mybir.dt.float32
F32R = mybir.dt.float32r
BF16 = mybir.dt.bfloat16
I32 = mybir.dt.int32
ALU = mybir.AluOpType
ACT = mybir.ActivationFunctionType
X = mybir.AxisListType.X


def product(pe, out, left, right, start, stop, skip=False):
    (lh, ll), (rh, rl) = left, right
    pe.matmul(out, ll, rh, start=start, stop=False, skip_group_check=skip)
    pe.matmul(out, lh, rl, start=False, stop=False, skip_group_check=skip)
    return pe.matmul(out, lh, rh, start=False, stop=stop, skip_group_check=skip)


class Chain:

    def __init__(self, engine, sem, per_pass, before=0):
        self.engine, self.sem, self.per_pass, self.n, self.before = engine, sem, per_pass, 0, before

    def link(self, ins, passes=0):
        self.n += 1
        ins.then_inc(self.sem, 1)
        self.engine.wait_ge(self.sem, passes * self.per_pass + self.before + self.n)


def context_part(nc, ctxT, wkT, wvT, mask, kT_d, vm_d, vr_d, mask_d):
    NB = B * CTX
    with ExitStack() as scope:
        def sb(name, shape, dt=F32):
            return scope.enter_context(nc.sbuf_tensor("ctx_" + name, shape, dt))

        def sem(name):
            return scope.enter_context(nc.semaphore(name))

        ctx_sb = sb("ctx_sb", [P, C, NB])
        wk = sb("wk", [P, C, D])
        wv = sb("wv", [P, C, D])
        kT = sb("kT_all", [P, B, C, CTX])
        vm = sb("vm_all", [P, B, HEADS * VB])
        vr = sb("vr_all", [P, B, 4, 4 * VB])
        mask_in = sb("mask_in", [1, B, CTX], I32)
        mask_row = sb("mask_row", [1, B, 2, CTX], BF16)
        bank = [scope.enter_context(nc.psum_tensor(f"c_bank{i}", [P, 512], F32)) for i in range(8)]

        loaded = sem("c_loaded")
        preset = sem("c_preset")
        k_full = sem("c_k_full")
        v_full = sem("c_v_full")
        k_kept = sem("c_k_kept")
        v_kept = sem("c_v_kept")
        mask_loaded = sem("c_mask_loaded")
        mask_made = sem("c_mask_made")
        stored = sem("c_stored")
        block = scope.enter_context(nc.Block())

        @block.sync
        def _(sp):
            sp.dma_start(ctx_sb[:], ctxT.rearrange("(c p) n -> p c n", p=P)).then_inc(loaded, 16)
            sp.dma_start(wk[:], wkT.rearrange("(c p) n -> p c n", p=P)).then_inc(loaded, 16)
            sp.dma_start(wv[:], wvT.rearrange("(c p) n -> p c n", p=P)).then_inc(loaded, 16)
            sp.dma_start(mask_in[:], mask.rearrange("(a b) n -> a b n", a=1)).then_inc(mask_loaded, 16)
            sp.wait_ge(mask_made, 2)
            sp.dma_start(mask_d.rearrange("(a b) n -> a b n", a=1), mask_row[:].rearrange("a b c n -> a b (c n)")) \
              .then_inc(stored, 16)
            sp.wait_ge(k_kept, 8)
            sp.dma_start(kT_d.rearrange("b p n -> p b n"), kT[:].rearrange("p b c n -> p b (c n)")).then_inc(stored, 16)
            sp.wait_ge(v_kept, B)
            sp.wait_ge(preset, 6)
            sp.dma_start(vm_d.rearrange("b p n -> p b n"), vm[:]).then_inc(stored, 16)
            sp.dma_start(vr_d.rearrange("b p n -> p b n"), vr[:].rearrange("p b q n -> p b (q n)")).then_inc(stored, 16)
            sp.wait_ge(stored, 64)

        @block.gpsimd
        def _(pool):
            pool.memset(vm[:], 1.0).then_inc(preset, 1)
            pool.memset(vr[:], 0.0).then_inc(preset, 1)
            pool.wait_ge(preset, 2)
            for j in range(4):
                pool.memset(vr[32 * j:32 * j + CREM, :, :, j * VB + DH:(j + 1) * VB], 1.0).then_inc(preset, 1)

        @block.tensor
        def _(pe):
            pe.wait_ge(loaded, 48)
            for c in range(C):
                for pair in range(2):
                    for e in range(C):
                        mm = pe.matmul(bank[2 * c + pair][:, 0:2 * CTX], wk[:, e, c * P:(c + 1) * P],
                                       ctx_sb[:, e, pair * 2 * CTX:(pair + 1) * 2 * CTX],
                                       start=(e == 0), stop=(e == C - 1))
                    mm.then_inc(k_full, 1)
            for b in range(B):
                for part, at, n in ((0, b * CTX, P), (1, b * CTX + P, CREM)):
                    pe.wait_ge(k_kept, b + 4 * part + 1)
                    for e in range(C):
                        mm = pe.matmul(bank[b + 4 * part][0:n, :], ctx_sb[:, e, at:at + n], wv[:, e, :],
                                       start=(e == 0), stop=(e == C - 1))
                mm.then_inc(v_full, 1)

        @block.scalar
        def _(act):
            for c in range(C):
                for pair in range(2):
                    act.wait_ge(k_full, 2 * c + pair + 1)
                    act.activation(kT[:, 2 * pair:2 * pair + 2, c, :],
                                   bank[2 * c + pair][:, 0:2 * CTX].rearrange("p (b n) -> p b n", b=2),
                                   ACT.Copy).then_inc(k_kept, 1)

        @block.vector
        def _(dve):
            dve.wait_ge(mask_loaded, 16)
            for copy in range(2):
                dve.tensor_scalar(mask_row[:, :, copy, :], mask_in[:], 0, NEG, ALU.is_equal, ALU.mult) \
                   .then_inc(mask_made, 1)
            dve.wait_ge(preset, 6)
            for b in range(B):
                dve.wait_ge(v_full, b + 1)
                for half in range(2):
                    dve.tensor_copy(
                        vm[:, b, half * HALF * VB:(half + 1) * HALF * VB].rearrange(
                            "p (r c v) -> p r c v", r=4, c=2)[:, :, :, 0:DH],
                        bank[b][:, half * 256:(half + 1) * 256].rearrange("p (c r d) -> p r c d", c=2, r=4))
                for j in range(4):
                    h0 = 4 * (j % 2) + j // 2
                    src = bank[4 + b][0:CREM, :].rearrange("p (a x) -> p a x", a=2)
                    for q in range(2):
                        last = dve.tensor_copy(
                            vr[32 * j:32 * j + CREM, b, :, j * VB:j * VB + DH].rearrange(
                                "p (a q) d -> p a q d", q=2)[:, :, q, :],
                            src[:, :, (h0 + 2 * q) * DH:(h0 + 2 * q + 1) * DH])
                last.then_inc(v_kept, 1)


def attention_part(nc, x_rows, xT_tiles, wqk_d, wvT_d, slope_d, x1_d):
    NCH = [(i + 4) // 4 for i in range(NT)]
    CUM = [sum(NCH[:i]) for i in range(NT + 1)]
    ROWS = CUM[NT]

    tr_of, mm_of = {}, {}

    def tr(*key):
        tr_of[key] = len(tr_of)

    def mm(*key):
        mm_of[key] = len(mm_of)

    for j in range(NT):
        mm("v", j)
    mm("q", 0)
    tr("q", 0)
    for i in range(NT + 1):
        if i + 1 < NT:
            mm("q", i + 1)
        if i > 0:
            mm("o", i - 1)
            for c in range(NCH[i - 1]):
                tr("p", i - 1, c)
        if i + 1 < NT:
            tr("q", i + 1)
    TR, MM = len(tr_of), len(mm_of)
    assert TR % 2 == 0 and MM % 2 == 0

    with ExitStack() as scope:
        def sb(name, shape, dt=F32):
            return scope.enter_context(nc.sbuf_tensor("attn_" + name, shape, dt))

        def sem(name):
            return scope.enter_context(nc.semaphore(name))

        def split(name, shape):
            return sb(name + "_hi", shape, F32R), sb(name + "_lo", shape, F32R)

        xT = split("xT", [P, C, S])
        v = split("v", [P, NT, D])
        wqk = split("wqk", [P, C, D])
        wv = split("wv", [P, C, D])
        bias = sb("alibi", [P, S])
        probs = [sb(f"probs{i}", [P, S]) for i in range(2)]
        pT = [split(f"pT{i}", [P, 512]) for i in range(2)]
        qT = split("qT", [P, C, P])
        q_row = sb("q_row", [P, D])
        x_in = [sb(f"x_in{i}", [P, D]) for i in range(2)]
        res = [sb(f"res{i}", [P, D]) for i in range(2)]
        ident = sb("ident", [P, P])
        slope = sb("slope", [P, 1])
        chunk_max = sb("chunk_max", [P, 4])
        neg_max = sb("neg_max", [P, 2])
        row_sum = sb("row_sum", [P, 2])
        inv_sum = sb("inv_sum", [P, 1])
        stats = sb("stats", [P, 6])
        moments = sb("moments", [P, 2])
        spread = sb("spread", [P, 1])
        rstd = sb("rstd", [P, 1])
        minus_half = sb("minus_half", [P, 1])
        eps = sb("eps", [P, 1])
        unused = sb("unused", [P, 2])
        scores = [scope.enter_context(nc.psum_tensor(f"scores{i}", [P, 512], F32)) for i in range(4)]
        trp = [scope.enter_context(nc.psum_tensor(f"a_trp{i}", [P, 512], F32)) for i in range(2)]
        mmp = [scope.enter_context(nc.psum_tensor(f"a_mmp{i}", [P, 512], F32)) for i in range(2)]

        weight_in = sem("a_weight_in")
        weight_hi = sem("a_weight_hi")
        weight_lo = sem("a_weight_lo")
        slope_in = sem("a_slope_in")
        constants = sem("a_constants")
        x_in_full = [sem(f"a_x_in_full{i}") for i in range(2)]
        xT_hi = sem("a_xT_hi")
        xT_lo = sem("a_xT_lo")
        res_full = [sem(f"a_res_full{i}") for i in range(2)]
        stored = [sem(f"a_stored{i}") for i in range(2)]
        tr_full = sem("a_tr_full")
        tr_hi = sem("a_tr_hi")
        tr_free = [sem(f"a_tr_free{i}") for i in range(2)]
        v_full = sem("a_v_full")
        q_full = sem("a_q_full")
        v_hi = sem("a_v_hi")
        mm_free = [sem(f"a_mm_free{i}") for i in range(2)]
        s_full = sem("a_s_full")
        s_free = sem("a_s_free")
        max_ready = sem("a_max_ready")
        exp_done = sem("a_exp_done")
        pv_done = sem("a_pv_done")
        moments_ready = sem("a_moments_ready")
        spread_ready = sem("a_spread_ready")
        rstd_ready = sem("a_rstd_ready")
        x1_ready = sem("a_x1_ready")
        chain_sem = sem("a_chain")
        passed = sem("a_passed")
        block = scope.enter_context(nc.Block())

        def tr_split(b, n):
            return tr_free[n % 2], b * (TR // 2) + (FROM_ONE + n // 2 + 1)

        def mm_out(b, n):
            return mm_free[n % 2], b * (MM // 2) + (FROM_ONE + n // 2 + 1)

        stage = [probs[i][:].rearrange("p (c n) -> p c n", c=C) for i in range(2)]

        @block.sync
        def _(sp):
            sp.dma_start(stage[0], wqk_d.rearrange("(c p) n -> p c n", p=P)).then_inc(weight_in, 16)
            sp.wait_ge(weight_in, 16)
            sp.dma_start(stage[1], wvT_d.rearrange("(c p) n -> p c n", p=P)).then_inc(weight_in, 16)
            sp.dma_start(slope[:], slope_d.broadcast_to([P, 1])).then_inc(slope_in, 16)
            with sp.Fori(0, B) as b:
                for j in range(NT):
                    sp.wait_ge(xT_lo, b * NT + (FROM_ONE + max(j - 1, 0)))
                    sp.dma_start(x_in[j % 2][:], xT_tiles[bass.ds(b * NT + j, 1)].rearrange("a p n -> p (a n)")) \
                      .then_inc(x_in_full[j % 2], 16)

        @block.gpsimd
        def _(pool):
            pool.memset(ident[:], 0.0).then_inc(constants, 1)
            pool.wait_ge(constants, 1)
            pool.affine_select(out=ident[:], in_=ident[:], compare_op=ALU.not_equal, fill=1.0, base=0,
                               pattern=[[-1, P]], channel_multiplier=1).then_inc(constants, 1)
            pool.iota(bias[:], pattern=[[1, S]], base=-(S - P), channel_multiplier=-1,
                      allow_small_or_imprecise_dtypes=True).then_inc(constants, 1)
            pool.wait_ge(slope_in, 16)
            pool.wait_ge(constants, 3)
            pool.tensor_scalar(bias[:], bias[:], slope[:, 0:1], None, ALU.mult).then_inc(constants, 1)
            pool.wait_ge(constants, 4)
            pool.affine_select(out=bias[:], in_=bias[:], compare_op=ALU.is_ge, fill=CUT, base=S - P,
                               pattern=[[-1, S]], channel_multiplier=1).then_inc(constants, 1)
            pool.memset(minus_half[:], -0.5).then_inc(constants, 1)
            pool.memset(eps[:], EPS).then_inc(constants, 1)
            pool.wait_ge(constants, 7)
            for k, free in enumerate(stored):
                pool.dma_start(unused[:, k:k + 1], slope_d.broadcast_to([P, 1])).then_inc(free, 16)
            with pool.Fori(0, B) as b:
                for i in range(NT + 1):
                    if i < NT:
                        pool.wait_ge(stored[i % 2], 16 * (b * (NT // 2) + i // 2) + 16)
                        pool.sem_inc(passed, 1)
                        pool.dma_start(res[i % 2][:], x_rows[bass.ds(b * NT + i, 1)].rearrange("a p n -> p (a n)")) \
                            .then_inc(res_full[i % 2], 16)
                    if i > 0:
                        pool.wait_ge(moments_ready, b * NT + i)
                        pool.tensor_tensor(spread[:], moments[:, 1:2], eps[:], ALU.add).then_inc(spread_ready, 1)
                        pool.wait_ge(spread_ready, b * NT + i)
                        pool.tensor_tensor(rstd[:], spread[:], minus_half[:], ALU.pow).then_inc(rstd_ready, 1)
                        pool.wait_ge(x1_ready, b * NT + i)
                        pool.sem_inc(passed, 1)
                        pool.dma_start(x1_d[bass.ds(b * NT + i - 1, 1)].rearrange("a p n -> p (a n)"),
                                       res[(i - 1) % 2][:]).then_inc(stored[(i - 1) % 2], 16)
            for k in range(2):
                pool.wait_ge(stored[k], 16 * B * NT // 2 + 16)

        @block.tensor
        def _(pe):
            pe.wait_ge(weight_lo, 2)
            pe.wait_ge(constants, 2)
            for free in (s_full, pv_done):
                pe.sem_inc(free, FROM_ONE)
            with pe.Fori(0, B) as b:
                def tr_bank(*key):
                    n = tr_of[key]
                    pe.wait_ge(tr_free[n % 2], b * (TR // 2) + (FROM_ONE + n // 2))
                    return trp[n % 2]

                def mm_bank(*key):
                    n = mm_of[key]
                    pe.wait_ge(mm_free[n % 2], b * (MM // 2) + (FROM_ONE + n // 2))
                    return mmp[n % 2]

                def q_row_product(i):
                    out = mm_bank("q", i)
                    for c in range(C):
                        last = product(pe, out[:], [t[:, c, i * P:(i + 1) * P] for t in xT],
                                       [t[:, c, :] for t in wqk], c == 0, c == C - 1)
                    last.then_inc(q_full, 1)

                def q_transpose(i):
                    pe.wait_ge(*mm_out(b, mm_of["q", i]))
                    out = tr_bank("q", i)
                    for c in range(C):
                        last = pe.transpose(out[:, c * P:(c + 1) * P], q_row[:, c * P:(c + 1) * P], ident[:])
                    last.then_inc(tr_full, 1)

                def score_rows(i):
                    pe.wait_ge(*tr_split(b, tr_of["q", i]))
                    for k in range(NCH[i]):
                        earlier = CUM[i - 1] + k + 1 if i > 0 and k < NCH[i - 1] else 0
                        pe.wait_ge(s_free, b * ROWS + (FROM_ONE + earlier))
                        w = min(512, (i + 1) * P - k * 512)
                        for c in range(C):
                            last = product(pe, scores[k][:, 0:w], [t[:, c, :] for t in qT],
                                           [t[:, c, k * 512:k * 512 + w] for t in xT], c == 0, c == C - 1)
                        last.then_inc(s_full, 1)

                def probs_transpose(i, k):
                    out = tr_bank("p", i, k)
                    n = min(4, i + 1 - 4 * k)
                    for t in range(n):
                        at = (4 * k + t) * P
                        last = pe.transpose(out[:, t * P:(t + 1) * P], probs[i % 2][:, at:at + P], ident[:])
                    last.then_inc(tr_full, 1)

                def values(i):
                    pe.wait_ge(exp_done, b * NT + i + 1)
                    out = mm_bank("o", i)
                    probs_transpose(i, 0)
                    for k in range(NCH[i]):
                        if k + 1 < NCH[i]:
                            probs_transpose(i, k + 1)
                        pe.wait_ge(*tr_split(b, tr_of["p", i, k]))
                        n = min(4, i + 1 - 4 * k)
                        for t in range(n):
                            last = product(pe, out[:], [h[:, t * P:(t + 1) * P] for h in pT[(CUM[i] + k) % 2]],
                                           [h[:, 4 * k + t, :] for h in v], 4 * k + t == 0, 4 * k + t == i)
                        last.then_inc(pv_done, 1)

                for j in range(NT):
                    pe.wait_ge(xT_lo, b * NT + (FROM_ONE + j + 1))
                    out = mm_bank("v", j)
                    for c in range(C):
                        last = product(pe, out[:], [t[:, c, j * P:(j + 1) * P] for t in xT],
                                       [t[:, c, :] for t in wv], c == 0, c == C - 1)
                    last.then_inc(v_full, 1)
                q_row_product(0)
                q_transpose(0)
                for i in range(NT + 1):
                    if i < NT:
                        score_rows(i)
                    if i + 1 < NT:
                        q_row_product(i + 1)
                    if i > 0:
                        values(i - 1)
                    if i + 1 < NT:
                        q_transpose(i + 1)

        def exps(act, b, i):
            act.wait_ge(max_ready, b * NT + i + 1)
            act.activation(probs[i % 2][:, 0:(i + 1) * P], probs[i % 2][:, 0:(i + 1) * P], ACT.Exp,
                           bias=neg_max[:, i % 2:i % 2 + 1],
                           accum_out=row_sum[:, i % 2:i % 2 + 1]).then_inc(exp_done, 1)

        @block.scalar
        def _(act):
            for w, pair in enumerate((wqk, wv)):
                act.wait_ge(weight_in, 16 * (w + 1))
                act.activation(pair[0][:], stage[w], ACT.Copy).then_inc(weight_hi, 1)
            with act.Fori(0, B) as b:
                def high(out, *key):
                    n = tr_of[key]
                    act.wait_ge(tr_full, b * TR + n + 1)
                    w = out.shape[-1] if len(out.shape) == 2 else 512
                    src = trp[n % 2][:, 0:w]
                    if len(out.shape) == 3:
                        src = src.rearrange("p (c n) -> p c n", c=C)
                    act.activation(out, src, ACT.Copy).then_inc(tr_hi, 1)

                def q_out(i):
                    n = mm_of["q", i]
                    act.wait_ge(q_full, b * NT + i + 1)
                    act.activation(q_row[:], mmp[n % 2][:], ACT.Copy, scale=float(D) ** -0.5) \
                       .then_inc(mm_free[n % 2], 1)

                def v_high(j):
                    n = mm_of["v", j]
                    act.wait_ge(v_full, b * NT + j + 1)
                    act.activation(v[0][:, j, :], mmp[n % 2][:], ACT.Copy).then_inc(v_hi, 1)

                for j in range(NT):
                    act.wait_ge(x_in_full[j % 2], 16 * (b * (NT // 2) + j // 2 + 1))
                    act.wait_ge(s_full, b * ROWS + FROM_ONE)
                    act.activation(xT[0][:, :, j * P:(j + 1) * P], x_in[j % 2][:].rearrange("p (c n) -> p c n", c=C),
                                   ACT.Copy).then_inc(xT_hi, 1)
                    if j > 0:
                        v_high(j - 1)
                v_high(NT - 1)
                q_out(0)
                high(qT[0][:], "q", 0)
                for i in range(NT + 1):
                    if i + 1 < NT:
                        q_out(i + 1)
                    if i > 0:
                        for k in range(NCH[i - 1]):
                            m = CUM[i - 1] + k
                            act.wait_ge(pv_done, b * ROWS + (FROM_ONE + max(m - 1, 0)))
                            w = min(512, i * P - k * 512)
                            high(pT[m % 2][0][:, 0:w], "p", i - 1, k)
                            if k == 0 and i < NT:
                                exps(act, b, i)
                    elif i < NT:
                        exps(act, b, i)
                    if i + 1 < NT:
                        high(qT[0][:], "q", i + 1)

        @block.vector
        def _(dve):
            for w, pair in enumerate((wqk, wv)):
                dve.wait_ge(weight_hi, w + 1)
                dve.tensor_tensor(pair[1][:], stage[w], pair[0][:].bitcast(F32), ALU.subtract).then_inc(weight_lo, 1)
            dve.wait_ge(weight_lo, 2)
            dve.wait_ge(constants, 7)
            for free in (*tr_free, *mm_free, s_free, xT_lo):
                dve.sem_inc(free, FROM_ONE)
            with dve.Fori(0, B) as b:
                chain = Chain(dve, chain_sem, NT * 2)

                def low(pair_lo, pair_hi, *key):
                    n = tr_of[key]
                    dve.wait_ge(tr_hi, b * TR + n + 1)
                    w = pair_lo.shape[-1] if len(pair_lo.shape) == 2 else 512
                    src = trp[n % 2][:, 0:w]
                    if len(pair_lo.shape) == 3:
                        src = src.rearrange("p (c n) -> p c n", c=C)
                    dve.tensor_tensor(pair_lo, src, pair_hi.bitcast(F32), ALU.subtract).then_inc(tr_free[n % 2], 1)

                def v_low(j):
                    n = mm_of["v", j]
                    dve.wait_ge(v_hi, b * NT + j + 1)
                    dve.tensor_tensor(v[1][:, j, :], mmp[n % 2][:], v[0][:, j, :].bitcast(F32), ALU.subtract) \
                       .then_inc(mm_free[n % 2], 1)

                def biased(i):
                    for k in range(NCH[i]):
                        w = min(512, (i + 1) * P - k * 512)
                        at = S - (i + 1) * P + k * 512
                        dve.wait_ge(s_full, b * ROWS + (FROM_ONE + CUM[i] + k + 1))
                        dve.sem_inc(passed, 1)
                        dve.tensor_tensor_reduce(probs[i % 2][:, k * 512:k * 512 + w], scores[k][:, 0:w],
                                                 bias[:, at:at + w], 1.0, CUT, ALU.add, ALU.max,
                                                 chunk_max[:, k:k + 1]).then_inc(s_free, 1)
                    dve.wait_ge(s_free, b * ROWS + (FROM_ONE + CUM[i + 1]))
                    dve.tensor_reduce(neg_max[:, i % 2:i % 2 + 1], chunk_max[:, 0:NCH[i]], X, ALU.max,
                                      negate=True).then_inc(max_ready, 1)

                def finish(i):
                    r = res[i % 2]
                    n = mm_of["o", i]
                    chain.link(dve.reciprocal(inv_sum[:], row_sum[:, i % 2:i % 2 + 1]), b)
                    dve.wait_ge(res_full[i % 2], 16 * (b * (NT // 2) + i // 2 + 1))
                    dve.wait_ge(pv_done, b * ROWS + (FROM_ONE + CUM[i + 1]))
                    dve.scalar_tensor_tensor(r[:], mmp[n % 2][:], inv_sum[:, 0:1], r[:],
                                             ALU.mult, ALU.add).then_inc(mm_free[n % 2], 1)
                    dve.wait_ge(*mm_out(b, n))
                    chain.link(dve.bn_stats(stats[:], r[:]), b)
                    dve.sem_inc(passed, 1)
                    dve.bn_aggr(moments[:], stats[:]).then_inc(moments_ready, 1)

                def normalise(i):
                    r = res[i % 2]
                    dve.wait_ge(rstd_ready, b * NT + i + 1)
                    dve.tensor_scalar(r[:], r[:], moments[:, 0:1], rstd[:, 0:1],
                                      ALU.subtract, ALU.mult).then_inc(x1_ready, 1)

                for j in range(NT):
                    dve.wait_ge(xT_hi, b * NT + j + 1)
                    dve.tensor_tensor(xT[1][:, :, j * P:(j + 1) * P], x_in[j % 2][:].rearrange("p (c n) -> p c n", c=C),
                                      xT[0][:, :, j * P:(j + 1) * P].bitcast(F32), ALU.subtract).then_inc(xT_lo, 1)
                    if j > 0:
                        v_low(j - 1)
                v_low(NT - 1)
                low(qT[1][:], qT[0][:], "q", 0)
                for i in range(NT + 1):
                    if i < NT:
                        biased(i)
                    if i > 1:
                        normalise(i - 2)
                    if i > 0:
                        for k in range(NCH[i - 1]):
                            m = CUM[i - 1] + k
                            w = min(512, i * P - k * 512)
                            low(pT[m % 2][1][:, 0:w], pT[m % 2][0][:, 0:w], "p", i - 1, k)
                    if i + 1 < NT:
                        low(qT[1][:], qT[0][:], "q", i + 1)
                    if i > 0:
                        finish(i - 1)
                normalise(NT - 1)
                assert chain.n == chain.per_pass


def post_part(nc, x1_d, kT_d, vm_d, vr_d, mask_d, wq_d, wo_d, wv_d, bv_d, wg_d, bg_d, w2_d, alpha_d,
              gain_d, shift_d, out_d):
    T = 4
    G = B * NT // T
    NH = 2 * T
    END = NH + 2
    FIRST, LOOP, LAST = "first", "loop", "last"

    def steps(attend, mix):
        out = []
        if attend:
            out += [("x1T", t) for t in range(T)] + [("xq", c) for c in range(C)]
        for n in range(END):
            if attend and n < NH:
                out.append(("scores", n))
            t, odd = divmod(n - 3, 2)
            if attend and n >= 3 and not odd:
                out.append(("oT", t))
            if mix:
                out += [(what, n - lag) for what, lag in (("gate", 3), ("vT", 2), ("v", 1), ("x2T", 0))
                        if 0 <= n - lag < T]
            if attend and 1 <= n <= NH:
                out += [("pT", n - 1), ("pv", n - 1)]
            if attend and n >= 3 and not odd:
                out.append(("wo", t))
        if mix:
            out.append(("hT", 0))
            for t in range(T):
                if t + 1 < T:
                    out.append(("hT", t + 1))
                out.append(("w2", t))
        return out

    PLANS = {FIRST: steps(True, False), LOOP: steps(True, True), LAST: steps(False, True)}
    uses = {"tr": {}, "mm": {}}
    for kind, plan in PLANS.items():
        uses["tr"][kind], uses["mm"][kind] = {}, {}
        for what, at in plan:
            if what == "pT":
                for k in range(3):
                    uses["tr"][kind][what, at, k] = len(uses["tr"][kind])
            elif what in ("x1T", "oT", "x2T", "vT", "hT"):
                uses["tr"][kind][what, at] = len(uses["tr"][kind])
            elif what != "scores":
                uses["mm"][kind][what, at] = len(uses["mm"][kind])
    for ring in uses.values():
        assert len(ring[FIRST]) % 2 == 0 and len(ring[LOOP]) % 2 == 0

    def use(ring, kind, i, *key):
        n = uses[ring][kind][key]
        first, loop = len(uses[ring][FIRST]), len(uses[ring][LOOP])
        return n % 2, {FIRST: n, LOOP: i * loop + (first + n), LAST: first + (G - 1) * loop + n}[kind]

    def bank_use(ring, kind, i, *key):
        n = uses[ring][kind][key]
        first, loop = len(uses[ring][FIRST]) // 2, len(uses[ring][LOOP]) // 2
        n2 = n // 2
        return n % 2, {FIRST: n2, LOOP: i * loop + (first + n2), LAST: first + (G - 1) * loop + n2}[kind]

    with ExitStack() as scope:
        def sb(name, shape, dt=F32):
            return scope.enter_context(nc.sbuf_tensor("post_" + name, shape, dt))

        def sem(name):
            return scope.enter_context(nc.semaphore("p_" + name))

        def split(name, shape):
            return sb(name + "_hi", shape, F32R), sb(name + "_lo", shape, F32R)

        wq, wo, wv = (split(n, [P, C, D]) for n in ("wq", "wo", "wv"))
        wg = split("wg", [P, C, GW])
        w2 = split("w2", [P, 3, D])
        kT = sb("kT", [P, C, CTX])
        vm = sb("vm", [P, HEADS * VB])
        vr = sb("vr", [P, 4 * 4 * VB])
        mask_row = sb("mask_row", [P, 2 * CTX], BF16)
        ones = sb("ones", [P, P], BF16)
        x1 = sb("x1", [P, T, D])
        x1T = split("x1T", [P, C, T * P])
        qT = sb("qT", [P, C, T * P])
        shifted = sb("shifted", [P, HALF, CTX])
        probs = [sb(f"probs{i}", [P, HALF * P]) for i in range(2)]
        probs_end = [sb(f"probs_end{i}", [P, HALF * 32]) for i in range(2)]
        pT = [sb(f"pT{i}", [P, HALF + 2, P]) for i in range(2)]
        o = sb("o", [P, D])
        oT = split("oT", [P, C, P])
        x2 = sb("x2", [P, T, D])
        x2T = split("x2T", [P, C, P])
        val = sb("val", [P, T, D])
        vT = split("vT", [P, C, P])
        skip = sb("skip", [P, T, D])
        gate = sb("gate", [P, T, GW])
        tanh = sb("tanh", [P, T, E * INNER])
        hid = sb("hid", [P, T, HP])
        hT = [split(f"hT{i}", [P, 3, P]) for i in range(2)]
        y = [sb(f"y{i}", [P, D]) for i in range(2)]
        bv = sb("bv", [P, D])
        bg = sb("bg", [P, GW])
        alpha = sb("alpha", [P, 1])
        gains = sb("gains", [P, 2, E])
        shifts = sb("shifts", [P, 2, E])
        before = sb("before", [P, E, E])
        ident = sb("ident", [P, P])
        minus_half = sb("minus_half", [P, 2 * T])
        plus_half = sb("plus_half", [P, E])
        eps = sb("eps", [P, 1])
        unused = sb("unused", [P, 2])
        row_max = sb("row_max", [P, HALF])
        inv_sum = sb("inv_sum", [P, HALF])
        stats = sb("stats", [P, 6])
        mo_a = sb("mo_a", [P, 2])
        spread_a = sb("spread_a", [P, 1])
        rstd_a = sb("rstd_a", [P, 1])
        mo_y = sb("mo_y", [P, 2, 2])
        spread_y = sb("spread_y", [P, 2])
        rstd_y = sb("rstd_y", [P, 2])
        square = sb("square", [P, E * PV])
        norm2 = sb("norm2", [P, T, E])
        norm = sb("norm", [P, T, E])
        both = sb("both", [P, T, 2, E])
        both_sq = sb("both_sq", [P, T, 2, E])
        mean = sb("mean", [P, T * 2])
        spread_g = sb("spread_g", [P, T * 2])
        rstd_g = sb("rstd_g", [P, T * 2])
        s = sb("s", [P, T, E])
        s_max = sb("s_max", [P, T])
        s_rel = sb("s_rel", [P, T, E])
        s_exp = sb("s_exp", [P, T, E])
        beats = sb("beats", [P, T, E, E])
        ties = sb("ties", [P, T, E, E])
        rank = sb("rank", [P, T, E])
        den = sb("den", [P, T])
        half_w = sb("half_w", [P, T, E])
        scores = scope.enter_context(nc.psum_tensor("p_scores", [P, 4, 512], F32))
        trp = [scope.enter_context(nc.psum_tensor(f"p_trp{i}", [P, 512], F32)) for i in range(2)]
        mmp = [scope.enter_context(nc.psum_tensor(f"p_mmp{i}", [P, 512], F32)) for i in range(2)]

        weight_in = sem("weight_in")
        weight_hi = sem("weight_hi")
        weight_lo = sem("weight_lo")
        small_in = sem("small_in")
        constants = sem("constants")
        tables = sem("tables")
        alpha_tanh = sem("alpha_tanh")
        x1_in = sem("x1_in")
        ctx_in = sem("ctx_in")
        tr_full = sem("tr_full")
        tr_hi = sem("tr_hi")
        tr_free = [sem(f"tr_free{i}") for i in range(2)]
        mm_full = sem("mm_full")
        mm_free = [sem(f"mm_free{i}") for i in range(2)]
        s_full = sem("s_full")
        s_out = sem("s_out")
        exp_done = sem("exp_done")
        mo_a_ready = sem("mo_a_ready")
        spread_a_ready = sem("spread_a_ready")
        rstd_a_ready = sem("rstd_a_ready")
        x2_ready = sem("x2_ready")
        skip_ready = sem("skip_ready")
        norm2_ready = sem("norm2_ready")
        norm_ready = sem("norm_ready")
        spread_g_ready = sem("spread_g_ready")
        rstd_g_ready = sem("rstd_g_ready")
        tanh_ready = sem("tanh_ready")
        s_rel_ready = sem("s_rel_ready")
        s_exp_ready = sem("s_exp_ready")
        hid_ready = sem("hid_ready")
        mo_y_ready = sem("mo_y_ready")
        spread_y_ready = sem("spread_y_ready")
        rstd_y_ready = sem("rstd_y_ready")
        y_ready = sem("y_ready")
        stored = [sem(f"stored{i}") for i in range(2)]
        chain_a_sem = sem("chain_a")
        chain_m_sem = sem("chain_m")
        passed = sem("passed")
        block = scope.enter_context(nc.Block())

        landings = [skip, val]
        WEIGHTS = [(wq, wq_d, C), (wo, wo_d, C), (wv, wv_d, C), (wg, wg_d, C), (w2, w2_d, 3)]
        NW = len(WEIGHTS)

        def landing(w):
            _, dram, chunks = WEIGHTS[w]
            n = dram.shape[-1]
            return landings[w % 2][:].rearrange("p t n -> p (t n)")[:, 0:chunks * n].rearrange("p (c n) -> p c n", c=chunks)

        SPLIT_TR = ("x1T", "oT", "x2T", "vT", "hT")

        def product_out(engine, kind, i, *key):
            k, n = bank_use("mm", kind, i, *key)
            engine.wait_ge(mm_free[k], n + 1)

        def hi_of(kind, what, at):
            keys = [k for k in uses["tr"][kind] if k[0] in SPLIT_TR]
            return keys.index((what, at))

        NHI = {kind: sum(k[0] in SPLIT_TR for k in uses["tr"][kind]) for kind in PLANS}

        def hi_value(kind, i, what, at):
            n = hi_of(kind, what, at)
            return {FIRST: n, LOOP: i * NHI[LOOP] + (NHI[FIRST] + n), LAST: NHI[FIRST] + (G - 1) * NHI[LOOP] + n}[kind]

        def iterations(engine, body):
            body(FIRST, 0, None, 0)
            with engine.Fori(0, G - 1) as i:
                body(LOOP, i + 1, i, i)
            body(LAST, None, G - 1, 0)

        @block.sync
        def _(sp):
            for w, (_, dram, chunks) in enumerate(WEIGHTS):
                if w >= 2:
                    sp.wait_ge(weight_lo, w - 1)
                if w == 1:
                    for t, src in ((bv, bv_d), (bg, bg_d), (alpha, alpha_d)):
                        sp.dma_start(t[:], src.broadcast_to([P, src.shape[-1]])).then_inc(small_in, 16)
                    for t, src in ((gains, gain_d), (shifts, shift_d)):
                        sp.dma_start(t[:].rearrange("p a e -> p (a e)"), src.broadcast_to([P, 2 * E])) \
                          .then_inc(small_in, 16)
                sp.dma_start(landing(w), dram.rearrange("(c p) n -> p c n", p=P)).then_inc(weight_in, 16)
                sp.wait_ge(weight_in, 16 * (w + 1))
            with sp.Fori(0, B) as b:
                for k in range(NT // T):
                    g = b * (NT // T) + k
                    sp.wait_ge(x2_ready, g * T + FROM_ONE)
                    sp.dma_start(x1[:], x1_d[bass.ds(g * T, T)].rearrange("t p n -> p t n")).then_inc(x1_in, 16)
                    sp.dma_start(mask_row[0:97:32, :], mask_d[bass.ds(b, 1)].broadcast_to([4, 2 * CTX])) \
                      .then_inc(ctx_in, 16)
                    sp.dma_start(kT[:].rearrange("p c n -> p (c n)"),
                                 kT_d[bass.ds(b, 1)].rearrange("a p n -> p (a n)")).then_inc(ctx_in, 16)
                    sp.dma_start(vm[:], vm_d[bass.ds(b, 1)].rearrange("a p n -> p (a n)")).then_inc(ctx_in, 16)
                    sp.dma_start(vr[:], vr_d[bass.ds(b, 1)].rearrange("a p n -> p (a n)")).then_inc(ctx_in, 16)

        @block.gpsimd
        def _(pool):
            pool.memset(ident[:], 0.0).then_inc(constants, 1)
            pool.memset(before[:], 1.0).then_inc(constants, 1)
            pool.memset(ones[:], 1.0).then_inc(constants, 1)
            pool.memset(hid[:], 0.0).then_inc(constants, 1)
            pool.memset(minus_half[:], -0.5).then_inc(constants, 1)
            pool.memset(plus_half[:], 0.5).then_inc(constants, 1)
            pool.memset(probs_end[0][:], 0.0).then_inc(constants, 1)
            pool.memset(probs_end[1][:], 0.0).then_inc(constants, 1)
            pool.memset(eps[:], EPS).then_inc(constants, 1)
            pool.wait_ge(constants, 9)
            pool.affine_select(out=ident[:], in_=ident[:], compare_op=ALU.not_equal, fill=1.0, base=0,
                               pattern=[[-1, P]], channel_multiplier=1).then_inc(constants, 1)
            pool.affine_select(out=before[:], in_=before[:], compare_op=ALU.is_gt, fill=0.0, base=0,
                               pattern=[[1, E], [-1, E]], channel_multiplier=0).then_inc(constants, 1)
            pool.wait_ge(constants, 11)

            def body(kind, a, m, i):
                for n in range(END + T + 1):
                    t = n - 3
                    if m is not None and 0 <= t < T:
                        pool.wait_ge(norm2_ready, m * T + t + 1)
                        pool.tensor_tensor(norm[:, t, :], norm2[:, t, :], plus_half[:], ALU.pow).then_inc(norm_ready, 1)
                    t = n - 1
                    if m is not None and 0 <= t < T:
                        product_out(pool, kind, i, "v", t)
                        pool.tensor_tensor(skip[:, t, :], val[:, t, :], x2[:, t, :], ALU.add).then_inc(skip_ready, 1)
                    if m is not None and n == 7:
                        pool.wait_ge(spread_g_ready, m + 1)
                        pool.tensor_tensor(rstd_g[:], spread_g[:], minus_half[:], ALU.pow).then_inc(rstd_g_ready, 1)
                    t, odd = divmod(n - 3, 2)
                    if a is not None and 3 <= n < END and not odd:
                        pool.wait_ge(mo_a_ready, a * T + t + 1)
                        pool.tensor_tensor(spread_a[:], mo_a[:, 1:2], eps[:], ALU.add).then_inc(spread_a_ready, 1)
                        pool.wait_ge(spread_a_ready, a * T + t + 1)
                        pool.tensor_tensor(rstd_a[:], spread_a[:], minus_half[:, 0:1], ALU.pow) \
                            .then_inc(rstd_a_ready, 1)
                    t = n - END
                    if m is not None and 0 <= t < T:
                        pool.wait_ge(mo_y_ready, m * T + t + 1)
                        k = t % 2
                        pool.tensor_tensor(spread_y[:, k:k + 1], mo_y[:, k, 1:2], eps[:], ALU.add) \
                            .then_inc(spread_y_ready, 1)
                        pool.wait_ge(spread_y_ready, m * T + t + 1)
                        pool.tensor_tensor(rstd_y[:, k:k + 1], spread_y[:, k:k + 1], minus_half[:, 0:1], ALU.pow) \
                            .then_inc(rstd_y_ready, 1)
                    t = n - END - 1
                    if m is not None and 0 <= t < T:
                        pool.wait_ge(y_ready, m * T + t + 1)
                        pool.sem_inc(passed, 1)
                        pool.dma_start(out_d[bass.ds(m * T + t, 1)].rearrange("a p n -> p (a n)"), y[t % 2][:]) \
                            .then_inc(stored[t % 2], 16)

            for k, free in enumerate(stored):
                pool.dma_start(unused[:, k:k + 1], alpha_d.broadcast_to([P, 1])).then_inc(free, 16)
            iterations(pool, body)
            for k in range(2):
                pool.wait_ge(stored[k], 16 * G * T // 2 + 16)

        @block.tensor
        def _(pe):
            pe.wait_ge(weight_lo, NW)
            pe.wait_ge(constants, 11)

            def body(kind, a, m, i):
                def tr_bank(*key):
                    k, n = bank_use("tr", kind, i, *key)
                    pe.wait_ge(tr_free[k], n)
                    return trp[k]

                def mm_bank(*key):
                    k, n = bank_use("mm", kind, i, *key)
                    pe.wait_ge(mm_free[k], n)
                    return mmp[k]

                def tr_out(*key):
                    k, n = bank_use("tr", kind, i, *key)
                    pe.wait_ge(tr_free[k], n + 1)

                def turn(src, chunks, *key):
                    out = tr_bank(*key)
                    for c in range(chunks):
                        last = pe.transpose(out[:, c * P:(c + 1) * P], src[:, c * P:(c + 1) * P], ident[:])
                    last.then_inc(tr_full, 1)

                def multiply(left, right, chunks, width, *key):
                    out = mm_bank(*key)
                    for c in range(chunks):
                        last = product(pe, out[:, 0:width], [h[:, c, :] for h in left], [h[:, c, :] for h in right],
                                       c == 0, c == chunks - 1)
                    last.then_inc(mm_full, 1)

                for what, at in PLANS[kind]:
                    if what == "x1T":
                        if at == 0:
                            pe.wait_ge(x1_in, 16 * (a + 1))
                        turn(x1[:, at, :], C, what, at)
                    elif what == "xq":
                        if at == 0:
                            tr_out("x1T", T - 2)
                            tr_out("x1T", T - 1)
                        out = mm_bank(what, at)
                        for c in range(C):
                            last = product(pe, out[:], [h[:, c, at * P:(at + 1) * P] for h in wq],
                                           [h[:, c, :] for h in x1T], c == 0, c == C - 1)
                        last.then_inc(mm_full, 1)
                    elif what == "scores":
                        t, half = divmod(at, 2)
                        if at == 0:
                            for c in range(C - 2, C):
                                product_out(pe, kind, i, "xq", c)
                            pe.wait_ge(ctx_in, 64 * (a + 1))
                        pe.wait_ge(s_out, a * NH + at)
                        for r in range(4):
                            rows = slice(32 * r, 32 * r + 1)
                            pe.matmul(scores[:, r, 0:2 * CTX], ones[rows, :], mask_row[rows, :],
                                      start=True, stop=False, skip_group_check=True)
                        for c2 in range(2):
                            c = 2 * half + c2
                            for r in range(4):
                                rows = slice(32 * r, 32 * r + 32)
                                last = pe.matmul(scores[:, r, c2 * CTX:(c2 + 1) * CTX],
                                                 qT[rows, c, t * P:(t + 1) * P], kT[rows, c, :],
                                                 start=False, stop=True, skip_group_check=True)
                        last.then_inc(s_full, 1)
                    elif what == "pT":
                        pe.wait_ge(exp_done, a * (2 * NH) + (2 * at + 2))
                        for k in range(3):
                            out = tr_bank(what, at, k)
                            for j in range(4 if k < 2 else 2):
                                src = probs[at % 2] if k < 2 else probs_end[at % 2]
                                src = src[:, (4 * k % 8 + j) * P:(4 * k % 8 + j + 1) * P]
                                last = pe.transpose(out[:, j * P:(j + 1) * P], src, ident[:])
                            last.then_inc(tr_full, 1)
                    elif what == "pv":
                        out = mm_bank(what, at)
                        half = at % 2
                        tr_out("pT", at, 1)
                        tr_out("pT", at, 2)
                        turned = pT[at % 2]
                        for q in range(2):
                            w = 4 * VB
                            pe.matmul(out[:, q * w:(q + 1) * w], turned[:, HALF + q, :],
                                      vr[:, (2 * half + q) * w:(2 * half + q + 1) * w],
                                      start=(q == 0), stop=False, skip_group_check=True)
                        for j in range(HALF):
                            h = half * HALF + j
                            last = pe.matmul(out[:, j * VB:(j + 1) * VB], turned[:, j, :],
                                             vm[:, h * VB:(h + 1) * VB], start=False, stop=True,
                                             skip_group_check=True)
                        last.then_inc(mm_full, 1)
                    elif what == "oT":
                        product_out(pe, kind, i, "pv", 2 * at)
                        product_out(pe, kind, i, "pv", 2 * at + 1)
                        turn(o[:], C, what, at)
                    elif what == "wo":
                        tr_out("oT", at)
                        multiply(oT, wo, C, D, what, at)
                    elif what == "x2T":
                        pe.wait_ge(x2_ready, m * T + (FROM_ONE + at + 1))
                        turn(x2[:, at, :], C, what, at)
                    elif what == "v":
                        tr_out("x2T", at)
                        multiply(x2T, wv, C, D, what, at)
                    elif what == "vT":
                        product_out(pe, kind, i, "v", at)
                        turn(val[:, at, :], C, what, at)
                    elif what == "gate":
                        tr_out("vT", at)
                        multiply(vT, wg, C, GW, what, at)
                    elif what == "hT":
                        pe.wait_ge(hid_ready, m + 1)
                        turn(hid[:, at, :], 3, what, at)
                    elif what == "w2":
                        tr_out("hT", at)
                        multiply(hT[at % 2], w2, 3, D, what, at)

            iterations(pe, body)

        @block.scalar
        def _(act):
            for w, (pair, dram, chunks) in enumerate(WEIGHTS):
                act.wait_ge(weight_in, 16 * (w + 1))
                act.activation(pair[0][:], landing(w), ACT.Copy).then_inc(weight_hi, 1)
            act.wait_ge(small_in, 80)
            act.activation(alpha[:], alpha[:], ACT.Tanh, scale=0.5).then_inc(alpha_tanh, 1)

            def body(kind, a, m, i):
                def high(out, chunks, *key):
                    k, n = use("tr", kind, i, *key)
                    act.wait_ge(tr_full, n + 1)
                    act.activation(out, trp[k][:, 0:chunks * P].rearrange("p (c n) -> p c n", c=chunks),
                                   ACT.Copy).then_inc(tr_hi, 1)

                if a is not None:
                    for t in range(T):
                        high(x1T[0][:, :, t * P:(t + 1) * P], C, "x1T", t)
                    for c in range(C):
                        k, n = use("mm", kind, i, "xq", c)
                        act.wait_ge(mm_full, n + 1)
                        act.activation(qT[:, c, :], mmp[k][:], ACT.Copy).then_inc(mm_free[k], 1)
                for n in range(END):
                    t, odd = divmod(n - 3, 2)
                    if a is not None and n >= 3 and not odd:
                        high(oT[0][:], C, "oT", t)
                    if m is not None and 0 <= n - 2 < T:
                        high(vT[0][:], C, "vT", n - 2)
                    if m is not None and n < T:
                        high(x2T[0][:], C, "x2T", n)
                    if m is not None and n == 7:
                        product_out(act, kind, i, "gate", T - 2)
                        product_out(act, kind, i, "gate", T - 1)
                        act.activation(tanh[:], gate[:, :, E + E * PV:GW], ACT.Tanh, scale=0.5) \
                           .then_inc(tanh_ready, 1)
                    if a is not None and 1 <= n <= NH:
                        for part in range(2):
                            k, u = use("tr", kind, i, "pT", n - 1, part)
                            act.wait_ge(tr_full, u + 1)
                            act.activation(pT[(n - 1) % 2][:, 4 * part:4 * part + 4, :],
                                           trp[k][:].rearrange("p (c n) -> p c n", c=4), ACT.Copy) \
                               .then_inc(tr_free[k], 1)
                    if a is not None and n < NH:
                        act.wait_ge(s_out, a * NH + n + 1)
                        for out, keys in ((probs, slice(0, P)), (probs_end, slice(P, CTX))):
                            out = out[n % 2][:].rearrange("p (j k) -> p j k", j=HALF)[:, :, 0:keys.stop - keys.start]
                            act.activation(out, shifted[:, :, keys], ACT.Exp, scale=float(DH) ** -0.5) \
                               .then_inc(exp_done, 1)
                    if m is not None and n == 8:
                        act.wait_ge(s_rel_ready, m + 1)
                        act.activation(s_exp[:], s_rel[:], ACT.Exp).then_inc(s_exp_ready, 1)
                if m is not None:
                    for t in range(T):
                        high(hT[t % 2][0][:], 3, "hT", t)

            iterations(act, body)

        @block.vector
        def _(dve):
            for w, (pair, dram, chunks) in enumerate(WEIGHTS):
                dve.wait_ge(weight_hi, w + 1)
                dve.tensor_tensor(pair[1][:], landing(w), pair[0][:].bitcast(F32), ALU.subtract) \
                   .then_inc(weight_lo, 1)
            dve.wait_ge(weight_lo, NW)
            dve.wait_ge(alpha_tanh, 1)
            dve.wait_ge(constants, 11)
            dve.tensor_scalar(alpha[:], alpha[:], 1.0, 0.5, ALU.add, ALU.mult).then_inc(tables, 1)
            dve.wait_ge(tables, 1)
            for t in (gains, shifts):
                dve.tensor_scalar(t[:, 1, :], t[:, 1, :], alpha[:, 0:1], None, ALU.mult).then_inc(tables, 1)
            dve.wait_ge(tables, 3)

            def body(kind, a, m, i):
                chain_a = Chain(dve, chain_a_sem, 2 * NH + T)
                chain_m = Chain(dve, chain_m_sem, T + 7 + 10 + 6 + T)

                def low(out, hi, chunks, what, at):
                    k, _ = use("tr", kind, i, what, at)
                    dve.wait_ge(tr_hi, hi_value(kind, i, what, at) + 1)
                    dve.tensor_tensor(out, trp[k][:, 0:chunks * P].rearrange("p (c n) -> p c n", c=chunks),
                                      hi.bitcast(F32), ALU.subtract).then_inc(tr_free[k], 1)

                def mm_ready(*key):
                    k, n = use("mm", kind, i, *key)
                    dve.wait_ge(mm_full, n + 1)
                    return k, mmp[k]

                def layernorm(out, moments, rstd):
                    return dve.tensor_scalar(out, out, moments, rstd, ALU.subtract, ALU.mult)

                def softmax_shift(n):
                    view = scores[:, :, 0:2 * CTX].rearrange("p r (c k) -> p r c k", c=2)
                    dve.wait_ge(s_full, a * NH + n + 1)
                    chain_a.link(dve.tensor_reduce(row_max[:].rearrange("p (r c) -> p r c", c=2), view, X, ALU.max), a)
                    dve.wait_ge(exp_done, a * (2 * NH) + 2 * n)
                    dve.tensor_tensor(
                        shifted[:].rearrange("p (r c) k -> p r c k", c=2), view,
                        row_max[:].rearrange("p (r c) -> p r c", c=2).unsqueeze(3).broadcast_to([P, 4, 2, CTX]),
                        ALU.subtract).then_inc(s_out, 1)

                def head_outputs(n):
                    k, bank = mm_ready("pv", n)
                    heads = bank[:, 0:HALF * VB].rearrange("p (j v) -> p j v", v=VB)
                    chain_a.link(dve.reciprocal(inv_sum[:].unsqueeze(2), heads[:, :, DH:VB]), a)
                    dve.tensor_tensor(
                        o[:, (n % 2) * 256:(n % 2 + 1) * 256].rearrange("p (c r d) -> p r c d", c=2, r=4),
                        heads[:, :, 0:DH].rearrange("p (r c) d -> p r c d", c=2),
                        inv_sum[:].rearrange("p (r c) -> p r c", c=2).unsqueeze(3).broadcast_to([P, 4, 2, DH]),
                        ALU.mult).then_inc(mm_free[k], 1)

                def add_attention(t):
                    k, bank = mm_ready("wo", t)
                    if m is not None:
                        dve.wait_ge(skip_ready, m * T + t + 1)
                    dve.tensor_tensor(x2[:, t, :], bank[:], x1[:, t, :], ALU.add).then_inc(mm_free[k], 1)
                    product_out(dve, kind, i, "wo", t)
                    chain_a.link(dve.bn_stats(stats[:], x2[:, t, :]), a)
                    dve.sem_inc(passed, 1)
                    dve.bn_aggr(mo_a[:], stats[:]).then_inc(mo_a_ready, 1)

                def finish_x2(t):
                    dve.wait_ge(rstd_a_ready, a * T + t + 1)
                    layernorm(x2[:, t, :], mo_a[:, 0:1], rstd_a[:, 0:1]).then_inc(x2_ready, 1)

                def gate_out(t):
                    k, bank = mm_ready("gate", t)
                    dve.tensor_tensor(gate[:, t, :], bank[:, 0:GW], bg[:], ALU.add).then_inc(mm_free[k], 1)
                    product_out(dve, kind, i, "gate", t)
                    pv = gate[:, t, E:E + E * PV]
                    chain_m.link(dve.tensor_tensor(square[:], pv, pv, ALU.mult), m)
                    dve.tensor_reduce(norm2[:, t, :], square[:].rearrange("p (e k) -> p e k", e=E), X, ALU.add) \
                       .then_inc(norm2_ready, 1)

                def value_out(t):
                    k, bank = mm_ready("v", t)
                    dve.tensor_tensor(val[:, t, :], bank[:], bv[:], ALU.add).then_inc(mm_free[k], 1)

                flat = both[:].rearrange("p t a e -> p (t a) e")
                flat_sq = both_sq[:].rearrange("p t a e -> p (t a) e")

                def gate_moments():
                    dve.wait_ge(norm_ready, m * T + T)
                    chain_m.link(dve.tensor_copy(both[:, :, 0, :], gate[:, :, 0:E]), m)
                    chain_m.link(dve.tensor_scalar(both[:, :, 1, :], norm[:], float(PV) ** -0.5, None, ALU.mult), m)
                    chain_m.link(dve.tensor_reduce(mean[:], flat, X, ALU.add), m)
                    chain_m.link(dve.tensor_scalar(mean[:], mean[:], 1.0 / E, None, ALU.mult), m)
                    chain_m.link(dve.tensor_tensor(flat, flat, mean[:].unsqueeze(2).broadcast_to([P, 2 * T, E]),
                                                   ALU.subtract), m)
                    chain_m.link(dve.tensor_tensor(flat_sq, flat, flat, ALU.mult), m)
                    chain_m.link(dve.tensor_reduce(spread_g[:], flat_sq, X, ALU.add), m)
                    dve.tensor_scalar(spread_g[:], spread_g[:], 1.0 / E, EPS, ALU.mult, ALU.add) \
                       .then_inc(spread_g_ready, 1)

                def gate_ranks():
                    dve.wait_ge(rstd_g_ready, m + 1)
                    over_tiles = [P, T, 2, E]
                    chain_m.link(dve.tensor_tensor(flat, flat, rstd_g[:].unsqueeze(2).broadcast_to([P, 2 * T, E]),
                                                   ALU.mult), m)
                    chain_m.link(dve.tensor_tensor(both[:], both[:], gains[:].unsqueeze(1).broadcast_to(over_tiles),
                                                   ALU.mult), m)
                    chain_m.link(dve.tensor_tensor(both[:], both[:], shifts[:].unsqueeze(1).broadcast_to(over_tiles),
                                                   ALU.add), m)
                    chain_m.link(dve.tensor_tensor(s[:], both[:, :, 0, :], both[:, :, 1, :], ALU.add), m)
                    chain_m.link(dve.tensor_reduce(s_max[:], s[:], X, ALU.max), m)
                    dve.tensor_tensor(s_rel[:], s[:], s_max[:].unsqueeze(2).broadcast_to([P, T, E]),
                                      ALU.subtract).then_inc(s_rel_ready, 1)
                    pairs = [P, T, E, E]
                    other, own = s[:].unsqueeze(2).broadcast_to(pairs), s[:].unsqueeze(3).broadcast_to(pairs)
                    chain_m.link(dve.tensor_tensor(beats[:], other, own, ALU.is_gt), m)
                    chain_m.link(dve.tensor_tensor(ties[:], other, own, ALU.is_equal), m)
                    chain_m.link(dve.tensor_tensor(ties[:], ties[:], before[:].unsqueeze(1).broadcast_to(pairs),
                                                   ALU.mult), m)
                    chain_m.link(dve.tensor_tensor(beats[:], beats[:], ties[:], ALU.add), m)
                    chain_m.link(dve.tensor_reduce(rank[:], beats[:], X, ALU.add), m)

                def weigh_hidden():
                    dve.wait_ge(s_exp_ready, m + 1)
                    dve.wait_ge(tanh_ready, m + 1)
                    w = hid[:, :, E * INNER:E * INNER + E]
                    chain_m.link(dve.scalar_tensor_tensor(rank[:], rank[:], 1.5, s_exp[:], ALU.is_lt, ALU.mult), m)
                    chain_m.link(dve.tensor_reduce(den[:], rank[:], X, ALU.add), m)
                    chain_m.link(dve.reciprocal(den[:], den[:]), m)
                    chain_m.link(dve.tensor_tensor(w, rank[:], den[:].unsqueeze(2).broadcast_to([P, T, E]),
                                                   ALU.mult), m)
                    chain_m.link(dve.tensor_scalar(half_w[:], w, 0.5, None, ALU.mult), m)
                    chain_m.link(dve.scalar_tensor_tensor(tanh[:], tanh[:], 1.0, gate[:, :, E + E * PV:GW],
                                                          ALU.add, ALU.mult), m)
                    dve.tensor_tensor(
                        hid[:, :, 0:E * INNER].rearrange("p t (e j) -> p t e j", e=E),
                        tanh[:].rearrange("p t (e j) -> p t e j", e=E),
                        half_w[:].unsqueeze(3).broadcast_to([P, T, E, INNER]), ALU.mult).then_inc(hid_ready, 1)

                def add_mixture(t):
                    k, bank = mm_ready("w2", t)
                    dve.wait_ge(skip_ready, m * T + t + 1)
                    dve.wait_ge(stored[t % 2], 16 * (m * (T // 2) + t // 2) + 16)
                    dve.tensor_tensor(y[t % 2][:], bank[:], skip[:, t, :], ALU.add).then_inc(mm_free[k], 1)
                    product_out(dve, kind, i, "w2", t)
                    chain_m.link(dve.bn_stats(stats[:], y[t % 2][:]), m)
                    dve.sem_inc(passed, 1)
                    dve.bn_aggr(mo_y[:, t % 2, :], stats[:]).then_inc(mo_y_ready, 1)

                def finish_y(t):
                    dve.wait_ge(rstd_y_ready, m * T + t + 1)
                    layernorm(y[t % 2][:], mo_y[:, t % 2, 0:1], rstd_y[:, t % 2:t % 2 + 1]).then_inc(y_ready, 1)

                if a is not None:
                    for t in range(T):
                        low(x1T[1][:, :, t * P:(t + 1) * P], x1T[0][:, :, t * P:(t + 1) * P], C, "x1T", t)
                for n in range(END + 1):
                    t, odd = divmod(n - 3, 2)
                    if a is not None and n < NH:
                        softmax_shift(n)
                    if a is not None and n >= 4 and odd:
                        finish_x2(t)
                    if a is not None and 3 <= n < END and not odd:
                        low(oT[1][:], oT[0][:], C, "oT", t)
                    if m is not None:
                        if 0 <= n - 3 < T:
                            gate_out(n - 3)
                        if 0 <= n - 2 < T:
                            low(vT[1][:], vT[0][:], C, "vT", n - 2)
                        if 0 <= n - 1 < T:
                            value_out(n - 1)
                        if n < T:
                            low(x2T[1][:], x2T[0][:], C, "x2T", n)
                        if n == 7:
                            gate_moments()
                        if n == 8:
                            gate_ranks()
                        if n == 9:
                            weigh_hidden()
                    if a is not None and 1 <= n <= NH:
                        k, u = use("tr", kind, i, "pT", n - 1, 2)
                        dve.wait_ge(tr_full, u + 1)
                        dve.tensor_copy(pT[(n - 1) % 2][:, HALF:HALF + 2, :],
                                        trp[k][:, 0:2 * P].rearrange("p (c n) -> p c n", c=2)).then_inc(tr_free[k], 1)
                        head_outputs(n - 1)
                    if a is not None and 3 <= n < END and not odd:
                        add_attention(t)
                if m is not None:
                    for t in range(T):
                        low(hT[t % 2][1][:], hT[t % 2][0][:], 3, "hT", t)
                        if t > 0:
                            finish_y(t - 1)
                        add_mixture(t)
                    finish_y(T - 1)
                if a is not None:
                    assert chain_a.n == chain_a.per_pass, chain_a.n
                if m is not None:
                    assert chain_m.n == chain_m.per_pass, chain_m.n

            dve.sem_inc(x2_ready, FROM_ONE)
            iterations(dve, body)


def build(nc, a):
    def scratch(name, shape, dt=F32):
        return nc.dram_tensor(name, shape, dt, kind="Internal").ap()

    kT = scratch("ctx_kT", [B, P, C * CTX])
    vm = scratch("ctx_vm", [B, P, HEADS * VB])
    vr = scratch("ctx_vr", [B, P, 4 * 4 * VB])
    mask = scratch("ctx_mask", [B, 2 * CTX], BF16)
    x1 = scratch("x1", [B * NT, P, D])
    context_part(nc, a["ctxT"], a["xattn_wkT"], a["xattn_wvT"], a["mask"], kT, vm, vr, mask)
    attention_part(nc, a["x_rows"], a["xT_tiles"], a["attn_wqk"], a["attn_wvT"], a["slope"], x1)
    post_part(nc, x1, kT, vm, vr, mask, a["xattn_wqT"], a["xattn_woT"], a["ffn_wvT"], a["ffn_bv"], a["gate_wT"],
              a["gate_b"], a["w2T"], a["alpha"], a["gains"], a["shifts"], a["out"])


def kernel(**inputs):
    import numpy as np
    import concourse.bacc as bacc
    from concourse.bass_utils import run_bass_kernel_spmd

    g = {k: np.asarray(v) for k, v in inputs.items()}
    f = {k[len("L0_ffn_"):]: v for k, v in g.items() if k.startswith("L0_ffn_")}
    x = g["x"].reshape(B * NT, P, D)
    experts = E * INNER
    arrays = {
        "x_rows": x,
        "xT_tiles": x.reshape(B * NT, P, C, P).transpose(0, 3, 2, 1).reshape(B * NT, P, D),
        "ctxT": g["ctx_1024"].reshape(B * CTX, D).T,
        "mask": g["mask_Bx1x1xS2_ik0"].reshape(B, CTX),
        "attn_wqk": g["L0_attn_W_qk"],
        "attn_wvT": g["L0_attn_W_v"].T,
        "slope": g["L0_attn_alibi_slope"].reshape(1, 1),
        "xattn_wkT": g["L0_xattn_Wk"].T,
        "xattn_wvT": g["L0_xattn_Wv"].T,
        "xattn_wqT": g["L0_xattn_Wq"].T,
        "xattn_woT": g["L0_xattn_Wo"].T,
        "ffn_wvT": f["Wv"].T,
        "ffn_bv": f["bv"].reshape(1, D),
        "gate_wT": np.concatenate([f["Wg"], f["Wp"].reshape(E * PV, D), f["W1"].reshape(experts, D)]).T,
        "gate_b": np.concatenate([f["bg"], np.zeros(E * PV, np.float32), f["b1"].reshape(experts)]).reshape(1, GW),
        "w2T": np.concatenate([f["W2"].transpose(0, 2, 1).reshape(experts, D), f["b2"],
                               np.zeros((HP - experts - E, D), np.float32)]),
        "alpha": f["alpha"].reshape(1, 1),
        "gains": np.concatenate([f["g_r"], f["g_c"]]).reshape(1, 2 * E),
        "shifts": np.concatenate([f["b_r"], f["b_c"]]).reshape(1, 2 * E),
    }
    arrays = {k: np.ascontiguousarray(v) for k, v in arrays.items()}
    nc = bacc.Bacc("TRN2", target_bir_lowering=False, num_devices=1)
    aps = {k: nc.dram_tensor(k + "_in", v.shape, mybir.dt.from_np(v.dtype), kind="ExternalInput").ap()
           for k, v in arrays.items()}
    aps["out"] = nc.dram_tensor("result", [B * NT, P, D], F32, kind="ExternalOutput").ap()
    build(nc, aps)
    r = run_bass_kernel_spmd(nc, [{k + "_in": v for k, v in arrays.items()}], core_ids=[0])
    return r.results[0]["result"].reshape(B, S, D)
```

```python
from contextlib import ExitStack

import concourse.bass as bass
from concourse import mybir

P = 128
B, S, D = 4, 2048, 512
C = D // P
NT = S // P
CTX = 154
CREM = CTX - P
HEADS, DH = 16, 32
E, INNER, PV = 8, 32, 8
EPS = 1e-5
GW = E + E * PV + E * INNER
HP = 3 * P
VB = DH + 1
HALF = 8
NEG = -1.0e20
FROM_ONE = 1
CUT = -3.0e38

F32 = mybir.dt.float32
F32R = mybir.dt.float32r
BF16 = mybir.dt.bfloat16
I32 = mybir.dt.int32
ALU = mybir.AluOpType
ACT = mybir.ActivationFunctionType
X = mybir.AxisListType.X


def product(pe, out, left, right, start, stop, skip=False):
    (lh, ll), (rh, rl) = left, right
    pe.matmul(out, ll, rh, start=start, stop=False, skip_group_check=skip)
    pe.matmul(out, lh, rl, start=False, stop=False, skip_group_check=skip)
    return pe.matmul(out, lh, rh, start=False, stop=stop, skip_group_check=skip)


class Chain:

    def __init__(self, engine, sem, per_pass, before=0):
        self.engine, self.sem, self.per_pass, self.n, self.before = engine, sem, per_pass, 0, before

    def link(self, ins, passes=0):
        self.n += 1
        ins.then_inc(self.sem, 1)
        self.engine.wait_ge(self.sem, passes * self.per_pass + self.before + self.n)


def context_part(nc, ctxT, wkT, wvT, mask, kT_d, vm_d, vr_d, mask_d):
    NB = B * CTX
    with ExitStack() as scope:
        def sb(name, shape, dt=F32):
            return scope.enter_context(nc.sbuf_tensor("ctx_" + name, shape, dt))

        def sem(name):
            return scope.enter_context(nc.semaphore(name))

        ctx_sb = sb("ctx_sb", [P, C, NB])
        wk = sb("wk", [P, C, D])
        wv = sb("wv", [P, C, D])
        kT = sb("kT_all", [P, B, C, CTX])
        vm = sb("vm_all", [P, B, HEADS * VB])
        vr = sb("vr_all", [P, B, 4, 4 * VB])
        mask_in = sb("mask_in", [1, B, CTX], I32)
        mask_row = sb("mask_row", [1, B, 2, CTX], BF16)
        bank = [scope.enter_context(nc.psum_tensor(f"c_bank{i}", [P, 512], F32)) for i in range(8)]

        loaded = sem("c_loaded")
        preset = sem("c_preset")
        k_full = sem("c_k_full")
        v_full = sem("c_v_full")
        k_kept = sem("c_k_kept")
        v_kept = sem("c_v_kept")
        mask_loaded = sem("c_mask_loaded")
        mask_made = sem("c_mask_made")
        stored = sem("c_stored")
        block = scope.enter_context(nc.Block())

        @block.sync
        def _(sp):
            sp.dma_start(ctx_sb[:], ctxT.rearrange("(c p) n -> p c n", p=P)).then_inc(loaded, 16)
            sp.dma_start(wk[:], wkT.rearrange("(c p) n -> p c n", p=P)).then_inc(loaded, 16)
            sp.dma_start(wv[:], wvT.rearrange("(c p) n -> p c n", p=P)).then_inc(loaded, 16)
            sp.dma_start(mask_in[:], mask.rearrange("(a b) n -> a b n", a=1)).then_inc(mask_loaded, 16)
            sp.wait_ge(mask_made, 2)
            sp.dma_start(mask_d.rearrange("(a b) n -> a b n", a=1), mask_row[:].rearrange("a b c n -> a b (c n)")) \
              .then_inc(stored, 16)
            sp.wait_ge(k_kept, 8)
            sp.dma_start(kT_d.rearrange("b p n -> p b n"), kT[:].rearrange("p b c n -> p b (c n)")).then_inc(stored, 16)
            sp.wait_ge(v_kept, B)
            sp.wait_ge(preset, 6)
            sp.dma_start(vm_d.rearrange("b p n -> p b n"), vm[:]).then_inc(stored, 16)
            sp.dma_start(vr_d.rearrange("b p n -> p b n"), vr[:].rearrange("p b q n -> p b (q n)")).then_inc(stored, 16)
            sp.wait_ge(stored, 64)

        @block.gpsimd
        def _(pool):
            pool.memset(vm[:], 1.0).then_inc(preset, 1)
            pool.memset(vr[:], 0.0).then_inc(preset, 1)
            pool.wait_ge(preset, 2)
            for j in range(4):
                pool.memset(vr[32 * j:32 * j + CREM, :, :, j * VB + DH:(j + 1) * VB], 1.0).then_inc(preset, 1)

        @block.tensor
        def _(pe):
            pe.wait_ge(loaded, 48)
            for c in range(C):
                for pair in range(2):
                    for e in range(C):
                        mm = pe.matmul(bank[2 * c + pair][:, 0:2 * CTX], wk[:, e, c * P:(c + 1) * P],
                                       ctx_sb[:, e, pair * 2 * CTX:(pair + 1) * 2 * CTX],
                                       start=(e == 0), stop=(e == C - 1))
                    mm.then_inc(k_full, 1)
            for b in range(B):
                for part, at, n in ((0, b * CTX, P), (1, b * CTX + P, CREM)):
                    pe.wait_ge(k_kept, b + 4 * part + 1)
                    for e in range(C):
                        mm = pe.matmul(bank[b + 4 * part][0:n, :], ctx_sb[:, e, at:at + n], wv[:, e, :],
                                       start=(e == 0), stop=(e == C - 1))
                mm.then_inc(v_full, 1)

        @block.scalar
        def _(act):
            for c in range(C):
                for pair in range(2):
                    act.wait_ge(k_full, 2 * c + pair + 1)
                    act.activation(kT[:, 2 * pair:2 * pair + 2, c, :],
                                   bank[2 * c + pair][:, 0:2 * CTX].rearrange("p (b n) -> p b n", b=2),
                                   ACT.Copy).then_inc(k_kept, 1)

        @block.vector
        def _(dve):
            dve.wait_ge(mask_loaded, 16)
            for copy in range(2):
                dve.tensor_scalar(mask_row[:, :, copy, :], mask_in[:], 0, NEG, ALU.is_equal, ALU.mult) \
                   .then_inc(mask_made, 1)
            dve.wait_ge(preset, 6)
            for b in range(B):
                dve.wait_ge(v_full, b + 1)
                for half in range(2):
                    dve.tensor_copy(
                        vm[:, b, half * HALF * VB:(half + 1) * HALF * VB].rearrange(
                            "p (r c v) -> p r c v", r=4, c=2)[:, :, :, 0:DH],
                        bank[b][:, half * 256:(half + 1) * 256].rearrange("p (c r d) -> p r c d", c=2, r=4))
                for j in range(4):
                    h0 = 4 * (j % 2) + j // 2
                    src = bank[4 + b][0:CREM, :].rearrange("p (a x) -> p a x", a=2)
                    for q in range(2):
                        last = dve.tensor_copy(
                            vr[32 * j:32 * j + CREM, b, :, j * VB:j * VB + DH].rearrange(
                                "p (a q) d -> p a q d", q=2)[:, :, q, :],
                            src[:, :, (h0 + 2 * q) * DH:(h0 + 2 * q + 1) * DH])
                last.then_inc(v_kept, 1)


def attention_part(nc, x_rows, xT_tiles, wqk_d, wvT_d, slope_d, x1_d):
    NCH = [(i + 4) // 4 for i in range(NT)]
    CUM = [sum(NCH[:i]) for i in range(NT + 1)]
    ROWS = CUM[NT]

    tr_of, mm_of = {}, {}

    def tr(*key):
        tr_of[key] = len(tr_of)

    def mm(*key):
        mm_of[key] = len(mm_of)

    for j in range(NT):
        mm("v", j)
    mm("q", 0)
    tr("q", 0)
    for i in range(NT + 1):
        if i + 1 < NT:
            mm("q", i + 1)
        if i > 0:
            mm("o", i - 1)
            for c in range(NCH[i - 1]):
                tr("p", i - 1, c)
        if i + 1 < NT:
            tr("q", i + 1)
    TR, MM = len(tr_of), len(mm_of)
    assert TR % 2 == 0 and MM % 2 == 0

    with ExitStack() as scope:
        def sb(name, shape, dt=F32):
            return scope.enter_context(nc.sbuf_tensor("attn_" + name, shape, dt))

        def sem(name):
            return scope.enter_context(nc.semaphore(name))

        def split(name, shape):
            return sb(name + "_hi", shape, F32R), sb(name + "_lo", shape, F32R)

        xT = split("xT", [P, C, S])
        v = split("v", [P, NT, D])
        wqk = split("wqk", [P, C, D])
        wv = split("wv", [P, C, D])
        bias = sb("alibi", [P, S])
        probs = [sb(f"probs{i}", [P, S]) for i in range(2)]
        pT = [split(f"pT{i}", [P, 512]) for i in range(2)]
        qT = split("qT", [P, C, P])
        q_row = sb("q_row", [P, D])
        x_in = [sb(f"x_in{i}", [P, D]) for i in range(2)]
        res = [sb(f"res{i}", [P, D]) for i in range(2)]
        ident = sb("ident", [P, P])
        slope = sb("slope", [P, 1])
        chunk_max = sb("chunk_max", [P, 4])
        neg_max = sb("neg_max", [P, 2])
        row_sum = sb("row_sum", [P, 2])
        inv_sum = sb("inv_sum", [P, 1])
        stats = sb("stats", [P, 6])
        moments = sb("moments", [P, 2])
        spread = sb("spread", [P, 1])
        rstd = sb("rstd", [P, 1])
        minus_half = sb("minus_half", [P, 1])
        eps = sb("eps", [P, 1])
        unused = sb("unused", [P, 2])
        scores = [scope.enter_context(nc.psum_tensor(f"scores{i}", [P, 512], F32)) for i in range(4)]
        trp = [scope.enter_context(nc.psum_tensor(f"a_trp{i}", [P, 512], F32)) for i in range(2)]
        mmp = [scope.enter_context(nc.psum_tensor(f"a_mmp{i}", [P, 512], F32)) for i in range(2)]

        weight_in = sem("a_weight_in")
        weight_hi = sem("a_weight_hi")
        weight_lo = sem("a_weight_lo")
        slope_in = sem("a_slope_in")
        constants = sem("a_constants")
        x_in_full = [sem(f"a_x_in_full{i}") for i in range(2)]
        xT_hi = sem("a_xT_hi")
        xT_lo = sem("a_xT_lo")
        res_full = [sem(f"a_res_full{i}") for i in range(2)]
        stored = [sem(f"a_stored{i}") for i in range(2)]
        tr_full = sem("a_tr_full")
        tr_hi = sem("a_tr_hi")
        tr_free = [sem(f"a_tr_free{i}") for i in range(2)]
        v_full = sem("a_v_full")
        q_full = sem("a_q_full")
        v_hi = sem("a_v_hi")
        mm_free = [sem(f"a_mm_free{i}") for i in range(2)]
        s_full = sem("a_s_full")
        s_free = sem("a_s_free")
        max_ready = sem("a_max_ready")
        exp_done = sem("a_exp_done")
        pv_done = sem("a_pv_done")
        moments_ready = sem("a_moments_ready")
        spread_ready = sem("a_spread_ready")
        rstd_ready = sem("a_rstd_ready")
        x1_ready = sem("a_x1_ready")
        chain_sem = sem("a_chain")
        passed = sem("a_passed")
        block = scope.enter_context(nc.Block())

        def tr_split(b, n):
            return tr_free[n % 2], b * (TR // 2) + (FROM_ONE + n // 2 + 1)

        def mm_out(b, n):
            return mm_free[n % 2], b * (MM // 2) + (FROM_ONE + n // 2 + 1)

        stage = [probs[i][:].rearrange("p (c n) -> p c n", c=C) for i in range(2)]

        @block.sync
        def _(sp):
            sp.dma_start(stage[0], wqk_d.rearrange("(c p) n -> p c n", p=P)).then_inc(weight_in, 16)
            sp.wait_ge(weight_in, 16)
            sp.dma_start(stage[1], wvT_d.rearrange("(c p) n -> p c n", p=P)).then_inc(weight_in, 16)
            sp.dma_start(slope[:], slope_d.broadcast_to([P, 1])).then_inc(slope_in, 16)
            with sp.Fori(0, B) as b:
                for j in range(NT):
                    sp.wait_ge(xT_lo, b * NT + (FROM_ONE + max(j - 1, 0)))
                    sp.dma_start(x_in[j % 2][:], xT_tiles[bass.ds(b * NT + j, 1)].rearrange("a p n -> p (a n)")) \
                      .then_inc(x_in_full[j % 2], 16)

        @block.gpsimd
        def _(pool):
            pool.memset(ident[:], 0.0).then_inc(constants, 1)
            pool.wait_ge(constants, 1)
            pool.affine_select(out=ident[:], in_=ident[:], compare_op=ALU.not_equal, fill=1.0, base=0,
                               pattern=[[-1, P]], channel_multiplier=1).then_inc(constants, 1)
            pool.iota(bias[:], pattern=[[1, S]], base=-(S - P), channel_multiplier=-1,
                      allow_small_or_imprecise_dtypes=True).then_inc(constants, 1)
            pool.wait_ge(slope_in, 16)
            pool.wait_ge(constants, 3)
            pool.tensor_scalar(bias[:], bias[:], slope[:, 0:1], None, ALU.mult).then_inc(constants, 1)
            pool.wait_ge(constants, 4)
            pool.affine_select(out=bias[:], in_=bias[:], compare_op=ALU.is_ge, fill=CUT, base=S - P,
                               pattern=[[-1, S]], channel_multiplier=1).then_inc(constants, 1)
            pool.memset(minus_half[:], -0.5).then_inc(constants, 1)
            pool.memset(eps[:], EPS).then_inc(constants, 1)
            pool.wait_ge(constants, 7)
            for k, free in enumerate(stored):
                pool.dma_start(unused[:, k:k + 1], slope_d.broadcast_to([P, 1])).then_inc(free, 16)
            with pool.Fori(0, B) as b:
                for i in range(NT + 1):
                    if i < NT:
                        pool.wait_ge(stored[i % 2], 16 * (b * (NT // 2) + i // 2) + 16)
                        pool.sem_inc(passed, 1)
                        pool.dma_start(res[i % 2][:], x_rows[bass.ds(b * NT + i, 1)].rearrange("a p n -> p (a n)")) \
                            .then_inc(res_full[i % 2], 16)
                    if i > 0:
                        pool.wait_ge(moments_ready, b * NT + i)
                        pool.tensor_tensor(spread[:], moments[:, 1:2], eps[:], ALU.add).then_inc(spread_ready, 1)
                        pool.wait_ge(spread_ready, b * NT + i)
                        pool.tensor_tensor(rstd[:], spread[:], minus_half[:], ALU.pow).then_inc(rstd_ready, 1)
                        pool.wait_ge(x1_ready, b * NT + i)
                        pool.sem_inc(passed, 1)
                        pool.dma_start(x1_d[bass.ds(b * NT + i - 1, 1)].rearrange("a p n -> p (a n)"),
                                       res[(i - 1) % 2][:]).then_inc(stored[(i - 1) % 2], 16)
            for k in range(2):
                pool.wait_ge(stored[k], 16 * B * NT // 2 + 16)

        @block.tensor
        def _(pe):
            pe.wait_ge(weight_lo, 2)
            pe.wait_ge(constants, 2)
            for free in (s_full, pv_done):
                pe.sem_inc(free, FROM_ONE)
            with pe.Fori(0, B) as b:
                def tr_bank(*key):
                    n = tr_of[key]
                    pe.wait_ge(tr_free[n % 2], b * (TR // 2) + (FROM_ONE + n // 2))
                    return trp[n % 2]

                def mm_bank(*key):
                    n = mm_of[key]
                    pe.wait_ge(mm_free[n % 2], b * (MM // 2) + (FROM_ONE + n // 2))
                    return mmp[n % 2]

                def q_row_product(i):
                    out = mm_bank("q", i)
                    for c in range(C):
                        last = product(pe, out[:], [t[:, c, i * P:(i + 1) * P] for t in xT],
                                       [t[:, c, :] for t in wqk], c == 0, c == C - 1)
                    last.then_inc(q_full, 1)

                def q_transpose(i):
                    pe.wait_ge(*mm_out(b, mm_of["q", i]))
                    out = tr_bank("q", i)
                    for c in range(C):
                        last = pe.transpose(out[:, c * P:(c + 1) * P], q_row[:, c * P:(c + 1) * P], ident[:])
                    last.then_inc(tr_full, 1)

                def score_rows(i):
                    pe.wait_ge(*tr_split(b, tr_of["q", i]))
                    for k in range(NCH[i]):
                        earlier = CUM[i - 1] + k + 1 if i > 0 and k < NCH[i - 1] else 0
                        pe.wait_ge(s_free, b * ROWS + (FROM_ONE + earlier))
                        w = min(512, (i + 1) * P - k * 512)
                        for c in range(C):
                            last = product(pe, scores[k][:, 0:w], [t[:, c, :] for t in qT],
                                           [t[:, c, k * 512:k * 512 + w] for t in xT], c == 0, c == C - 1)
                        last.then_inc(s_full, 1)

                def probs_transpose(i, k):
                    out = tr_bank("p", i, k)
                    n = min(4, i + 1 - 4 * k)
                    for t in range(n):
                        at = (4 * k + t) * P
                        last = pe.transpose(out[:, t * P:(t + 1) * P], probs[i % 2][:, at:at + P], ident[:])
                    last.then_inc(tr_full, 1)

                def values(i):
                    pe.wait_ge(exp_done, b * NT + i + 1)
                    out = mm_bank("o", i)
                    probs_transpose(i, 0)
                    for k in range(NCH[i]):
                        if k + 1 < NCH[i]:
                            probs_transpose(i, k + 1)
                        pe.wait_ge(*tr_split(b, tr_of["p", i, k]))
                        n = min(4, i + 1 - 4 * k)
                        for t in range(n):
                            last = product(pe, out[:], [h[:, t * P:(t + 1) * P] for h in pT[(CUM[i] + k) % 2]],
                                           [h[:, 4 * k + t, :] for h in v], 4 * k + t == 0, 4 * k + t == i)
                        last.then_inc(pv_done, 1)

                for j in range(NT):
                    pe.wait_ge(xT_lo, b * NT + (FROM_ONE + j + 1))
                    out = mm_bank("v", j)
                    for c in range(C):
                        last = product(pe, out[:], [t[:, c, j * P:(j + 1) * P] for t in xT],
                                       [t[:, c, :] for t in wv], c == 0, c == C - 1)
                    last.then_inc(v_full, 1)
                q_row_product(0)
                q_transpose(0)
                for i in range(NT + 1):
                    if i < NT:
                        score_rows(i)
                    if i + 1 < NT:
                        q_row_product(i + 1)
                    if i > 0:
                        values(i - 1)
                    if i + 1 < NT:
                        q_transpose(i + 1)

        def exps(act, b, i):
            act.wait_ge(max_ready, b * NT + i + 1)
            act.activation(probs[i % 2][:, 0:(i + 1) * P], probs[i % 2][:, 0:(i + 1) * P], ACT.Exp,
                           bias=neg_max[:, i % 2:i % 2 + 1],
                           accum_out=row_sum[:, i % 2:i % 2 + 1]).then_inc(exp_done, 1)

        @block.scalar
        def _(act):
            for w, pair in enumerate((wqk, wv)):
                act.wait_ge(weight_in, 16 * (w + 1))
                act.activation(pair[0][:], stage[w], ACT.Copy).then_inc(weight_hi, 1)
            with act.Fori(0, B) as b:
                def high(out, *key):
                    n = tr_of[key]
                    act.wait_ge(tr_full, b * TR + n + 1)
                    w = out.shape[-1] if len(out.shape) == 2 else 512
                    src = trp[n % 2][:, 0:w]
                    if len(out.shape) == 3:
                        src = src.rearrange("p (c n) -> p c n", c=C)
                    act.activation(out, src, ACT.Copy).then_inc(tr_hi, 1)

                def q_out(i):
                    n = mm_of["q", i]
                    act.wait_ge(q_full, b * NT + i + 1)
                    act.activation(q_row[:], mmp[n % 2][:], ACT.Copy, scale=float(D) ** -0.5) \
                       .then_inc(mm_free[n % 2], 1)

                def v_high(j):
                    n = mm_of["v", j]
                    act.wait_ge(v_full, b * NT + j + 1)
                    act.activation(v[0][:, j, :], mmp[n % 2][:], ACT.Copy).then_inc(v_hi, 1)

                for j in range(NT):
                    act.wait_ge(x_in_full[j % 2], 16 * (b * (NT // 2) + j // 2 + 1))
                    act.wait_ge(s_full, b * ROWS + FROM_ONE)
                    act.activation(xT[0][:, :, j * P:(j + 1) * P], x_in[j % 2][:].rearrange("p (c n) -> p c n", c=C),
                                   ACT.Copy).then_inc(xT_hi, 1)
                    if j > 0:
                        v_high(j - 1)
                v_high(NT - 1)
                q_out(0)
                high(qT[0][:], "q", 0)
                for i in range(NT + 1):
                    if i + 1 < NT:
                        q_out(i + 1)
                    if i > 0:
                        for k in range(NCH[i - 1]):
                            m = CUM[i - 1] + k
                            act.wait_ge(pv_done, b * ROWS + (FROM_ONE + max(m - 1, 0)))
                            w = min(512, i * P - k * 512)
                            high(pT[m % 2][0][:, 0:w], "p", i - 1, k)
                            if k == 0 and i < NT:
                                exps(act, b, i)
                    elif i < NT:
                        exps(act, b, i)
                    if i + 1 < NT:
                        high(qT[0][:], "q", i + 1)

        @block.vector
        def _(dve):
            for w, pair in enumerate((wqk, wv)):
                dve.wait_ge(weight_hi, w + 1)
                dve.tensor_tensor(pair[1][:], stage[w], pair[0][:].bitcast(F32), ALU.subtract).then_inc(weight_lo, 1)
            dve.wait_ge(weight_lo, 2)
            dve.wait_ge(constants, 7)
            for free in (*tr_free, *mm_free, s_free, xT_lo):
                dve.sem_inc(free, FROM_ONE)
            with dve.Fori(0, B) as b:
                chain = Chain(dve, chain_sem, NT * 2)

                def low(pair_lo, pair_hi, *key):
                    n = tr_of[key]
                    dve.wait_ge(tr_hi, b * TR + n + 1)
                    w = pair_lo.shape[-1] if len(pair_lo.shape) == 2 else 512
                    src = trp[n % 2][:, 0:w]
                    if len(pair_lo.shape) == 3:
                        src = src.rearrange("p (c n) -> p c n", c=C)
                    dve.tensor_tensor(pair_lo, src, pair_hi.bitcast(F32), ALU.subtract).then_inc(tr_free[n % 2], 1)

                def v_low(j):
                    n = mm_of["v", j]
                    dve.wait_ge(v_hi, b * NT + j + 1)
                    dve.tensor_tensor(v[1][:, j, :], mmp[n % 2][:], v[0][:, j, :].bitcast(F32), ALU.subtract) \
                       .then_inc(mm_free[n % 2], 1)

                def biased(i):
                    for k in range(NCH[i]):
                        w = min(512, (i + 1) * P - k * 512)
                        at = S - (i + 1) * P + k * 512
                        dve.wait_ge(s_full, b * ROWS + (FROM_ONE + CUM[i] + k + 1))
                        dve.sem_inc(passed, 1)
                        dve.tensor_tensor_reduce(probs[i % 2][:, k * 512:k * 512 + w], scores[k][:, 0:w],
                                                 bias[:, at:at + w], 1.0, CUT, ALU.add, ALU.max,
                                                 chunk_max[:, k:k + 1]).then_inc(s_free, 1)
                    dve.wait_ge(s_free, b * ROWS + (FROM_ONE + CUM[i + 1]))
                    dve.tensor_reduce(neg_max[:, i % 2:i % 2 + 1], chunk_max[:, 0:NCH[i]], X, ALU.max,
                                      negate=True).then_inc(max_ready, 1)

                def finish(i):
                    r = res[i % 2]
                    n = mm_of["o", i]
                    chain.link(dve.reciprocal(inv_sum[:], row_sum[:, i % 2:i % 2 + 1]), b)
                    dve.wait_ge(res_full[i % 2], 16 * (b * (NT // 2) + i // 2 + 1))
                    dve.wait_ge(pv_done, b * ROWS + (FROM_ONE + CUM[i + 1]))
                    dve.scalar_tensor_tensor(r[:], mmp[n % 2][:], inv_sum[:, 0:1], r[:],
                                             ALU.mult, ALU.add).then_inc(mm_free[n % 2], 1)
                    dve.wait_ge(*mm_out(b, n))
                    chain.link(dve.bn_stats(stats[:], r[:]), b)
                    dve.sem_inc(passed, 1)
                    dve.bn_aggr(moments[:], stats[:]).then_inc(moments_ready, 1)

                def normalise(i):
                    r = res[i % 2]
                    dve.wait_ge(rstd_ready, b * NT + i + 1)
                    dve.tensor_scalar(r[:], r[:], moments[:, 0:1], rstd[:, 0:1],
                                      ALU.subtract, ALU.mult).then_inc(x1_ready, 1)

                for j in range(NT):
                    dve.wait_ge(xT_hi, b * NT + j + 1)
                    dve.tensor_tensor(xT[1][:, :, j * P:(j + 1) * P], x_in[j % 2][:].rearrange("p (c n) -> p c n", c=C),
                                      xT[0][:, :, j * P:(j + 1) * P].bitcast(F32), ALU.subtract).then_inc(xT_lo, 1)
                    if j > 0:
                        v_low(j - 1)
                v_low(NT - 1)
                low(qT[1][:], qT[0][:], "q", 0)
                for i in range(NT + 1):
                    if i < NT:
                        biased(i)
                    if i > 1:
                        normalise(i - 2)
                    if i > 0:
                        for k in range(NCH[i - 1]):
                            m = CUM[i - 1] + k
                            w = min(512, i * P - k * 512)
                            low(pT[m % 2][1][:, 0:w], pT[m % 2][0][:, 0:w], "p", i - 1, k)
                    if i + 1 < NT:
                        low(qT[1][:], qT[0][:], "q", i + 1)
                    if i > 0:
                        finish(i - 1)
                normalise(NT - 1)
                assert chain.n == chain.per_pass


def post_part(nc, x1_d, kT_d, vm_d, vr_d, mask_d, wq_d, wo_d, wv_d, bv_d, wg_d, bg_d, w2_d, alpha_d,
              gain_d, shift_d, out_d):
    T = 4
    G = B * NT // T
    NH = 2 * T
    KINDS = {"Q": 1, "QA": 1, "QAM": 1, "QAMF": G - 3, "AMF": 1, "MF": 1, "F": 1}
    SCHEDULE = """
        scores.0 xq.2 x2T.0 exps.0 xq.3 ranks v.0 gate_exp x2T.1
        scores.1 pT.0.0 pT.0.1 v.1  pT.0.2 exps.1 vT.0 pv.0 weigh
        scores.2 pT.1.0 pT.1.1 gate.0 pT.1.2 exps.2 vT.1 pv.1 hT.0
        scores.3 pT.2.0 pT.2.1 w2.0 pT.2.2 oT.0 skip.0 exps.3 gate.1 hT.1 y.0 x2T.2 pv.2 wo.0
        scores.4 pT.3.0 pT.3.1 w2.1 pT.3.2 hT.2 skip.1 exps.4 x2.0 v.2 y.1 x2T.3 pv.3 vT.2
        scores.5 pT.4.0 pT.4.1 w2.2 pT.4.2 oT.1 skip.2 exps.5 gate.2 hT.3 y.2 pv.4 wo.1
        scores.6 pT.5.0 pT.5.1 v.3  pT.5.2 x1T.0 exps.6 x2.1 pv.5 x1T.1 vT.3
        scores.7 pT.6.0 pT.6.1 w2.3 pT.6.2 oT.2 skip.3 exps.7 x1T.2 y.3 pv.6 wo.2
        pT.7.0 pT.7.1 gate.3 pT.7.2 x1T.3 tanh x2.2 pv.7
        xq.0 oT.3 xq.1 moments wo.3 x2.3
    """
    STAGE = {step: stage for stage, steps in {
        "Q": "x1T xq.0 xq.1",
        "A": "xq.2 xq.3 scores exps pT pv oT wo x2",
        "M": "x2T v skip vT gate tanh moments",
        "F": "ranks gate_exp weigh hT w2 y"}.items() for step in steps.split()}

    def plan(kind):
        steps = [step for step in SCHEDULE.split()
                 if STAGE[step if step.startswith("xq") else step.split(".")[0]] in kind]
        return [(name, *map(int, at)) for name, *at in (step.split(".") for step in steps)]

    TRANSPOSES = ("x1T", "pT", "oT", "x2T", "vT", "hT")
    SPLIT = ("x1T", "oT", "x2T", "vT", "hT")
    PRODUCTS = ("xq", "pv", "wo", "v", "gate", "w2")
    PLANS = {kind: plan(kind) for kind in KINDS}
    uses = {ring: {kind: [s for s in plan if s[0] in names] for kind, plan in PLANS.items()}
            for ring, names in (("tr", TRANSPOSES), ("mm", PRODUCTS), ("hi", SPLIT))}

    def position(ring, kind, i, key, per=1):
        n, before = uses[ring][kind].index(key), 0
        for other, times in KINDS.items():
            if other == kind:
                break
            before += times * len(uses[ring][other])
        count = len(uses[ring][kind])
        assert per == 1 or (count % per == 0 and before % per == 0)
        fixed = before // per + n // per
        return i * (count // per) + fixed if KINDS[kind] > 1 else fixed

    def use(ring, kind, i, *key):
        return uses[ring][kind].index(key) % 2, position(ring, kind, i, key)

    def bank_use(ring, kind, i, *key):
        return uses[ring][kind].index(key) % 2, position(ring, kind, i, key, 2)

    with ExitStack() as scope:
        def sb(name, shape, dt=F32):
            return scope.enter_context(nc.sbuf_tensor("post_" + name, shape, dt))

        def sem(name):
            return scope.enter_context(nc.semaphore("p_" + name))

        def split(name, shape):
            return sb(name + "_hi", shape, F32R), sb(name + "_lo", shape, F32R)

        wq, wo, wv = (split(n, [P, C, D]) for n in ("wq", "wo", "wv"))
        wg = split("wg", [P, C, GW])
        w2 = split("w2", [P, 3, D])
        kT = sb("kT", [P, C, CTX])
        vm = sb("vm", [P, HEADS * VB])
        vr = sb("vr", [P, 4 * 4 * VB])
        mask_row = sb("mask_row", [P, 2 * CTX], BF16)
        ones = sb("ones", [P, P], BF16)
        x1 = sb("x1", [P, T, D])
        x1_res = [sb(f"x1_res{i}", [P, D]) for i in range(2)]
        x1T = split("x1T", [P, C, T * P])
        qT = sb("qT", [P, C, T * P])
        shifted = sb("shifted", [P, HALF, CTX])
        probs = [sb(f"probs{i}", [P, HALF * P]) for i in range(2)]
        probs_end = [sb(f"probs_end{i}", [P, HALF * 32]) for i in range(2)]
        pT = [sb(f"pT{i}", [P, HALF + 2, P]) for i in range(2)]
        o = sb("o", [P, D])
        oT = split("oT", [P, C, P])
        x2 = sb("x2", [P, T, D])
        x2T = split("x2T", [P, C, P])
        val = sb("val", [P, T, D])
        vT = split("vT", [P, C, P])
        skip = sb("skip", [P, T, D])
        gate = sb("gate", [P, T, GW])
        hid = sb("hid", [P, T, HP])
        hT = [split(f"hT{i}", [P, 3, P]) for i in range(2)]
        y = [sb(f"y{i}", [P, D]) for i in range(2)]
        bv = sb("bv", [P, D])
        bg = sb("bg", [P, GW])
        alpha = sb("alpha", [P, 1])
        gains = sb("gains", [P, 2, E])
        shifts = sb("shifts", [P, 2, E])
        before = sb("before", [P, E, E])
        ident = sb("ident", [P, P])
        minus_half = sb("minus_half", [P, 2 * T])
        plus_half = sb("plus_half", [P, E])
        eps = sb("eps", [P, 1])
        unused = sb("unused", [P, 2])
        row_max = sb("row_max", [P, HALF])
        inv_sum = sb("inv_sum", [P, HALF])
        stats = sb("stats", [P, 6])
        mo_a = sb("mo_a", [P, 2])
        spread_a = sb("spread_a", [P, 1])
        rstd_a = sb("rstd_a", [P, 1])
        mo_y = sb("mo_y", [P, 2, 2])
        spread_y = sb("spread_y", [P, 2])
        rstd_y = sb("rstd_y", [P, 2])
        square = sb("square", [P, E * PV])
        norm2 = sb("norm2", [P, T, E])
        norm = sb("norm", [P, T, E])
        both = sb("both", [P, T, 2, E])
        both_sq = sb("both_sq", [P, T, 2, E])
        mean = sb("mean", [P, T * 2])
        spread_g = sb("spread_g", [P, T * 2])
        rstd_g = sb("rstd_g", [P, T * 2])
        s = sb("s", [P, T, E])
        s_max = sb("s_max", [P, T])
        s_rel = sb("s_rel", [P, T, E])
        s_exp = sb("s_exp", [P, T, E])
        beats = sb("beats", [P, T, E, E])
        ties = sb("ties", [P, T, E, E])
        rank = sb("rank", [P, T, E])
        den = sb("den", [P, T])
        half_w = sb("half_w", [P, T, E])
        scores = scope.enter_context(nc.psum_tensor("p_scores", [P, 4, 512], F32))
        trp = [scope.enter_context(nc.psum_tensor(f"p_trp{i}", [P, 512], F32)) for i in range(2)]
        mmp = [scope.enter_context(nc.psum_tensor(f"p_mmp{i}", [P, 512], F32)) for i in range(2)]

        weight_in = sem("weight_in")
        weight_hi = sem("weight_hi")
        weight_lo = sem("weight_lo")
        small_in = sem("small_in")
        constants = sem("constants")
        tables = sem("tables")
        alpha_tanh = sem("alpha_tanh")
        x1_in = sem("x1_in")
        x1_res_in = [sem(f"x1_res_in{i}") for i in range(2)]
        keys_in = sem("keys_in")
        values_in = sem("values_in")
        tr_full = sem("tr_full")
        tr_hi = sem("tr_hi")
        tr_free = [sem(f"tr_free{i}") for i in range(2)]
        mm_full = sem("mm_full")
        mm_free = [sem(f"mm_free{i}") for i in range(2)]
        q_out = sem("q_out")
        s_full = sem("s_full")
        s_out = sem("s_out")
        exp_done = sem("exp_done")
        mo_a_ready = sem("mo_a_ready")
        spread_a_ready = sem("spread_a_ready")
        rstd_a_ready = sem("rstd_a_ready")
        x2_ready = sem("x2_ready")
        skip_ready = sem("skip_ready")
        norm2_ready = sem("norm2_ready")
        norm_ready = sem("norm_ready")
        spread_g_ready = sem("spread_g_ready")
        rstd_g_ready = sem("rstd_g_ready")
        tanh_ready = sem("tanh_ready")
        s_rel_ready = sem("s_rel_ready")
        s_exp_ready = sem("s_exp_ready")
        hid_ready = sem("hid_ready")
        mo_y_ready = sem("mo_y_ready")
        spread_y_ready = sem("spread_y_ready")
        rstd_y_ready = sem("rstd_y_ready")
        y_ready = sem("y_ready")
        stored = [sem(f"stored{i}") for i in range(2)]
        chain_a_sem = sem("chain_a")
        chain_m_sem = sem("chain_m")
        chain_f_sem = sem("chain_f")
        passed = sem("passed")
        block = scope.enter_context(nc.Block())

        landings = [skip, val]
        WEIGHTS = [(wq, wq_d, C), (wo, wo_d, C), (wv, wv_d, C), (wg, wg_d, C), (w2, w2_d, 3)]
        NW = len(WEIGHTS)

        def landing(w):
            _, dram, chunks = WEIGHTS[w]
            n = dram.shape[-1]
            return landings[w % 2][:].rearrange("p t n -> p (t n)")[:, 0:chunks * n].rearrange("p (c n) -> p c n", c=chunks)

        def high_taken(engine, kind, i, *key):
            engine.wait_ge(tr_hi, position("hi", kind, i, key) + 1)

        def product_out(engine, kind, i, *key):
            k, n = bank_use("mm", kind, i, *key)
            engine.wait_ge(mm_free[k], n + 1)

        def iterations(engine, body):
            body("Q", 0, None, None, None, 0)
            body("QA", 1, 0, None, None, 0)
            body("QAM", 2, 1, 0, None, 0)
            with engine.Fori(0, G - 3) as i:
                body("QAMF", i + 3, i + 2, i + 1, i, i)
            body("AMF", None, G - 1, G - 2, G - 3, 0)
            body("MF", None, None, G - 1, G - 2, 0)
            body("F", None, None, None, G - 1, 0)

        @block.sync
        def _(sp):
            for w, (_, dram, chunks) in enumerate(WEIGHTS):
                if w >= 2:
                    sp.wait_ge(weight_lo, w - 1)
                if w == 1:
                    for t, src in ((bv, bv_d), (bg, bg_d), (alpha, alpha_d)):
                        sp.dma_start(t[:], src.broadcast_to([P, src.shape[-1]])).then_inc(small_in, 16)
                    for t, src in ((gains, gain_d), (shifts, shift_d)):
                        sp.dma_start(t[:].rearrange("p a e -> p (a e)"), src.broadcast_to([P, 2 * E])) \
                          .then_inc(small_in, 16)
                sp.dma_start(landing(w), dram.rearrange("(c p) n -> p c n", p=P)).then_inc(weight_in, 16)
                sp.wait_ge(weight_in, 16 * (w + 1))

            def load_x1(g):
                sp.dma_start(x1[:], x1_d[bass.ds(g * T, T)].rearrange("t p n -> p t n")).then_inc(x1_in, 16)

            def load_keys(g):
                b = g // (NT // T)
                sp.dma_start(mask_row[0:97:32, :], mask_d[bass.ds(b, 1)].broadcast_to([4, 2 * CTX])) \
                  .then_inc(keys_in, 16)
                sp.dma_start(kT[:].rearrange("p c n -> p (c n)"),
                             kT_d[bass.ds(b, 1)].rearrange("a p n -> p (a n)")).then_inc(keys_in, 16)

            def load_values(g):
                b = g // (NT // T)
                sp.dma_start(vm[:], vm_d[bass.ds(b, 1)].rearrange("a p n -> p (a n)")).then_inc(values_in, 16)
                sp.dma_start(vr[:], vr_d[bass.ds(b, 1)].rearrange("a p n -> p (a n)")).then_inc(values_in, 16)

            def body(a, last=False):
                if not last:
                    sp.wait_ge(s_full, a * NH + 1)
                    load_x1(a + 1)
                for t in range(T):
                    if t >= 2 or not isinstance(a, int) or a > 0:
                        sp.wait_ge(mo_a_ready, a * T + (t - 1))
                    sp.dma_start(x1_res[t % 2][:], x1_d[bass.ds(a * T + t, 1)].rearrange("a p n -> p (a n)")) \
                      .then_inc(x1_res_in[t % 2], 16)
                if not last:
                    sp.wait_ge(s_full, a * NH + NH)
                    load_keys(a + 1)
                    sp.wait_ge(mo_a_ready, a * T + T)
                    load_values(a + 1)

            load_x1(0)
            load_keys(0)
            load_values(0)
            body(0)
            with sp.Fori(0, G - 2) as i:
                body(i + 1)
            body(G - 1, last=True)

        @block.gpsimd
        def _(pool):
            pool.memset(ident[:], 0.0).then_inc(constants, 1)
            pool.memset(before[:], 1.0).then_inc(constants, 1)
            pool.memset(ones[:], 1.0).then_inc(constants, 1)
            pool.memset(hid[:], 0.0).then_inc(constants, 1)
            pool.memset(minus_half[:], -0.5).then_inc(constants, 1)
            pool.memset(plus_half[:], 0.5).then_inc(constants, 1)
            pool.memset(probs_end[0][:], 0.0).then_inc(constants, 1)
            pool.memset(probs_end[1][:], 0.0).then_inc(constants, 1)
            pool.memset(eps[:], EPS).then_inc(constants, 1)
            pool.wait_ge(constants, 9)
            pool.affine_select(out=ident[:], in_=ident[:], compare_op=ALU.not_equal, fill=1.0, base=0,
                               pattern=[[-1, P]], channel_multiplier=1).then_inc(constants, 1)
            pool.affine_select(out=before[:], in_=before[:], compare_op=ALU.is_gt, fill=0.0, base=0,
                               pattern=[[1, E], [-1, E]], channel_multiplier=0).then_inc(constants, 1)
            pool.wait_ge(constants, 11)

            def body(kind, q, a, m, f, i):
                for what, *at in PLANS[kind]:
                    t = at[0] if at else 0
                    if what == "w2":
                        pool.wait_ge(mo_y_ready, f * T + t + 1)
                        k = t % 2
                        pool.tensor_tensor(spread_y[:, k:k + 1], mo_y[:, k, 1:2], eps[:], ALU.add) \
                            .then_inc(spread_y_ready, 1)
                        pool.wait_ge(spread_y_ready, f * T + t + 1)
                        pool.tensor_tensor(rstd_y[:, k:k + 1], spread_y[:, k:k + 1], minus_half[:, 0:1],
                                           ALU.pow).then_inc(rstd_y_ready, 1)
                    elif what == "y":
                        pool.wait_ge(y_ready, f * T + t + 1)
                        pool.sem_inc(passed, 1)
                        pool.dma_start(out_d[bass.ds(f * T + t, 1)].rearrange("a p n -> p (a n)"),
                                       y[t % 2][:]).then_inc(stored[t % 2], 16)
                    elif what == "gate":
                        pool.wait_ge(norm2_ready, m * T + t + 1)
                        pool.tensor_tensor(norm[:, t, :], norm2[:, t, :], plus_half[:], ALU.pow).then_inc(norm_ready, 1)
                    elif what == "skip":
                        product_out(pool, kind, i, "v", t)
                        if f is not None:
                            product_out(pool, kind, i, "w2", t)
                        pool.tensor_tensor(skip[:, t, :], val[:, t, :], x2[:, t, :], ALU.add).then_inc(skip_ready, 1)
                    elif what == "wo":
                        pool.wait_ge(mo_a_ready, a * T + t + 1)
                        pool.tensor_tensor(spread_a[:], mo_a[:, 1:2], eps[:], ALU.add).then_inc(spread_a_ready, 1)
                        pool.wait_ge(spread_a_ready, a * T + t + 1)
                        pool.tensor_tensor(rstd_a[:], spread_a[:], minus_half[:, 0:1], ALU.pow) \
                            .then_inc(rstd_a_ready, 1)
                    elif what == "moments":
                        pool.wait_ge(spread_g_ready, m + 1)
                        pool.tensor_tensor(rstd_g[:], spread_g[:], minus_half[:], ALU.pow).then_inc(rstd_g_ready, 1)

            for k, free in enumerate(stored):
                pool.dma_start(unused[:, k:k + 1], alpha_d.broadcast_to([P, 1])).then_inc(free, 16)
            iterations(pool, body)
            for k in range(2):
                pool.wait_ge(stored[k], 16 * G * T // 2 + 16)

        @block.tensor
        def _(pe):
            pe.wait_ge(constants, 11)

            def body(kind, q, a, m, f, i):
                def tr_bank(*key):
                    k, n = bank_use("tr", kind, i, *key)
                    pe.wait_ge(tr_free[k], n)
                    return trp[k]

                def mm_bank(*key):
                    k, n = bank_use("mm", kind, i, *key)
                    pe.wait_ge(mm_free[k], n)
                    return mmp[k]

                def tr_out(*key):
                    k, n = bank_use("tr", kind, i, *key)
                    pe.wait_ge(tr_free[k], n + 1)

                def q_ready(a, half):
                    pe.wait_ge(q_out, a * C + 2 * half + 2)

                def turn(src, chunks, *key):
                    out = tr_bank(*key)
                    for c in range(chunks):
                        last = pe.transpose(out[:, c * P:(c + 1) * P], src[:, c * P:(c + 1) * P], ident[:])
                    last.then_inc(tr_full, 1)

                def multiply(left, right, chunks, width, *key):
                    out = mm_bank(*key)
                    for c in range(chunks):
                        last = product(pe, out[:, 0:width], [h[:, c, :] for h in left], [h[:, c, :] for h in right],
                                       c == 0, c == chunks - 1)
                    last.then_inc(mm_full, 1)

                pe.wait_ge(weight_lo, {"Q": 1, "QA": 2, "QAM": 4}.get(kind, NW))
                for what, *numbers in PLANS[kind]:
                    at, *part = numbers or (0,)
                    if what == "x1T":
                        if at == 0:
                            pe.wait_ge(x1_in, 16 * (q + 1))
                        turn(x1[:, at, :], C, what, at)
                    elif what == "xq":
                        if at == 0:
                            tr_out("x1T", T - 2)
                            tr_out("x1T", T - 1)
                        out = mm_bank(what, at)
                        for c in range(C):
                            last = product(pe, out[:], [h[:, c, at * P:(at + 1) * P] for h in wq],
                                           [h[:, c, :] for h in x1T], c == 0, c == C - 1)
                        last.then_inc(mm_full, 1)
                    elif what == "scores":
                        t, half = divmod(at, 2)
                        if at == 0:
                            pe.wait_ge(keys_in, 32 * (a + 1))
                        if at < 2:
                            q_ready(a, at)
                        pe.wait_ge(s_out, a * NH + at)
                        for r in range(4):
                            rows = slice(32 * r, 32 * r + 1)
                            pe.matmul(scores[:, r, 0:2 * CTX], ones[rows, :], mask_row[rows, :],
                                      start=True, stop=False, skip_group_check=True)
                        for c2 in range(2):
                            c = 2 * half + c2
                            for r in range(4):
                                rows = slice(32 * r, 32 * r + 32)
                                last = pe.matmul(scores[:, r, c2 * CTX:(c2 + 1) * CTX],
                                                 qT[rows, c, t * P:(t + 1) * P], kT[rows, c, :],
                                                 start=False, stop=True, skip_group_check=True)
                        last.then_inc(s_full, 1)
                    elif what == "pT":
                        k = part[0]
                        if k == 0:
                            pe.wait_ge(exp_done, a * (2 * NH) + (2 * at + 2))
                        out = tr_bank(what, at, k)
                        src = probs[at % 2] if k < 2 else probs_end[at % 2]
                        for j in range(4 if k < 2 else 2):
                            col = (4 * k % 8 + j) * P
                            last = pe.transpose(out[:, j * P:(j + 1) * P], src[:, col:col + P], ident[:])
                        last.then_inc(tr_full, 1)
                    elif what == "pv":
                        if at == 0:
                            pe.wait_ge(values_in, 32 * (a + 1))
                        out = mm_bank(what, at)
                        half = at % 2
                        tr_out("pT", at, 1)
                        tr_out("pT", at, 2)
                        turned = pT[at % 2]
                        for four in range(2):
                            w = 4 * VB
                            at_v = (2 * half + four) * w
                            pe.matmul(out[:, four * w:(four + 1) * w], turned[:, HALF + four, :],
                                      vr[:, at_v:at_v + w], start=(four == 0), stop=False, skip_group_check=True)
                        for j in range(HALF):
                            h = half * HALF + j
                            last = pe.matmul(out[:, j * VB:(j + 1) * VB], turned[:, j, :],
                                             vm[:, h * VB:(h + 1) * VB], start=False, stop=True,
                                             skip_group_check=True)
                        last.then_inc(mm_full, 1)
                    elif what == "oT":
                        product_out(pe, kind, i, "pv", 2 * at)
                        product_out(pe, kind, i, "pv", 2 * at + 1)
                        turn(o[:], C, what, at)
                    elif what == "wo":
                        tr_out("oT", at)
                        multiply(oT, wo, C, D, what, at)
                    elif what == "x2T":
                        pe.wait_ge(x2_ready, m * T + (FROM_ONE + at + 1))
                        turn(x2[:, at, :], C, what, at)
                    elif what == "v":
                        tr_out("x2T", at)
                        multiply(x2T, wv, C, D, what, at)
                    elif what == "vT":
                        product_out(pe, kind, i, "v", at)
                        turn(val[:, at, :], C, what, at)
                    elif what == "gate":
                        tr_out("vT", at)
                        multiply(vT, wg, C, GW, what, at)
                    elif what == "hT":
                        pe.wait_ge(hid_ready, f + 1)
                        turn(hid[:, at, :], 3, what, at)
                    elif what == "w2":
                        tr_out("hT", at)
                        multiply(hT[at % 2], w2, 3, D, what, at)

            iterations(pe, body)

        @block.scalar
        def _(act):
            for w, (pair, dram, chunks) in enumerate(WEIGHTS):
                act.wait_ge(weight_in, 16 * (w + 1))
                act.activation(pair[0][:], landing(w), ACT.Copy).then_inc(weight_hi, 1)
            act.wait_ge(small_in, 80)
            act.activation(alpha[:], alpha[:], ACT.Tanh, scale=0.5).then_inc(alpha_tanh, 1)

            def body(kind, q, a, m, f, i):
                def high(out, chunks, *key):
                    k, n = use("tr", kind, i, *key)
                    act.wait_ge(tr_full, n + 1)
                    act.activation(out, trp[k][:, 0:chunks * P].rearrange("p (c n) -> p c n", c=chunks),
                                   ACT.Copy).then_inc(tr_hi, 1)

                def query(chunk):
                    k, n = use("mm", kind, i, "xq", chunk)
                    act.wait_ge(mm_full, n + 1)
                    act.activation(qT[:, chunk, :], mmp[k][:], ACT.Copy).then_inc(mm_free[k], 1)
                    product_out(act, kind, i, "xq", chunk)
                    act.sem_inc(q_out, 1)

                for what, *numbers in PLANS[kind]:
                    at, *part = numbers or (0,)
                    if what == "pT":
                        k, u = use("tr", kind, i, what, at, *part)
                        first, heads = 4 * part[0], 4 if part[0] < 2 else 2
                        act.wait_ge(tr_full, u + 1)
                        act.activation(pT[at % 2][:, first:first + heads, :],
                                       trp[k][:, 0:heads * P].rearrange("p (c n) -> p c n", c=heads), ACT.Copy) \
                           .then_inc(tr_free[k], 1)
                    elif what == "exps":
                        act.wait_ge(s_out, a * NH + at + 1)
                        for out, keys in ((probs, slice(0, P)), (probs_end, slice(P, CTX))):
                            out = out[at % 2][:].rearrange("p (j k) -> p j k", j=HALF)[:, :, 0:keys.stop - keys.start]
                            act.activation(out, shifted[:, :, keys], ACT.Exp, scale=float(DH) ** -0.5) \
                               .then_inc(exp_done, 1)
                    elif what == "oT":
                        high(oT[0][:], C, what, at)
                    elif what == "vT":
                        high(vT[0][:], C, what, at)
                    elif what == "x2T":
                        high(x2T[0][:], C, what, at)
                    elif what == "hT":
                        high(hT[at % 2][0][:], 3, what, at)
                    elif what == "x1T":
                        high(x1T[0][:, :, at * P:(at + 1) * P], C, what, at)
                    elif what == "xq":
                        query(at)
                    elif what == "tanh":
                        product_out(act, kind, i, "gate", T - 2)
                        product_out(act, kind, i, "gate", T - 1)
                        act.activation(hid[:, :, 0:E * INNER], gate[:, :, E + E * PV:GW], ACT.Tanh, scale=0.5) \
                           .then_inc(tanh_ready, 1)
                    elif what == "gate_exp":
                        act.wait_ge(s_rel_ready, f + 1)
                        act.activation(s_exp[:], s_rel[:], ACT.Exp).then_inc(s_exp_ready, 1)

            iterations(act, body)

        @block.vector
        def _(dve):
            for w, (pair, dram, chunks) in enumerate(WEIGHTS):
                dve.wait_ge(weight_hi, w + 1)
                dve.tensor_tensor(pair[1][:], landing(w), pair[0][:].bitcast(F32), ALU.subtract) \
                   .then_inc(weight_lo, 1)
            dve.wait_ge(weight_lo, NW)
            dve.wait_ge(alpha_tanh, 1)
            dve.wait_ge(constants, 11)
            dve.tensor_scalar(alpha[:], alpha[:], 1.0, 0.5, ALU.add, ALU.mult).then_inc(tables, 1)
            dve.wait_ge(tables, 1)
            for t in (gains, shifts):
                dve.tensor_scalar(t[:, 1, :], t[:, 1, :], alpha[:, 0:1], None, ALU.mult).then_inc(tables, 1)
            dve.wait_ge(tables, 3)

            def body(kind, q, a, m, f, i):
                chain_a = Chain(dve, chain_a_sem, 2 * NH + T)
                chain_m = Chain(dve, chain_m_sem, T + 7)
                chain_f = Chain(dve, chain_f_sem, 10 + 6 + T)

                def low(out, hi, chunks, what, at):
                    k, _ = use("tr", kind, i, what, at)
                    high_taken(dve, kind, i, what, at)
                    dve.tensor_tensor(out, trp[k][:, 0:chunks * P].rearrange("p (c n) -> p c n", c=chunks),
                                      hi.bitcast(F32), ALU.subtract).then_inc(tr_free[k], 1)

                def mm_ready(*key):
                    k, n = use("mm", kind, i, *key)
                    dve.wait_ge(mm_full, n + 1)
                    return k, mmp[k]

                def layernorm(out, moments, rstd):
                    return dve.tensor_scalar(out, out, moments, rstd, ALU.subtract, ALU.mult)

                def softmax_shift(n):
                    view = scores[:, :, 0:2 * CTX].rearrange("p r (c k) -> p r c k", c=2)
                    dve.wait_ge(s_full, a * NH + n + 1)
                    chain_a.link(dve.tensor_reduce(row_max[:].rearrange("p (r c) -> p r c", c=2), view, X, ALU.max), a)
                    dve.wait_ge(exp_done, a * (2 * NH) + 2 * n)
                    dve.tensor_tensor(
                        shifted[:].rearrange("p (r c) k -> p r c k", c=2), view,
                        row_max[:].rearrange("p (r c) -> p r c", c=2).unsqueeze(3).broadcast_to([P, 4, 2, CTX]),
                        ALU.subtract).then_inc(s_out, 1)

                def head_outputs(n):
                    k, bank = mm_ready("pv", n)
                    heads = bank[:, 0:HALF * VB].rearrange("p (j v) -> p j v", v=VB)
                    chain_a.link(dve.reciprocal(inv_sum[:].unsqueeze(2), heads[:, :, DH:VB]), a)
                    dve.tensor_tensor(
                        o[:, (n % 2) * 256:(n % 2 + 1) * 256].rearrange("p (c r d) -> p r c d", c=2, r=4),
                        heads[:, :, 0:DH].rearrange("p (r c) d -> p r c d", c=2),
                        inv_sum[:].rearrange("p (r c) -> p r c", c=2).unsqueeze(3).broadcast_to([P, 4, 2, DH]),
                        ALU.mult).then_inc(mm_free[k], 1)

                def add_attention(t):
                    k, bank = mm_ready("wo", t)
                    if m is not None:
                        dve.wait_ge(skip_ready, m * T + t + 1)
                    dve.wait_ge(x1_res_in[t % 2], 16 * (a * (T // 2) + (t // 2 + 1)))
                    dve.tensor_tensor(x2[:, t, :], bank[:], x1_res[t % 2][:], ALU.add).then_inc(mm_free[k], 1)
                    product_out(dve, kind, i, "wo", t)
                    chain_a.link(dve.bn_stats(stats[:], x2[:, t, :]), a)
                    dve.sem_inc(passed, 1)
                    dve.bn_aggr(mo_a[:], stats[:]).then_inc(mo_a_ready, 1)

                def finish_x2(t):
                    dve.wait_ge(rstd_a_ready, a * T + t + 1)
                    layernorm(x2[:, t, :], mo_a[:, 0:1], rstd_a[:, 0:1]).then_inc(x2_ready, 1)

                def gate_out(t):
                    k, bank = mm_ready("gate", t)
                    dve.tensor_tensor(gate[:, t, :], bank[:, 0:GW], bg[:], ALU.add).then_inc(mm_free[k], 1)
                    product_out(dve, kind, i, "gate", t)
                    pv = gate[:, t, E:E + E * PV]
                    chain_m.link(dve.tensor_tensor(square[:], pv, pv, ALU.mult), m)
                    dve.tensor_reduce(norm2[:, t, :], square[:].rearrange("p (e k) -> p e k", e=E), X, ALU.add) \
                       .then_inc(norm2_ready, 1)

                def value_out(t):
                    k, bank = mm_ready("v", t)
                    dve.tensor_tensor(val[:, t, :], bank[:], bv[:], ALU.add).then_inc(mm_free[k], 1)

                flat = both[:].rearrange("p t a e -> p (t a) e")
                flat_sq = both_sq[:].rearrange("p t a e -> p (t a) e")

                def gate_moments():
                    dve.wait_ge(norm_ready, m * T + T)
                    chain_m.link(dve.tensor_copy(both[:, :, 0, :], gate[:, :, 0:E]), m)
                    chain_m.link(dve.tensor_scalar(both[:, :, 1, :], norm[:], float(PV) ** -0.5, None, ALU.mult), m)
                    chain_m.link(dve.tensor_reduce(mean[:], flat, X, ALU.add), m)
                    chain_m.link(dve.tensor_scalar(mean[:], mean[:], 1.0 / E, None, ALU.mult), m)
                    chain_m.link(dve.tensor_tensor(flat, flat, mean[:].unsqueeze(2).broadcast_to([P, 2 * T, E]),
                                                   ALU.subtract), m)
                    chain_m.link(dve.tensor_tensor(flat_sq, flat, flat, ALU.mult), m)
                    chain_m.link(dve.tensor_reduce(spread_g[:], flat_sq, X, ALU.add), m)
                    dve.tensor_scalar(spread_g[:], spread_g[:], 1.0 / E, EPS, ALU.mult, ALU.add) \
                       .then_inc(spread_g_ready, 1)

                def gate_ranks():
                    dve.wait_ge(rstd_g_ready, f + 1)
                    over_tiles = [P, T, 2, E]
                    chain_f.link(dve.tensor_tensor(flat, flat, rstd_g[:].unsqueeze(2).broadcast_to([P, 2 * T, E]),
                                                   ALU.mult), f)
                    chain_f.link(dve.tensor_tensor(both[:], both[:], gains[:].unsqueeze(1).broadcast_to(over_tiles),
                                                   ALU.mult), f)
                    chain_f.link(dve.tensor_tensor(both[:], both[:], shifts[:].unsqueeze(1).broadcast_to(over_tiles),
                                                   ALU.add), f)
                    chain_f.link(dve.tensor_tensor(s[:], both[:, :, 0, :], both[:, :, 1, :], ALU.add), f)
                    chain_f.link(dve.tensor_reduce(s_max[:], s[:], X, ALU.max), f)
                    dve.tensor_tensor(s_rel[:], s[:], s_max[:].unsqueeze(2).broadcast_to([P, T, E]),
                                      ALU.subtract).then_inc(s_rel_ready, 1)
                    pairs = [P, T, E, E]
                    other, own = s[:].unsqueeze(2).broadcast_to(pairs), s[:].unsqueeze(3).broadcast_to(pairs)
                    chain_f.link(dve.tensor_tensor(beats[:], other, own, ALU.is_gt), f)
                    chain_f.link(dve.tensor_tensor(ties[:], other, own, ALU.is_equal), f)
                    chain_f.link(dve.tensor_tensor(ties[:], ties[:], before[:].unsqueeze(1).broadcast_to(pairs),
                                                   ALU.mult), f)
                    chain_f.link(dve.tensor_tensor(beats[:], beats[:], ties[:], ALU.add), f)
                    chain_f.link(dve.tensor_reduce(rank[:], beats[:], X, ALU.add), f)

                def weigh_hidden():
                    dve.wait_ge(s_exp_ready, f + 1)
                    dve.wait_ge(tanh_ready, f + 1)
                    w = hid[:, :, E * INNER:E * INNER + E]
                    chain_f.link(dve.scalar_tensor_tensor(rank[:], rank[:], 1.5, s_exp[:], ALU.is_lt, ALU.mult), f)
                    chain_f.link(dve.tensor_reduce(den[:], rank[:], X, ALU.add), f)
                    chain_f.link(dve.reciprocal(den[:], den[:]), f)
                    chain_f.link(dve.tensor_tensor(w, rank[:], den[:].unsqueeze(2).broadcast_to([P, T, E]),
                                                   ALU.mult), f)
                    chain_f.link(dve.tensor_scalar(half_w[:], w, 0.5, None, ALU.mult), f)
                    h = hid[:, :, 0:E * INNER]
                    chain_f.link(dve.scalar_tensor_tensor(h, h, 1.0, gate[:, :, E + E * PV:GW],
                                                          ALU.add, ALU.mult), f)
                    dve.tensor_tensor(
                        h.rearrange("p t (e j) -> p t e j", e=E), h.rearrange("p t (e j) -> p t e j", e=E),
                        half_w[:].unsqueeze(3).broadcast_to([P, T, E, INNER]), ALU.mult).then_inc(hid_ready, 1)

                def add_mixture(t):
                    k, bank = mm_ready("w2", t)
                    dve.wait_ge(skip_ready, f * T + t + 1)
                    dve.wait_ge(stored[t % 2], 16 * (f * (T // 2) + t // 2) + 16)
                    dve.tensor_tensor(y[t % 2][:], bank[:], skip[:, t, :], ALU.add).then_inc(mm_free[k], 1)
                    product_out(dve, kind, i, "w2", t)
                    chain_f.link(dve.bn_stats(stats[:], y[t % 2][:]), f)
                    dve.sem_inc(passed, 1)
                    dve.bn_aggr(mo_y[:, t % 2, :], stats[:]).then_inc(mo_y_ready, 1)

                def finish_y(t):
                    dve.wait_ge(rstd_y_ready, f * T + t + 1)
                    layernorm(y[t % 2][:], mo_y[:, t % 2, 0:1], rstd_y[:, t % 2:t % 2 + 1]).then_inc(y_ready, 1)

                for what, *numbers in PLANS[kind]:
                    at = numbers[0] if numbers else 0
                    if what == "scores":
                        softmax_shift(at)
                    elif what == "pv":
                        head_outputs(at)
                    elif what == "oT":
                        low(oT[1][:], oT[0][:], C, what, at)
                    elif what == "wo":
                        add_attention(at)
                    elif what == "x2":
                        finish_x2(at)
                    elif what == "x2T":
                        low(x2T[1][:], x2T[0][:], C, what, at)
                    elif what == "v":
                        value_out(at)
                    elif what == "vT":
                        low(vT[1][:], vT[0][:], C, what, at)
                    elif what == "gate":
                        gate_out(at)
                    elif what == "moments":
                        gate_moments()
                    elif what == "ranks":
                        gate_ranks()
                    elif what == "weigh":
                        weigh_hidden()
                    elif what == "hT":
                        low(hT[at % 2][1][:], hT[at % 2][0][:], 3, what, at)
                    elif what == "w2":
                        add_mixture(at)
                    elif what == "y":
                        finish_y(at)
                    elif what == "x1T":
                        low(x1T[1][:, :, at * P:(at + 1) * P], x1T[0][:, :, at * P:(at + 1) * P], C, what, at)
                if a is not None:
                    assert chain_a.n == chain_a.per_pass, chain_a.n
                if m is not None:
                    assert chain_m.n == chain_m.per_pass, chain_m.n
                if f is not None:
                    assert chain_f.n == chain_f.per_pass, chain_f.n

            dve.sem_inc(x2_ready, FROM_ONE)
            iterations(dve, body)


def build(nc, a):
    def scratch(name, shape, dt=F32):
        return nc.dram_tensor(name, shape, dt, kind="Internal").ap()

    kT = scratch("ctx_kT", [B, P, C * CTX])
    vm = scratch("ctx_vm", [B, P, HEADS * VB])
    vr = scratch("ctx_vr", [B, P, 4 * 4 * VB])
    mask = scratch("ctx_mask", [B, 2 * CTX], BF16)
    x1 = scratch("x1", [B * NT, P, D])
    context_part(nc, a["ctxT"], a["xattn_wkT"], a["xattn_wvT"], a["mask"], kT, vm, vr, mask)
    attention_part(nc, a["x_rows"], a["xT_tiles"], a["attn_wqk"], a["attn_wvT"], a["slope"], x1)
    post_part(nc, x1, kT, vm, vr, mask, a["xattn_wqT"], a["xattn_woT"], a["ffn_wvT"], a["ffn_bv"], a["gate_wT"],
              a["gate_b"], a["w2T"], a["alpha"], a["gains"], a["shifts"], a["out"])


def kernel(**inputs):
    import numpy as np
    import concourse.bacc as bacc
    from concourse.bass_utils import run_bass_kernel_spmd

    g = {k: np.asarray(v) for k, v in inputs.items()}
    f = {k[len("L0_ffn_"):]: v for k, v in g.items() if k.startswith("L0_ffn_")}
    x = g["x"].reshape(B * NT, P, D)
    experts = E * INNER
    arrays = {
        "x_rows": x,
        "xT_tiles": x.reshape(B * NT, P, C, P).transpose(0, 3, 2, 1).reshape(B * NT, P, D),
        "ctxT": g["ctx_1024"].reshape(B * CTX, D).T,
        "mask": g["mask_Bx1x1xS2_ik0"].reshape(B, CTX),
        "attn_wqk": g["L0_attn_W_qk"],
        "attn_wvT": g["L0_attn_W_v"].T,
        "slope": g["L0_attn_alibi_slope"].reshape(1, 1),
        "xattn_wkT": g["L0_xattn_Wk"].T,
        "xattn_wvT": g["L0_xattn_Wv"].T,
        "xattn_wqT": g["L0_xattn_Wq"].T,
        "xattn_woT": g["L0_xattn_Wo"].T,
        "ffn_wvT": f["Wv"].T,
        "ffn_bv": f["bv"].reshape(1, D),
        "gate_wT": np.concatenate([f["Wg"], f["Wp"].reshape(E * PV, D), f["W1"].reshape(experts, D)]).T,
        "gate_b": np.concatenate([f["bg"], np.zeros(E * PV, np.float32), f["b1"].reshape(experts)]).reshape(1, GW),
        "w2T": np.concatenate([f["W2"].transpose(0, 2, 1).reshape(experts, D), f["b2"],
                               np.zeros((HP - experts - E, D), np.float32)]),
        "alpha": f["alpha"].reshape(1, 1),
        "gains": np.concatenate([f["g_r"], f["g_c"]]).reshape(1, 2 * E),
        "shifts": np.concatenate([f["b_r"], f["b_c"]]).reshape(1, 2 * E),
    }
    arrays = {k: np.ascontiguousarray(v) for k, v in arrays.items()}
    nc = bacc.Bacc("TRN2", target_bir_lowering=False, num_devices=1)
    aps = {k: nc.dram_tensor(k + "_in", v.shape, mybir.dt.from_np(v.dtype), kind="ExternalInput").ap()
           for k, v in arrays.items()}
    aps["out"] = nc.dram_tensor("result", [B * NT, P, D], F32, kind="ExternalOutput").ap()
    build(nc, aps)
    r = run_bass_kernel_spmd(nc, [{k + "_in": v for k, v in arrays.items()}], core_ids=[0])
    return r.results[0]["result"].reshape(B, S, D)
```

```python
from contextlib import ExitStack

import concourse.bass as bass
from concourse import mybir

P = 128
B, S, D = 4, 2048, 512
C = D // P
NT = S // P
CTX = 154
CREM = CTX - P
HEADS, DH = 16, 32
E, INNER, PV = 8, 32, 8
EPS = 1e-5
GW = E + E * PV + E * INNER
HP = 3 * P
VB = DH + 1
HALF = 8
NEG = -1.0e20
FROM_ONE = 1
CUT = -3.0e38

F32 = mybir.dt.float32
F32R = mybir.dt.float32r
I32 = mybir.dt.int32
ALU = mybir.AluOpType
ACT = mybir.ActivationFunctionType
X = mybir.AxisListType.X


def product(pe, out, left, right, start, stop, skip=False):
    (lh, ll), (rh, rl) = left, right
    pe.matmul(out, ll, rh, start=start, stop=False, skip_group_check=skip)
    pe.matmul(out, lh, rl, start=False, stop=False, skip_group_check=skip)
    return pe.matmul(out, lh, rh, start=False, stop=stop, skip_group_check=skip)


class Chain:

    def __init__(self, engine, sem, per_pass, before=0):
        self.engine, self.sem, self.per_pass, self.n, self.before = engine, sem, per_pass, 0, before

    def link(self, ins, passes=0):
        self.n += 1
        ins.then_inc(self.sem, 1)
        self.engine.wait_ge(self.sem, passes * self.per_pass + self.before + self.n)


class Weight:

    def __init__(self, nc, scope, name, dram):
        rows, n = dram.shape
        self.chunks, self.dram = rows // P, dram
        shape = [P, self.chunks, n]
        self.high = scope.enter_context(nc.sbuf_tensor(f"post_{name}_hi", shape, F32R))
        with ExitStack() as first:
            self.whole = first.enter_context(nc.sbuf_tensor(f"post_{name}", shape, F32))
        self.low = scope.enter_context(nc.sbuf_tensor(f"post_{name}_lo", shape, F32R))
        self.pair = self.high, self.low
        self.loaded = scope.enter_context(nc.semaphore(f"{name}_loaded"))
        self.high_taken = scope.enter_context(nc.semaphore(f"{name}_high_taken"))
        self.low_taken = scope.enter_context(nc.semaphore(f"{name}_low_taken"))

    def load(self, engine):
        engine.dma_start(self.whole[:], self.dram.rearrange("(c p) n -> p c n", p=P)).then_inc(self.loaded, 16)

    def take_high(self, act, c):
        act.wait_ge(self.loaded, 16)
        act.activation(self.high[:, c, :], self.whole[:, c, :], ACT.Copy).then_inc(self.high_taken, 1)

    def take_low(self, dve, c):
        dve.wait_ge(self.high_taken, c + 1)
        dve.tensor_tensor(self.low[:, c, :], self.whole[:, c, :], self.high[:, c, :].bitcast(F32),
                          ALU.subtract).then_inc(self.low_taken, 1)

    def wait_split(self, pe):
        pe.wait_ge(self.low_taken, self.chunks)


def attention_part(nc, xT, rest, ident, ready, ctx, x_rows, xT_tiles, wqk_d, wvT_d, slope_d, x1_d):
    NCH = [(i + 4) // 4 for i in range(NT)]
    CUM = [sum(NCH[:i]) for i in range(NT + 1)]
    ROWS = CUM[NT]

    def step(name, *at, ahead=False):
        return (name, ahead, *at)

    def weighted(i, between):
        n = NCH[i]
        steps = [step("pT", i, 0)] + between[0]
        for k in range(n):
            steps += [step("pT", i, k + 1)] * (k + 1 < n) + [step("pv", i, k)]
            steps += [step("out", i)] * (k == n - 1)
            steps += between[1] if k == 0 else between[2] if k == n - 2 else []
        return steps + between[3]

    LEAD = 3
    PAIRS = (NT - 2) // 2

    def loop_steps(more):
        steps = []
        for i in range(NT):
            steps += [step("scores", i, k) for k in range(NCH[i])]
            steps += [step("x1", i - 2)] * (i > 1)
            splits = [step("xT", j) for j in (2 * i + LEAD, 2 * i + LEAD + 1) if j < NT]
            vs = [[step("v", 2 * i + 1)], [step("v", 2 * i + 2)]] if i < PAIRS else [[], []]
            if i == 0:
                steps += [step("exps", 0), *splits, step("q", 1), *vs[0], step("qT", 1), *vs[1]]
            elif i < NT - 1:
                turned = [*vs[0], step("qT", i + 1)]
                steps += weighted(i - 1, ([step("exps", i), *splits, step("q", i + 1)], turned, [], vs[1]))
            else:
                ahead = [[step("xT", j, ahead=True)] if more else [] for j in range(LEAD)]
                steps += weighted(i - 1, ([step("exps", i), step("v", i), *ahead[0]], ahead[1], ahead[2], []))
        if more:
            between = [[step(name, 0, ahead=True)] for name in ("q", "qT", "v")] + [[]]
        else:
            between = [[], [step("w", 0)], [step("w", 1)], [step("w", 2), step("w", 3)]]
        between[1].insert(0, step("x1", NT - 2))
        between[3].insert(0, step("x1", NT - 1))
        return steps + weighted(NT - 1, between)

    KINDS = {"first": 1, "loop": B - 1, "last": 1}
    PLANS = {"first": [step("xT", j) for j in range(LEAD)] + [step("q", 0), step("v", 0), step("qT", 0)],
             "loop": loop_steps(True), "last": loop_steps(False)}
    uses = {"tr": {kind: [s for s in plan if s[0] in ("qT", "pT")] for kind, plan in PLANS.items()},
            "mm": {kind: [s for s in plan if s[0] in ("q", "v") or (s[0] == "pv" and s[-1] == 0)]
                   for kind, plan in PLANS.items()}}

    def position(ring, kind, i, key, per=1):
        before = sum(KINDS[other] * len(uses[ring][other]) for other in list(KINDS)[:list(KINDS).index(kind)])
        count = len(uses[ring][kind])
        n = before + uses[ring][kind].index(key)
        if KINDS[kind] == 1:
            return n // per
        assert count % 2 == 0
        return i * (count // per) + n // per

    def bank_of(ring, kind, key):
        return position(ring, kind, 0, key) % 2

    with ExitStack() as scope:
        def sb(name, shape, dt=F32):
            return scope.enter_context(nc.sbuf_tensor("attn_" + name, shape, dt))

        def sem(name):
            return scope.enter_context(nc.semaphore(name))

        def split(name, shape):
            return sb(name + "_hi", shape, F32R), sb(name + "_lo", shape, F32R)

        sb("rest_of_xT", [P, rest])
        NB = B * CTX
        with ExitStack() as early:
            def early_sb(name, shape, dt=F32):
                return early.enter_context(nc.sbuf_tensor("ctx_" + name, shape, dt))

            ctx_sb = early_sb("ctx", [P, C, NB])
            ctx_wk = early_sb("wk", [P, C, D])
            ctx_wv = early_sb("wv", [P, C, D])
            ctx_kT = early_sb("kT_all", [P, B, C, CTX])
            ctx_vm = early_sb("vm_all", [P, B, HEADS * VB])
            ctx_vr = early_sb("vr_all", [P, B, 4, 4 * VB])
            mask_in = early_sb("mask_in", [1, B, CTX], I32)
            mask_row = early_sb("mask_row", [1, B, CTX])
        v = split("v", [P, NT, D])
        wqk = split("wqk", [P, C, D])
        wv = split("wv", [P, C, D])
        bias = sb("alibi", [P, S])
        probs = [sb(f"probs{i}", [P, S]) for i in range(2)]
        pT = [split(f"pT{i}", [P, 512]) for i in range(2)]
        qT = split("qT", [P, C, P])
        q_row = sb("q_row", [P, D])
        x_in = [sb(f"x_in{i}", [P, D]) for i in range(2)]
        res = [sb(f"res{i}", [P, D]) for i in range(2)]
        slope = sb("slope", [P, 1])
        chunk_max = sb("chunk_max", [P, 4])
        neg_max = sb("neg_max", [P, 2])
        row_sum = sb("row_sum", [P, 2])
        inv_sum = sb("inv_sum", [P, 1])
        stats = sb("stats", [P, 6])
        moments = sb("moments", [P, 2])
        spread = sb("spread", [P, 1])
        rstd = sb("rstd", [P, 1])
        minus_half = sb("minus_half", [P, 1])
        eps = sb("eps", [P, 1])
        unused = sb("unused", [P, 2])
        scores = [scope.enter_context(nc.psum_tensor(f"scores{i}", [P, 512], F32)) for i in range(4)]
        trp = [scope.enter_context(nc.psum_tensor(f"a_trp{i}", [P, 512], F32)) for i in range(2)]
        mmp = [scope.enter_context(nc.psum_tensor(f"a_mmp{i}", [P, 512], F32)) for i in range(2)]

        bank = scores + trp + mmp
        c_loaded = sem("c_loaded")
        c_wv_loaded = sem("c_wv_loaded")
        c_preset = sem("c_preset")
        c_k_full = sem("c_k_full")
        c_v_full = sem("c_v_full")
        c_k_kept = sem("c_k_kept")
        c_v_kept = sem("c_v_kept")
        c_mask_loaded = sem("c_mask_loaded")
        c_mask_made = sem("c_mask_made")
        c_stored = sem("c_stored")
        weight_in = sem("a_weight_in")
        weight_hi = sem("a_weight_hi")
        weight_lo = sem("a_weight_lo")
        slope_in = sem("a_slope_in")
        constants = sem("a_constants")
        x_in_full = [sem(f"a_x_in_full{i}") for i in range(2)]
        xT_hi = sem("a_xT_hi")
        xT_lo = sem("a_xT_lo")
        res_full = [sem(f"a_res_full{i}") for i in range(2)]
        stored = [sem(f"a_stored{i}") for i in range(2)]
        tr_full = sem("a_tr_full")
        tr_hi = sem("a_tr_hi")
        tr_free = [sem(f"a_tr_free{i}") for i in range(2)]
        v_full = sem("a_v_full")
        q_full = sem("a_q_full")
        v_hi = sem("a_v_hi")
        mm_free = [sem(f"a_mm_free{i}") for i in range(2)]
        s_full = sem("a_s_full")
        s_free = sem("a_s_free")
        max_ready = sem("a_max_ready")
        exp_done = sem("a_exp_done")
        pv_done = sem("a_pv_done")
        moments_ready = sem("a_moments_ready")
        spread_ready = sem("a_spread_ready")
        rstd_ready = sem("a_rstd_ready")
        x1_ready = sem("a_x1_ready")
        chain_sem = sem("a_chain")
        passed = sem("a_passed")
        block = scope.enter_context(nc.Block())

        def iterations(engine, body):
            body("first", 0, 0)
            with engine.Fori(0, B - 1) as i:
                body("loop", i, i)
            body("last", B - 1, 0)

        def taken(engine, ring, kind, i, key):
            k = bank_of(ring, kind, key)
            engine.wait_ge((tr_free if ring == "tr" else mm_free)[k], position(ring, kind, i, key, 2) + FROM_ONE)
            return (trp if ring == "tr" else mmp)[k]

        def out_of_bank(engine, ring, kind, i, key):
            k = bank_of(ring, kind, key)
            engine.wait_ge((tr_free if ring == "tr" else mm_free)[k], position(ring, kind, i, key, 2) + (FROM_ONE + 1))

        stage = [probs[i][:].rearrange("p (c n) -> p c n", c=C) for i in range(2)]

        @block.sync
        def _(sp):
            sp.dma_start(ctx_sb[:], ctx["ctxT"].rearrange("(c p) n -> p c n", p=P)).then_inc(c_loaded, 16)
            sp.dma_start(ctx_wk[:], ctx["wkT"].rearrange("(c p) n -> p c n", p=P)).then_inc(c_loaded, 16)
            sp.dma_start(ctx_wv[:], ctx["wvT"].rearrange("(c p) n -> p c n", p=P)).then_inc(c_wv_loaded, 16)
            sp.dma_start(mask_in[:], ctx["mask"].rearrange("(a b) n -> a b n", a=1)).then_inc(c_mask_loaded, 16)
            sp.dma_start(stage[0], wqk_d.rearrange("(c p) n -> p c n", p=P)).then_inc(weight_in, 16)
            sp.wait_ge(weight_in, 16)
            sp.dma_start(stage[1], wvT_d.rearrange("(c p) n -> p c n", p=P)).then_inc(weight_in, 16)
            sp.dma_start(slope[:], slope_d.broadcast_to([P, 1])).then_inc(slope_in, 16)
            with sp.Fori(0, B) as b:
                for j in range(NT):
                    sp.wait_ge(xT_lo, b * NT + (FROM_ONE + max(j - 1, 0)))
                    sp.dma_start(x_in[j % 2][:], xT_tiles[bass.ds(b * NT + j, 1)].rearrange("a p n -> p (a n)")) \
                      .then_inc(x_in_full[j % 2], 16)
            sp.wait_ge(s_full, B * ROWS + FROM_ONE)
            sp.wait_ge(v_full, B * NT)
            for weight in ready:
                weight.load(sp)

        @block.gpsimd
        def _(pool):
            pool.memset(ctx_vm[:], 1.0).then_inc(c_preset, 1)
            pool.memset(ctx_vr[:], 0.0).then_inc(c_preset, 1)
            pool.wait_ge(c_preset, 2)
            for j in range(4):
                pool.memset(ctx_vr[32 * j:32 * j + CREM, :, :, j * VB + DH:(j + 1) * VB], 1.0).then_inc(c_preset, 1)
            pool.wait_ge(c_preset, 6)
            pool.memset(ident[:], 0.0).then_inc(constants, 1)
            pool.wait_ge(constants, 1)
            pool.affine_select(out=ident[:], in_=ident[:], compare_op=ALU.not_equal, fill=1.0, base=0,
                               pattern=[[-1, P]], channel_multiplier=1).then_inc(constants, 1)
            pool.iota(bias[:], pattern=[[1, S]], base=-(S - P), channel_multiplier=-1,
                      allow_small_or_imprecise_dtypes=True).then_inc(constants, 1)
            pool.wait_ge(slope_in, 16)
            pool.wait_ge(constants, 3)
            pool.tensor_scalar(bias[:], bias[:], slope[:, 0:1], None, ALU.mult).then_inc(constants, 1)
            pool.wait_ge(constants, 4)
            pool.affine_select(out=bias[:], in_=bias[:], compare_op=ALU.is_ge, fill=CUT, base=S - P,
                               pattern=[[-1, S]], channel_multiplier=1).then_inc(constants, 1)
            pool.memset(minus_half[:], -0.5).then_inc(constants, 1)
            pool.memset(eps[:], EPS).then_inc(constants, 1)
            pool.wait_ge(constants, 7)
            pool.wait_ge(c_mask_made, 1)
            pool.dma_start(ctx["mask_d"].rearrange("(a b) n -> a b n", a=1), mask_row[:]).then_inc(c_stored, 16)
            pool.wait_ge(c_k_kept, 8)
            pool.dma_start(ctx["kT_d"].rearrange("b p n -> p b n"), ctx_kT[:].rearrange("p b c n -> p b (c n)")) \
                .then_inc(c_stored, 16)
            pool.wait_ge(c_v_kept, B)
            pool.wait_ge(c_preset, 6)
            pool.dma_start(ctx["vm_d"].rearrange("b p n -> p b n"), ctx_vm[:]).then_inc(c_stored, 16)
            pool.dma_start(ctx["vr_d"].rearrange("b p n -> p b n"), ctx_vr[:].rearrange("p b q n -> p b (q n)")) \
                .then_inc(c_stored, 16)
            for k, free in enumerate(stored):
                pool.dma_start(unused[:, k:k + 1], slope_d.broadcast_to([P, 1])).then_inc(free, 16)
            with pool.Fori(0, B) as b:
                for i in range(NT + 1):
                    if i < NT:
                        pool.wait_ge(stored[i % 2], 16 * (b * (NT // 2) + i // 2) + 16)
                        pool.sem_inc(passed, 1)
                        pool.dma_start(res[i % 2][:], x_rows[bass.ds(b * NT + i, 1)].rearrange("a p n -> p (a n)")) \
                            .then_inc(res_full[i % 2], 16)
                    if i > 0:
                        pool.wait_ge(moments_ready, b * NT + i)
                        pool.tensor_tensor(spread[:], moments[:, 1:2], eps[:], ALU.add).then_inc(spread_ready, 1)
                        pool.wait_ge(spread_ready, b * NT + i)
                        pool.tensor_tensor(rstd[:], spread[:], minus_half[:], ALU.pow).then_inc(rstd_ready, 1)
                        pool.wait_ge(x1_ready, b * NT + i)
                        pool.sem_inc(passed, 1)
                        pool.dma_start(x1_d[bass.ds(b * NT + i - 1, 1)].rearrange("a p n -> p (a n)"),
                                       res[(i - 1) % 2][:]).then_inc(stored[(i - 1) % 2], 16)
            pool.wait_ge(c_stored, 64)
            for k in range(2):
                pool.wait_ge(stored[k], 16 * B * NT // 2 + 16)

        @block.tensor
        def _(pe):
            pe.wait_ge(c_loaded, 32)
            for c in range(C):
                for pair in range(2):
                    for e in range(C):
                        mm = pe.matmul(bank[2 * c + pair][:, 0:2 * CTX], ctx_wk[:, e, c * P:(c + 1) * P],
                                       ctx_sb[:, e, pair * 2 * CTX:(pair + 1) * 2 * CTX],
                                       start=(e == 0), stop=(e == C - 1))
                    mm.then_inc(c_k_full, 1)
            pe.wait_ge(c_wv_loaded, 16)
            for b in range(B):
                for part, at, n in ((0, b * CTX, P), (1, b * CTX + P, CREM)):
                    pe.wait_ge(c_k_kept, b + 4 * part + 1)
                    for e in range(C):
                        mm = pe.matmul(bank[b + 4 * part][0:n, :], ctx_sb[:, e, at:at + n], ctx_wv[:, e, :],
                                       start=(e == 0), stop=(e == C - 1))
                mm.then_inc(c_v_full, 1)
            pe.wait_ge(weight_lo, 1)
            pe.wait_ge(constants, 2)
            for free in (s_full, pv_done):
                pe.sem_inc(free, FROM_ONE)

            def body(kind, batch, n):
                for key in PLANS[kind]:
                    what, ahead, i, *part = key
                    b = batch + 1 if ahead else batch
                    k = part[0] if part else 0
                    if what == "q":
                        pe.wait_ge(xT_lo, b * NT + (FROM_ONE + i + 1))
                        out = taken(pe, "mm", kind, n, key)
                        for c in range(C):
                            last = product(pe, out[:], [t[:, c, i * P:(i + 1) * P] for t in xT],
                                           [t[:, c, :] for t in wqk], c == 0, c == C - 1)
                        last.then_inc(q_full, 1)
                    elif what == "qT":
                        out_of_bank(pe, "mm", kind, n, ("q", ahead, i))
                        out = taken(pe, "tr", kind, n, key)
                        for c in range(C):
                            last = pe.transpose(out[:, c * P:(c + 1) * P], q_row[:, c * P:(c + 1) * P], ident[:])
                        last.then_inc(tr_full, 1)
                    elif what == "scores":
                        if k == 0 and i > 0:
                            out_of_bank(pe, "tr", kind, n, ("qT", False, i))
                        earlier = CUM[i - 1] + k + 1 if i > 0 and k < NCH[i - 1] else 0
                        pe.wait_ge(s_free, b * ROWS + (FROM_ONE + earlier))
                        w = min(512, (i + 1) * P - k * 512)
                        for c in range(C):
                            last = product(pe, scores[k][:, 0:w], [t[:, c, :] for t in qT],
                                           [t[:, c, k * 512:k * 512 + w] for t in xT], c == 0, c == C - 1)
                        last.then_inc(s_full, 1)
                    elif what == "pT":
                        pe.wait_ge(exp_done, b * NT + i + 1)
                        out = taken(pe, "tr", kind, n, key)
                        for t in range(min(4, i + 1 - 4 * k)):
                            at = (4 * k + t) * P
                            last = pe.transpose(out[:, t * P:(t + 1) * P], probs[i % 2][:, at:at + P], ident[:])
                        last.then_inc(tr_full, 1)
                    elif what == "pv":
                        if k == 0:
                            out_pv = taken(pe, "mm", kind, n, key)
                            if i > 0:
                                out_of_bank(pe, "mm", kind, n, ("v", False, i))
                        out_of_bank(pe, "tr", kind, n, ("pT", False, i, k))
                        for t in range(min(4, i + 1 - 4 * k)):
                            last = product(pe, out_pv[:], [h[:, t * P:(t + 1) * P] for h in pT[(CUM[i] + k) % 2]],
                                           [h[:, 4 * k + t, :] for h in v], 4 * k + t == 0, 4 * k + t == i)
                        last.then_inc(pv_done, 1)
                    elif what == "v":
                        if kind == "first":
                            pe.wait_ge(weight_lo, 2)
                        pe.wait_ge(xT_lo, b * NT + (FROM_ONE + i + 1))
                        out = taken(pe, "mm", kind, n, key)
                        for c in range(C):
                            last = product(pe, out[:], [t[:, c, i * P:(i + 1) * P] for t in xT],
                                           [t[:, c, :] for t in wv], c == 0, c == C - 1)
                        last.then_inc(v_full, 1)
                if kind != "last":
                    out_of_bank(pe, "tr", kind, n, ("qT", kind == "loop", 0))
                    out_of_bank(pe, "mm", kind, n, ("v", kind == "loop", 0))

            iterations(pe, body)

        @block.scalar
        def _(act):
            for c in range(C):
                for pair in range(2):
                    act.wait_ge(c_k_full, 2 * c + pair + 1)
                    act.activation(ctx_kT[:, 2 * pair:2 * pair + 2, c, :],
                                   bank[2 * c + pair][:, 0:2 * CTX].rearrange("p (b n) -> p b n", b=2),
                                   ACT.Copy).then_inc(c_k_kept, 1)
            for w, pair in enumerate((wqk, wv)):
                act.wait_ge(weight_in, 16 * (w + 1))
                act.activation(pair[0][:], stage[w], ACT.Copy).then_inc(weight_hi, 1)

            def body(kind, batch, n):
                for key in PLANS[kind]:
                    what, ahead, i, *part = key
                    b = batch + 1 if ahead else batch
                    if what == "xT":
                        act.wait_ge(x_in_full[i % 2], 16 * (b * (NT // 2) + i // 2 + 1))
                        act.wait_ge(s_full, b * ROWS + FROM_ONE)
                        act.activation(xT[0][:, :, i * P:(i + 1) * P], x_in[i % 2][:].rearrange("p (c n) -> p c n", c=C),
                                       ACT.Copy).then_inc(xT_hi, 1)
                    elif what == "v":
                        if kind == "first":
                            act.wait_ge(c_stored, 64)
                        act.wait_ge(v_full, b * NT + i + 1)
                        act.activation(v[0][:, i, :], mmp[bank_of("mm", kind, key)][:], ACT.Copy).then_inc(v_hi, 1)
                    elif what == "q":
                        act.wait_ge(q_full, b * NT + i + 1)
                        k = bank_of("mm", kind, key)
                        act.activation(q_row[:], mmp[k][:], ACT.Copy, scale=float(D) ** -0.5).then_inc(mm_free[k], 1)
                    elif what == "qT":
                        act.wait_ge(tr_full, position("tr", kind, n, key) + 1)
                        act.activation(qT[0][:], trp[bank_of("tr", kind, key)][:].rearrange("p (c n) -> p c n", c=C),
                                       ACT.Copy).then_inc(tr_hi, 1)
                    elif what == "pT":
                        k = part[0]
                        m = CUM[i] + k
                        act.wait_ge(pv_done, b * ROWS + (FROM_ONE + max(m - 1, 0)))
                        act.wait_ge(tr_full, position("tr", kind, n, key) + 1)
                        w = min(512, (i + 1) * P - k * 512)
                        act.activation(pT[m % 2][0][:, 0:w], trp[bank_of("tr", kind, key)][:, 0:w], ACT.Copy) \
                           .then_inc(tr_hi, 1)
                    elif what == "w":
                        ready[0].take_high(act, i)
                    elif what == "exps":
                        act.wait_ge(max_ready, b * NT + i + 1)
                        act.activation(probs[i % 2][:, 0:(i + 1) * P], probs[i % 2][:, 0:(i + 1) * P], ACT.Exp,
                                       bias=neg_max[:, i % 2:i % 2 + 1],
                                       accum_out=row_sum[:, i % 2:i % 2 + 1]).then_inc(exp_done, 1)

            iterations(act, body)

        @block.vector
        def _(dve):
            dve.sem_inc(xT_lo, FROM_ONE)
            for w, pair in enumerate((wqk, wv)):
                dve.wait_ge(weight_hi, w + 1)
                dve.tensor_tensor(pair[1][:], stage[w], pair[0][:].bitcast(F32), ALU.subtract).then_inc(weight_lo, 1)
            dve.wait_ge(weight_lo, 2)
            dve.wait_ge(c_mask_loaded, 16)
            dve.tensor_scalar(mask_row[:], mask_in[:], 0, NEG, ALU.is_equal, ALU.mult).then_inc(c_mask_made, 1)
            dve.wait_ge(c_preset, 6)
            for b in range(B):
                dve.wait_ge(c_v_full, b + 1)
                for half in range(2):
                    dve.tensor_copy(
                        ctx_vm[:, b, half * HALF * VB:(half + 1) * HALF * VB].rearrange(
                            "p (r c v) -> p r c v", r=4, c=2)[:, :, :, 0:DH],
                        bank[b][:, half * 256:(half + 1) * 256].rearrange("p (c r d) -> p r c d", c=2, r=4))
                for j in range(4):
                    h0 = 4 * (j % 2) + j // 2
                    src = bank[4 + b][0:CREM, :].rearrange("p (a x) -> p a x", a=2)
                    for q in range(2):
                        last = dve.tensor_copy(
                            ctx_vr[32 * j:32 * j + CREM, b, :, j * VB:j * VB + DH].rearrange(
                                "p (a q) d -> p a q d", q=2)[:, :, q, :],
                            src[:, :, (h0 + 2 * q) * DH:(h0 + 2 * q + 1) * DH])
                last.then_inc(c_v_kept, 1)
            dve.wait_ge(c_k_kept, 8)
            dve.wait_ge(c_v_kept, B)
            for free in (*tr_free, *mm_free, s_free):
                dve.sem_inc(free, FROM_ONE)

            def body(kind, batch, n):
                chain = Chain(dve, chain_sem, NT * 2)
                if kind != "first":
                    dve.wait_ge(constants, 7)
                for key in PLANS[kind]:
                    what, ahead, i, *part = key
                    b = batch + 1 if ahead else batch
                    r = res[i % 2]
                    if what == "xT":
                        dve.wait_ge(xT_hi, b * NT + i + 1)
                        dve.tensor_tensor(xT[1][:, :, i * P:(i + 1) * P],
                                          x_in[i % 2][:].rearrange("p (c n) -> p c n", c=C),
                                          xT[0][:, :, i * P:(i + 1) * P].bitcast(F32), ALU.subtract).then_inc(xT_lo, 1)
                    elif what == "v":
                        k = bank_of("mm", kind, key)
                        dve.wait_ge(v_hi, b * NT + i + 1)
                        dve.tensor_tensor(v[1][:, i, :], mmp[k][:], v[0][:, i, :].bitcast(F32), ALU.subtract) \
                           .then_inc(mm_free[k], 1)
                    elif what == "qT":
                        k = bank_of("tr", kind, key)
                        dve.wait_ge(tr_hi, position("tr", kind, n, key) + 1)
                        dve.tensor_tensor(qT[1][:], trp[k][:].rearrange("p (c n) -> p c n", c=C),
                                          qT[0][:].bitcast(F32), ALU.subtract).then_inc(tr_free[k], 1)
                    elif what == "pT":
                        k = bank_of("tr", kind, key)
                        pT_hi, pT_lo = pT[(CUM[i] + part[0]) % 2]
                        w = min(512, (i + 1) * P - part[0] * 512)
                        dve.wait_ge(tr_hi, position("tr", kind, n, key) + 1)
                        dve.tensor_tensor(pT_lo[:, 0:w], trp[k][:, 0:w], pT_hi[:, 0:w].bitcast(F32),
                                          ALU.subtract).then_inc(tr_free[k], 1)
                    elif what == "scores":
                        k = part[0]
                        w = min(512, (i + 1) * P - k * 512)
                        at = S - (i + 1) * P + k * 512
                        dve.wait_ge(s_full, b * ROWS + (FROM_ONE + CUM[i] + k + 1))
                        dve.sem_inc(passed, 1)
                        dve.tensor_tensor_reduce(probs[i % 2][:, k * 512:k * 512 + w], scores[k][:, 0:w],
                                                 bias[:, at:at + w], 1.0, CUT, ALU.add, ALU.max,
                                                 chunk_max[:, k:k + 1]).then_inc(s_free, 1)
                        if k == NCH[i] - 1:
                            dve.wait_ge(s_free, b * ROWS + (FROM_ONE + CUM[i + 1]))
                            dve.tensor_reduce(neg_max[:, i % 2:i % 2 + 1], chunk_max[:, 0:NCH[i]], X, ALU.max,
                                              negate=True).then_inc(max_ready, 1)
                    elif what == "out":
                        k = bank_of("mm", kind, ("pv", False, i, 0))
                        chain.link(dve.reciprocal(inv_sum[:], row_sum[:, i % 2:i % 2 + 1]), b)
                        dve.wait_ge(res_full[i % 2], 16 * (b * (NT // 2) + i // 2 + 1))
                        dve.wait_ge(pv_done, b * ROWS + (FROM_ONE + CUM[i + 1]))
                        dve.scalar_tensor_tensor(r[:], mmp[k][:], inv_sum[:, 0:1], r[:],
                                                 ALU.mult, ALU.add).then_inc(mm_free[k], 1)
                        out_of_bank(dve, "mm", kind, n, ("pv", False, i, 0))
                        chain.link(dve.bn_stats(stats[:], r[:]), b)
                        dve.sem_inc(passed, 1)
                        dve.bn_aggr(moments[:], stats[:]).then_inc(moments_ready, 1)
                    elif what == "w":
                        ready[0].take_low(dve, i)
                    elif what == "x1":
                        dve.wait_ge(rstd_ready, b * NT + i + 1)
                        dve.tensor_scalar(r[:], r[:], moments[:, 0:1], rstd[:, 0:1],
                                          ALU.subtract, ALU.mult).then_inc(x1_ready, 1)
                assert chain.n in (0, chain.per_pass)

            iterations(dve, body)


def post_part(nc, ident, ready, wg_d, x1_d, kT_d, vm_d, vr_d, mask_d, bv_d, bg_d, alpha_d, gain_d, shift_d, out_d):
    T = 4
    G = B * NT // T
    NH = 2 * T
    EXPS = HALF + 1
    KINDS = {"Q": 1, "QAW": 1, "QAM": 1, "QAMF": G - 3, "AMF": 1, "MF": 1, "F": 1}
    SCHEDULE = """
        scores.0 xq.2 x2T.0 exps.0 xq.3 ranks v.0 gate_exp x2T.1 split.0
        scores.1 pT.0.0 pT.0.1 v.1  pT.0.2 exps.1 vT.0 pv.0
        scores.2 weigh pT.1.0 pT.1.1 gate.0 pT.1.2 exps.2 vT.1 pv.1 hT.0 split.1
        scores.3 pT.2.0 pT.2.1 w2.0 pT.2.2 oT.0 skip.0 exps.3 gate.1 hT.1 y.0 x2T.2 pv.2 wo.0
        scores.4 pT.3.0 pT.3.1 w2.1 pT.3.2 hT.2 skip.1 exps.4 x2.0 v.2 y.1 x2T.3 pv.3 vT.2 split.2
        scores.5 pT.4.0 pT.4.1 w2.2 pT.4.2 oT.1 skip.2 exps.5 gate.2 hT.3 y.2 pv.4 wo.1
        scores.6 pT.5.0 pT.5.1 v.3  pT.5.2 x1T.0 exps.6 x2.1 pv.5 x1T.1 vT.3 split.3
        scores.7 pT.6.0 pT.6.1 w2.3 pT.6.2 oT.2 skip.3 exps.7 y.3 pv.6 x1T.2 wo.2
        pT.7.0 pT.7.1 gate.3 pT.7.2 x1T.3 tanh x2.2 pv.7
        xq.0 oT.3 xq.1 moments wo.3 x2.3
    """
    LAST = {
        "MF": """
            x2T.0 ranks v.0 gate_exp x2T.1 weigh vT.0 v.1 x2T.2 hT.0 gate.0 hT.1 vT.1 v.2 x2T.3
            w2.0 hT.2 skip.0 gate.1 y.0 vT.2 v.3 w2.1 hT.3 skip.1 gate.2 y.1 vT.3
            w2.2 skip.2 gate.3 y.2 moments tanh w2.3 skip.3 y.3
        """,
        "F": "ranks gate_exp weigh hT.0 hT.1 w2.0 hT.2 w2.1 y.0 hT.3 w2.2 y.1 w2.3 y.2 y.3",
    }
    STAGE = {step: stage for stage, steps in {
        "Q": "x1T xq.0 xq.1",
        "A": "xq.2 xq.3 scores exps pT pv oT wo x2",
        "M": "x2T v skip vT gate tanh moments",
        "F": "ranks gate_exp weigh hT w2 y",
        "W": "split"}.items() for step in steps.split()}

    def plan(kind):
        steps = [step for step in LAST.get(kind, SCHEDULE).split()
                 if STAGE[step if step.startswith("xq") else step.split(".")[0]] in kind]
        return [(name, *map(int, at)) for name, *at in (step.split(".") for step in steps)]

    TRANSPOSES = ("x1T", "pT", "oT", "x2T", "vT", "hT")
    SPLIT = ("x1T", "oT", "x2T", "vT", "hT")
    PRODUCTS = ("xq", "pv", "wo", "v", "gate", "w2")
    PLANS = {kind: plan(kind) for kind in KINDS}
    uses = {ring: {kind: [s for s in plan if s[0] in names] for kind, plan in PLANS.items()}
            for ring, names in (("tr", TRANSPOSES), ("mm", PRODUCTS), ("hi", SPLIT))}

    def position(ring, kind, i, key, per=1):
        n, before = uses[ring][kind].index(key), 0
        for other, times in KINDS.items():
            if other == kind:
                break
            before += times * len(uses[ring][other])
        count = len(uses[ring][kind])
        assert per == 1 or (count % per == 0 and before % per == 0)
        fixed = before // per + n // per
        return i * (count // per) + fixed if KINDS[kind] > 1 else fixed

    def use(ring, kind, i, *key):
        return uses[ring][kind].index(key) % 2, position(ring, kind, i, key)

    def bank_use(ring, kind, i, *key):
        return uses[ring][kind].index(key) % 2, position(ring, kind, i, key, 2)

    with ExitStack() as scope:
        def sb(name, shape, dt=F32):
            return scope.enter_context(nc.sbuf_tensor("post_" + name, shape, dt))

        def sem(name):
            return scope.enter_context(nc.semaphore("p_" + name))

        def split(name, shape):
            return sb(name + "_hi", shape, F32R), sb(name + "_lo", shape, F32R)

        gate_weight = Weight(nc, scope, "wg", wg_d)
        wq, wo, wv, w2 = (weight.pair for weight in ready)
        wg = gate_weight.pair
        whole = [ready[1], ready[2], gate_weight, ready[3]]
        kT = sb("kT", [P, C, CTX])
        vm = sb("vm", [P, HEADS * VB])
        vr = sb("vr", [P, 4 * 4 * VB])
        mask_row = sb("mask_row", [P, CTX])
        x1 = sb("x1", [P, T, D])
        x1_res = [sb(f"x1_res{i}", [P, D]) for i in range(2)]
        x1T = split("x1T", [P, C, T * P])
        qT = sb("qT", [P, C, T * P])
        probs = [sb(f"probs{i}", [P, HALF * CTX]) for i in range(2)]
        probs_end = [sb(f"probs_end{i}", [P, HALF * 32]) for i in range(2)]
        pT = [sb(f"pT{i}", [P, HALF + 2, P]) for i in range(2)]
        o = sb("o", [P, D])
        oT = split("oT", [P, C, P])
        x2 = sb("x2", [P, T, D])
        x2T = split("x2T", [P, C, P])
        val = sb("val", [P, T, D])
        vT = split("vT", [P, C, P])
        skip = sb("skip", [P, T, D])
        gate = sb("gate", [P, T, GW])
        hid = sb("hid", [P, T, HP])
        hT = [split(f"hT{i}", [P, 3, P]) for i in range(2)]
        y = [sb(f"y{i}", [P, D]) for i in range(2)]
        bv = sb("bv", [P, D])
        bg = sb("bg", [P, GW])
        alpha = sb("alpha", [P, 1])
        gains = sb("gains", [P, 2, E])
        shifts = sb("shifts", [P, 2, E])
        before = sb("before", [P, E, E])
        minus_half = sb("minus_half", [P, 2 * T])
        plus_half = sb("plus_half", [P, E])
        eps = sb("eps", [P, 1])
        unused = sb("unused", [P, 2])
        row_max = sb("row_max", [P, HALF])
        shift = sb("shift", [P, 2, HALF])
        inv_sum = sb("inv_sum", [P, HALF])
        stats = sb("stats", [P, 6])
        mo_a = sb("mo_a", [P, 2])
        spread_a = sb("spread_a", [P, 1])
        rstd_a = sb("rstd_a", [P, 1])
        mo_y = sb("mo_y", [P, 2, 2])
        spread_y = sb("spread_y", [P, 2])
        rstd_y = sb("rstd_y", [P, 2])
        square = sb("square", [P, E * PV])
        norm2 = sb("norm2", [P, T, E])
        norm = sb("norm", [P, T, E])
        both = sb("both", [P, T, 2, E])
        both_sq = sb("both_sq", [P, T, 2, E])
        mean = sb("mean", [P, T * 2])
        spread_g = sb("spread_g", [P, T * 2])
        rstd_g = sb("rstd_g", [P, T * 2])
        s = sb("s", [P, T, E])
        s_max = sb("s_max", [P, T])
        s_rel = sb("s_rel", [P, T, E])
        s_exp = sb("s_exp", [P, T, E])
        beats = sb("beats", [P, T, E, E])
        ties = sb("ties", [P, T, E, E])
        rank = sb("rank", [P, T, E])
        den = sb("den", [P, T])
        half_w = sb("half_w", [P, T, E])
        scores = scope.enter_context(nc.psum_tensor("p_scores", [P, 4, 512], F32))
        trp = [scope.enter_context(nc.psum_tensor(f"p_trp{i}", [P, 512], F32)) for i in range(2)]
        mmp = [scope.enter_context(nc.psum_tensor(f"p_mmp{i}", [P, 512], F32)) for i in range(2)]

        small_in = sem("small_in")
        constants = sem("constants")
        tables = sem("tables")
        alpha_tanh = sem("alpha_tanh")
        x1_in = sem("x1_in")
        x1_res_in = [sem(f"x1_res_in{i}") for i in range(2)]
        keys_in = sem("keys_in")
        values_in = sem("values_in")
        tr_full = sem("tr_full")
        tr_hi = sem("tr_hi")
        tr_free = [sem(f"tr_free{i}") for i in range(2)]
        mm_full = sem("mm_full")
        mm_free = [sem(f"mm_free{i}") for i in range(2)]
        q_out = sem("q_out")
        s_full = sem("s_full")
        s_kept = sem("s_kept")
        s_out = sem("s_out")
        exp_done = sem("exp_done")
        mo_a_ready = sem("mo_a_ready")
        spread_a_ready = sem("spread_a_ready")
        rstd_a_ready = sem("rstd_a_ready")
        x2_ready = sem("x2_ready")
        skip_ready = sem("skip_ready")
        norm2_ready = sem("norm2_ready")
        norm_ready = sem("norm_ready")
        spread_g_ready = sem("spread_g_ready")
        rstd_g_ready = sem("rstd_g_ready")
        tanh_ready = sem("tanh_ready")
        s_rel_ready = sem("s_rel_ready")
        s_exp_ready = sem("s_exp_ready")
        hid_ready = sem("hid_ready")
        mo_y_ready = sem("mo_y_ready")
        spread_y_ready = sem("spread_y_ready")
        rstd_y_ready = sem("rstd_y_ready")
        y_ready = sem("y_ready")
        stored = [sem(f"stored{i}") for i in range(2)]
        chain_a_sem = sem("chain_a")
        chain_m_sem = sem("chain_m")
        chain_f_sem = sem("chain_f")
        passed = sem("passed")
        block = scope.enter_context(nc.Block())

        def high_taken(engine, kind, i, *key):
            engine.wait_ge(tr_hi, position("hi", kind, i, key) + 1)

        def product_out(engine, kind, i, *key):
            k, n = bank_use("mm", kind, i, *key)
            engine.wait_ge(mm_free[k], n + 1)

        def iterations(engine, body):
            body("Q", 0, None, None, None, 0)
            body("QAW", 1, 0, None, None, 0)
            body("QAM", 2, 1, 0, None, 0)
            with engine.Fori(0, G - 3) as i:
                body("QAMF", i + 3, i + 2, i + 1, i, i)
            body("AMF", None, G - 1, G - 2, G - 3, 0)
            body("MF", None, None, G - 1, G - 2, 0)
            body("F", None, None, None, G - 1, 0)

        @block.sync
        def _(sp):
            def load_small():
                for t, src in ((bv, bv_d), (bg, bg_d), (alpha, alpha_d)):
                    sp.dma_start(t[:], src.broadcast_to([P, src.shape[-1]])).then_inc(small_in, 16)
                for t, src in ((gains, gain_d), (shifts, shift_d)):
                    sp.dma_start(t[:].rearrange("p a e -> p (a e)"), src.broadcast_to([P, 2 * E])).then_inc(small_in, 16)

            def load_x1(g):
                sp.dma_start(x1[:], x1_d[bass.ds(g * T, T)].rearrange("t p n -> p t n")).then_inc(x1_in, 16)

            def load_keys(g):
                b = g // (NT // T)
                sp.dma_start(mask_row[:], mask_d[bass.ds(b, 1)].broadcast_to([P, CTX])).then_inc(keys_in, 16)
                sp.dma_start(kT[:].rearrange("p c n -> p (c n)"),
                             kT_d[bass.ds(b, 1)].rearrange("a p n -> p (a n)")).then_inc(keys_in, 16)

            def load_values(g):
                b = g // (NT // T)
                sp.dma_start(vm[:], vm_d[bass.ds(b, 1)].rearrange("a p n -> p (a n)")).then_inc(values_in, 16)
                sp.dma_start(vr[:], vr_d[bass.ds(b, 1)].rearrange("a p n -> p (a n)")).then_inc(values_in, 16)

            def body(a, last=False):
                if not last:
                    sp.wait_ge(s_full, a * NH + 1)
                    load_x1(a + 1)
                for t in range(T):
                    if t >= 2 or not isinstance(a, int) or a > 0:
                        sp.wait_ge(mo_a_ready, a * T + (t - 1))
                    sp.dma_start(x1_res[t % 2][:], x1_d[bass.ds(a * T + t, 1)].rearrange("a p n -> p (a n)")) \
                      .then_inc(x1_res_in[t % 2], 16)
                if not last:
                    sp.wait_ge(s_out, a * NH + NH)
                    load_keys(a + 1)
                    sp.wait_ge(mo_a_ready, a * T + T)
                    load_values(a + 1)

            load_x1(0)
            load_keys(0)
            load_small()
            load_values(0)
            gate_weight.load(sp)
            body(0)
            with sp.Fori(0, G - 2) as i:
                body(i + 1)
            body(G - 1, last=True)

        @block.gpsimd
        def _(pool):
            pool.memset(before[:], 1.0).then_inc(constants, 1)
            pool.memset(hid[:], 0.0).then_inc(constants, 1)
            pool.memset(minus_half[:], -0.5).then_inc(constants, 1)
            pool.memset(plus_half[:], 0.5).then_inc(constants, 1)
            pool.memset(probs_end[0][:], 0.0).then_inc(constants, 1)
            pool.memset(probs_end[1][:], 0.0).then_inc(constants, 1)
            pool.memset(eps[:], EPS).then_inc(constants, 1)
            pool.wait_ge(constants, 7)
            pool.affine_select(out=before[:], in_=before[:], compare_op=ALU.is_gt, fill=0.0, base=0,
                               pattern=[[1, E], [-1, E]], channel_multiplier=0).then_inc(constants, 1)
            pool.wait_ge(constants, 8)

            def body(kind, q, a, m, f, i):
                for what, *at in PLANS[kind]:
                    t = at[0] if at else 0
                    if what == "w2":
                        pool.wait_ge(mo_y_ready, f * T + t + 1)
                        k = t % 2
                        pool.tensor_tensor(spread_y[:, k:k + 1], mo_y[:, k, 1:2], eps[:], ALU.add) \
                            .then_inc(spread_y_ready, 1)
                        pool.wait_ge(spread_y_ready, f * T + t + 1)
                        pool.tensor_tensor(rstd_y[:, k:k + 1], spread_y[:, k:k + 1], minus_half[:, 0:1],
                                           ALU.pow).then_inc(rstd_y_ready, 1)
                    elif what == "y":
                        pool.wait_ge(y_ready, f * T + t + 1)
                        pool.sem_inc(passed, 1)
                        pool.dma_start(out_d[bass.ds(f * T + t, 1)].rearrange("a p n -> p (a n)"),
                                       y[t % 2][:]).then_inc(stored[t % 2], 16)
                    elif what == "gate":
                        pool.wait_ge(norm2_ready, m * T + t + 1)
                        pool.tensor_tensor(norm[:, t, :], norm2[:, t, :], plus_half[:], ALU.pow).then_inc(norm_ready, 1)
                    elif what == "skip":
                        product_out(pool, kind, i, "v", t)
                        if f is not None:
                            product_out(pool, kind, i, "w2", t)
                        pool.tensor_tensor(skip[:, t, :], val[:, t, :], x2[:, t, :], ALU.add).then_inc(skip_ready, 1)
                    elif what == "wo":
                        pool.wait_ge(mo_a_ready, a * T + t + 1)
                        pool.tensor_tensor(spread_a[:], mo_a[:, 1:2], eps[:], ALU.add).then_inc(spread_a_ready, 1)
                        pool.wait_ge(spread_a_ready, a * T + t + 1)
                        pool.tensor_tensor(rstd_a[:], spread_a[:], minus_half[:, 0:1], ALU.pow) \
                            .then_inc(rstd_a_ready, 1)
                    elif what == "moments":
                        pool.wait_ge(spread_g_ready, m + 1)
                        pool.tensor_tensor(rstd_g[:], spread_g[:], minus_half[:], ALU.pow).then_inc(rstd_g_ready, 1)

            for k, free in enumerate(stored):
                pool.dma_start(unused[:, k:k + 1], alpha_d.broadcast_to([P, 1])).then_inc(free, 16)
            iterations(pool, body)
            for k in range(2):
                pool.wait_ge(stored[k], 16 * G * T // 2 + 16)

        @block.tensor
        def _(pe):
            pe.wait_ge(constants, 8)

            def body(kind, q, a, m, f, i):
                def tr_bank(*key):
                    k, n = bank_use("tr", kind, i, *key)
                    pe.wait_ge(tr_free[k], n)
                    return trp[k]

                def mm_bank(*key):
                    k, n = bank_use("mm", kind, i, *key)
                    pe.wait_ge(mm_free[k], n)
                    return mmp[k]

                def tr_out(*key):
                    k, n = bank_use("tr", kind, i, *key)
                    pe.wait_ge(tr_free[k], n + 1)

                def turn(src, chunks, *key):
                    out = tr_bank(*key)
                    for c in range(chunks):
                        last = pe.transpose(out[:, c * P:(c + 1) * P], src[:, c * P:(c + 1) * P], ident[:])
                    last.then_inc(tr_full, 1)

                def multiply(left, right, chunks, width, *key):
                    out = mm_bank(*key)
                    for c in range(chunks):
                        last = product(pe, out[:, 0:width], [h[:, c, :] for h in left], [h[:, c, :] for h in right],
                                       c == 0, c == chunks - 1)
                    last.then_inc(mm_full, 1)

                for weight in {"Q": ready[:1], "QAM": [ready[2], gate_weight], "QAMF": ready[3:]}.get(kind, ()):
                    weight.wait_split(pe)
                for what, *numbers in PLANS[kind]:
                    at, *part = numbers or (0,)
                    if what == "x1T":
                        if at == 0:
                            pe.wait_ge(x1_in, 16 * (q + 1))
                        turn(x1[:, at, :], C, what, at)
                    elif what == "xq":
                        if at == 0:
                            tr_out("x1T", T - 2)
                            tr_out("x1T", T - 1)
                        out = mm_bank(what, at)
                        for c in range(C):
                            last = product(pe, out[:], [h[:, c, at * P:(at + 1) * P] for h in wq],
                                           [h[:, c, :] for h in x1T], c == 0, c == C - 1)
                        last.then_inc(mm_full, 1)
                    elif what == "scores":
                        t, half = divmod(at, 2)
                        if at == 0:
                            pe.wait_ge(keys_in, 32 * (a + 1))
                        if at < 2:
                            pe.wait_ge(q_out, a * C + 2 * at + 2)
                        pe.wait_ge(s_out, a * NH + at)
                        for c2 in range(2):
                            c = 2 * half + c2
                            for r in range(4):
                                rows = slice(32 * r, 32 * r + 32)
                                last = pe.matmul(scores[:, r, c2 * CTX:(c2 + 1) * CTX],
                                                 qT[rows, c, t * P:(t + 1) * P], kT[rows, c, :],
                                                 start=True, stop=True, skip_group_check=True)
                        last.then_inc(s_full, 1)
                    elif what == "pT":
                        k = part[0]
                        if k == 0:
                            pe.wait_ge(exp_done, a * (EXPS * NH) + EXPS * (at + 1))
                        out = tr_bank(what, at, k)
                        src, width = (probs[at % 2], CTX) if k < 2 else (probs_end[at % 2], P)
                        for j in range(4 if k < 2 else 2):
                            col = (4 * k % 8 + j) * width
                            last = pe.transpose(out[:, j * P:(j + 1) * P], src[:, col:col + P], ident[:])
                        last.then_inc(tr_full, 1)
                    elif what == "pv":
                        if at == 0:
                            pe.wait_ge(values_in, 32 * (a + 1))
                        out = mm_bank(what, at)
                        half = at % 2
                        tr_out("pT", at, 0)
                        tr_out("pT", at, 1)
                        turned = pT[at % 2]
                        for j in range(HALF):
                            h = half * HALF + j
                            pe.matmul(out[:, j * VB:(j + 1) * VB], turned[:, j, :], vm[:, h * VB:(h + 1) * VB],
                                      start=(j == 0), stop=False, skip_group_check=True)
                        tr_out("pT", at, 2)
                        for four in range(2):
                            w = 4 * VB
                            at_v = (2 * half + four) * w
                            last = pe.matmul(out[:, four * w:(four + 1) * w], turned[:, HALF + four, :],
                                             vr[:, at_v:at_v + w], start=False, stop=True, skip_group_check=True)
                        last.then_inc(mm_full, 1)
                    elif what == "oT":
                        product_out(pe, kind, i, "pv", 2 * at)
                        product_out(pe, kind, i, "pv", 2 * at + 1)
                        turn(o[:], C, what, at)
                    elif what == "wo":
                        if kind == "QAW" and at == 0:
                            ready[1].wait_split(pe)
                        tr_out("oT", at)
                        multiply(oT, wo, C, D, what, at)
                    elif what == "x2T":
                        pe.wait_ge(x2_ready, m * T + (FROM_ONE + at + 1))
                        turn(x2[:, at, :], C, what, at)
                    elif what == "v":
                        tr_out("x2T", at)
                        multiply(x2T, wv, C, D, what, at)
                    elif what == "vT":
                        product_out(pe, kind, i, "v", at)
                        turn(val[:, at, :], C, what, at)
                    elif what == "gate":
                        tr_out("vT", at)
                        multiply(vT, wg, C, GW, what, at)
                    elif what == "hT":
                        pe.wait_ge(hid_ready, f + 1)
                        turn(hid[:, at, :], 3, what, at)
                    elif what == "w2":
                        tr_out("hT", at)
                        multiply(hT[at % 2], w2, 3, D, what, at)

            iterations(pe, body)

        @block.scalar
        def _(act):
            act.wait_ge(small_in, 80)
            act.activation(alpha[:], alpha[:], ACT.Tanh, scale=0.5).then_inc(alpha_tanh, 1)

            def body(kind, q, a, m, f, i):
                def high(out, chunks, *key):
                    k, n = use("tr", kind, i, *key)
                    act.wait_ge(tr_full, n + 1)
                    act.activation(out, trp[k][:, 0:chunks * P].rearrange("p (c n) -> p c n", c=chunks),
                                   ACT.Copy).then_inc(tr_hi, 1)

                def query(chunk):
                    k, n = use("mm", kind, i, "xq", chunk)
                    act.wait_ge(mm_full, n + 1)
                    act.activation(qT[:, chunk, :], mmp[k][:], ACT.Copy).then_inc(mm_free[k], 1)
                    product_out(act, kind, i, "xq", chunk)
                    act.sem_inc(q_out, 1)

                for what, *numbers in PLANS[kind]:
                    at, *part = numbers or (0,)
                    if what == "pT":
                        k, u = use("tr", kind, i, what, at, *part)
                        first, heads = 4 * part[0], 4 if part[0] < 2 else 2
                        act.wait_ge(tr_full, u + 1)
                        act.activation(pT[at % 2][:, first:first + heads, :],
                                       trp[k][:, 0:heads * P].rearrange("p (c n) -> p c n", c=heads), ACT.Copy) \
                           .then_inc(tr_free[k], 1)
                    elif what == "exps":
                        act.wait_ge(s_out, a * NH + at + 1)
                        for j in range(HALF):
                            head = probs[at % 2][:, j * CTX:(j + 1) * CTX]
                            act.activation(head, head, ACT.Exp, bias=shift[:, at % 2, j:j + 1],
                                           scale=float(DH) ** -0.5).then_inc(exp_done, 1)
                        act.wait_ge(exp_done, a * (EXPS * NH) + (EXPS * at + HALF))
                        act.activation(probs_end[at % 2][:].rearrange("p (j k) -> p j k", j=HALF)[:, :, 0:CREM],
                                       probs[at % 2][:].rearrange("p (j k) -> p j k", j=HALF)[:, :, P:CTX],
                                       ACT.Copy).then_inc(exp_done, 1)
                    elif what == "oT":
                        high(oT[0][:], C, what, at)
                    elif what == "vT":
                        high(vT[0][:], C, what, at)
                    elif what == "x2T":
                        high(x2T[0][:], C, what, at)
                    elif what == "hT":
                        high(hT[at % 2][0][:], 3, what, at)
                    elif what == "x1T":
                        high(x1T[0][:, :, at * P:(at + 1) * P], C, what, at)
                    elif what == "xq":
                        query(at)
                    elif what == "split":
                        for c in range(whole[at].chunks):
                            whole[at].take_high(act, c)
                    elif what == "tanh":
                        product_out(act, kind, i, "gate", T - 2)
                        product_out(act, kind, i, "gate", T - 1)
                        act.activation(hid[:, :, 0:E * INNER], gate[:, :, E + E * PV:GW], ACT.Tanh, scale=0.5) \
                           .then_inc(tanh_ready, 1)
                    elif what == "gate_exp":
                        act.wait_ge(s_rel_ready, f + 1)
                        act.activation(s_exp[:], s_rel[:], ACT.Exp).then_inc(s_exp_ready, 1)

            iterations(act, body)

        @block.vector
        def _(dve):
            dve.wait_ge(alpha_tanh, 1)
            dve.wait_ge(constants, 8)
            dve.tensor_scalar(alpha[:], alpha[:], 1.0, 0.5, ALU.add, ALU.mult).then_inc(tables, 1)
            dve.wait_ge(tables, 1)
            for t in (gains, shifts):
                dve.tensor_scalar(t[:, 1, :], t[:, 1, :], alpha[:, 0:1], None, ALU.mult).then_inc(tables, 1)
            dve.wait_ge(tables, 3)

            def body(kind, q, a, m, f, i):
                chain_a = Chain(dve, chain_a_sem, NH + T)
                chain_m = Chain(dve, chain_m_sem, T + 7)
                chain_f = Chain(dve, chain_f_sem, 10 + 6 + T)

                def low(out, hi, chunks, what, at):
                    k, _ = use("tr", kind, i, what, at)
                    high_taken(dve, kind, i, what, at)
                    dve.tensor_tensor(out, trp[k][:, 0:chunks * P].rearrange("p (c n) -> p c n", c=chunks),
                                      hi.bitcast(F32), ALU.subtract).then_inc(tr_free[k], 1)

                def mm_ready(*key):
                    k, n = use("mm", kind, i, *key)
                    dve.wait_ge(mm_full, n + 1)
                    return k, mmp[k]

                def layernorm(out, moments, rstd):
                    return dve.tensor_scalar(out, out, moments, rstd, ALU.subtract, ALU.mult)

                def masked_scores(n):
                    dve.wait_ge(s_full, a * NH + n + 1)
                    dve.sem_inc(passed, 1)
                    for j in range(HALF):
                        at = (j % 2) * CTX
                        dve.tensor_tensor_reduce(probs[n % 2][:, j * CTX:(j + 1) * CTX],
                                                 scores[:, j // 2, at:at + CTX], mask_row[:], 1.0, CUT,
                                                 ALU.add, ALU.max, row_max[:, j:j + 1]).then_inc(s_kept, 1)
                    dve.wait_ge(s_kept, a * (HALF * NH) + HALF * (n + 1))
                    dve.tensor_scalar(shift[:, n % 2, :], row_max[:], -float(DH) ** -0.5, None,
                                      ALU.mult).then_inc(s_out, 1)

                def head_outputs(n):
                    k, bank = mm_ready("pv", n)
                    heads = bank[:, 0:HALF * VB].rearrange("p (j v) -> p j v", v=VB)
                    chain_a.link(dve.reciprocal(inv_sum[:].unsqueeze(2), heads[:, :, DH:VB]), a)
                    dve.tensor_tensor(
                        o[:, (n % 2) * 256:(n % 2 + 1) * 256].rearrange("p (c r d) -> p r c d", c=2, r=4),
                        heads[:, :, 0:DH].rearrange("p (r c) d -> p r c d", c=2),
                        inv_sum[:].rearrange("p (r c) -> p r c", c=2).unsqueeze(3).broadcast_to([P, 4, 2, DH]),
                        ALU.mult).then_inc(mm_free[k], 1)

                def add_attention(t):
                    k, bank = mm_ready("wo", t)
                    if m is not None:
                        dve.wait_ge(skip_ready, m * T + t + 1)
                    dve.wait_ge(x1_res_in[t % 2], 16 * (a * (T // 2) + (t // 2 + 1)))
                    dve.tensor_tensor(x2[:, t, :], bank[:], x1_res[t % 2][:], ALU.add).then_inc(mm_free[k], 1)
                    product_out(dve, kind, i, "wo", t)
                    chain_a.link(dve.bn_stats(stats[:], x2[:, t, :]), a)
                    dve.sem_inc(passed, 1)
                    dve.bn_aggr(mo_a[:], stats[:]).then_inc(mo_a_ready, 1)

                def finish_x2(t):
                    dve.wait_ge(rstd_a_ready, a * T + t + 1)
                    layernorm(x2[:, t, :], mo_a[:, 0:1], rstd_a[:, 0:1]).then_inc(x2_ready, 1)

                def gate_out(t):
                    k, bank = mm_ready("gate", t)
                    dve.tensor_tensor(gate[:, t, :], bank[:, 0:GW], bg[:], ALU.add).then_inc(mm_free[k], 1)
                    product_out(dve, kind, i, "gate", t)
                    pv = gate[:, t, E:E + E * PV]
                    chain_m.link(dve.tensor_tensor(square[:], pv, pv, ALU.mult), m)
                    dve.tensor_reduce(norm2[:, t, :], square[:].rearrange("p (e k) -> p e k", e=E), X, ALU.add) \
                       .then_inc(norm2_ready, 1)

                def value_out(t):
                    k, bank = mm_ready("v", t)
                    dve.tensor_tensor(val[:, t, :], bank[:], bv[:], ALU.add).then_inc(mm_free[k], 1)

                flat = both[:].rearrange("p t a e -> p (t a) e")
                flat_sq = both_sq[:].rearrange("p t a e -> p (t a) e")

                def gate_moments():
                    dve.wait_ge(norm_ready, m * T + T)
                    chain_m.link(dve.tensor_copy(both[:, :, 0, :], gate[:, :, 0:E]), m)
                    chain_m.link(dve.tensor_scalar(both[:, :, 1, :], norm[:], float(PV) ** -0.5, None, ALU.mult), m)
                    chain_m.link(dve.tensor_reduce(mean[:], flat, X, ALU.add), m)
                    chain_m.link(dve.tensor_scalar(mean[:], mean[:], 1.0 / E, None, ALU.mult), m)
                    chain_m.link(dve.tensor_tensor(flat, flat, mean[:].unsqueeze(2).broadcast_to([P, 2 * T, E]),
                                                   ALU.subtract), m)
                    chain_m.link(dve.tensor_tensor(flat_sq, flat, flat, ALU.mult), m)
                    chain_m.link(dve.tensor_reduce(spread_g[:], flat_sq, X, ALU.add), m)
                    dve.tensor_scalar(spread_g[:], spread_g[:], 1.0 / E, EPS, ALU.mult, ALU.add) \
                       .then_inc(spread_g_ready, 1)

                def gate_ranks():
                    dve.wait_ge(rstd_g_ready, f + 1)
                    over_tiles = [P, T, 2, E]
                    chain_f.link(dve.tensor_tensor(flat, flat, rstd_g[:].unsqueeze(2).broadcast_to([P, 2 * T, E]),
                                                   ALU.mult), f)
                    chain_f.link(dve.tensor_tensor(both[:], both[:], gains[:].unsqueeze(1).broadcast_to(over_tiles),
                                                   ALU.mult), f)
                    chain_f.link(dve.tensor_tensor(both[:], both[:], shifts[:].unsqueeze(1).broadcast_to(over_tiles),
                                                   ALU.add), f)
                    chain_f.link(dve.tensor_tensor(s[:], both[:, :, 0, :], both[:, :, 1, :], ALU.add), f)
                    chain_f.link(dve.tensor_reduce(s_max[:], s[:], X, ALU.max), f)
                    dve.tensor_tensor(s_rel[:], s[:], s_max[:].unsqueeze(2).broadcast_to([P, T, E]),
                                      ALU.subtract).then_inc(s_rel_ready, 1)
                    pairs = [P, T, E, E]
                    other, own = s[:].unsqueeze(2).broadcast_to(pairs), s[:].unsqueeze(3).broadcast_to(pairs)
                    chain_f.link(dve.tensor_tensor(beats[:], other, own, ALU.is_gt), f)
                    chain_f.link(dve.tensor_tensor(ties[:], other, own, ALU.is_equal), f)
                    chain_f.link(dve.tensor_tensor(ties[:], ties[:], before[:].unsqueeze(1).broadcast_to(pairs),
                                                   ALU.mult), f)
                    chain_f.link(dve.tensor_tensor(beats[:], beats[:], ties[:], ALU.add), f)
                    chain_f.link(dve.tensor_reduce(rank[:], beats[:], X, ALU.add), f)

                def weigh_hidden():
                    dve.wait_ge(s_exp_ready, f + 1)
                    dve.wait_ge(tanh_ready, f + 1)
                    w = hid[:, :, E * INNER:E * INNER + E]
                    chain_f.link(dve.scalar_tensor_tensor(rank[:], rank[:], 1.5, s_exp[:], ALU.is_lt, ALU.mult), f)
                    chain_f.link(dve.tensor_reduce(den[:], rank[:], X, ALU.add), f)
                    chain_f.link(dve.reciprocal(den[:], den[:]), f)
                    chain_f.link(dve.tensor_tensor(w, rank[:], den[:].unsqueeze(2).broadcast_to([P, T, E]),
                                                   ALU.mult), f)
                    chain_f.link(dve.tensor_scalar(half_w[:], w, 0.5, None, ALU.mult), f)
                    h = hid[:, :, 0:E * INNER]
                    chain_f.link(dve.scalar_tensor_tensor(h, h, 1.0, gate[:, :, E + E * PV:GW],
                                                          ALU.add, ALU.mult), f)
                    dve.tensor_tensor(
                        h.rearrange("p t (e j) -> p t e j", e=E), h.rearrange("p t (e j) -> p t e j", e=E),
                        half_w[:].unsqueeze(3).broadcast_to([P, T, E, INNER]), ALU.mult).then_inc(hid_ready, 1)

                def add_mixture(t):
                    k, bank = mm_ready("w2", t)
                    dve.wait_ge(skip_ready, f * T + t + 1)
                    dve.wait_ge(stored[t % 2], 16 * (f * (T // 2) + t // 2) + 16)
                    dve.tensor_tensor(y[t % 2][:], bank[:], skip[:, t, :], ALU.add).then_inc(mm_free[k], 1)
                    product_out(dve, kind, i, "w2", t)
                    chain_f.link(dve.bn_stats(stats[:], y[t % 2][:]), f)
                    dve.sem_inc(passed, 1)
                    dve.bn_aggr(mo_y[:, t % 2, :], stats[:]).then_inc(mo_y_ready, 1)

                def finish_y(t):
                    dve.wait_ge(rstd_y_ready, f * T + t + 1)
                    layernorm(y[t % 2][:], mo_y[:, t % 2, 0:1], rstd_y[:, t % 2:t % 2 + 1]).then_inc(y_ready, 1)

                for what, *numbers in PLANS[kind]:
                    at = numbers[0] if numbers else 0
                    if what == "scores":
                        masked_scores(at)
                    elif what == "split":
                        for c in range(whole[at].chunks):
                            whole[at].take_low(dve, c)
                    elif what == "pv":
                        head_outputs(at)
                    elif what == "oT":
                        low(oT[1][:], oT[0][:], C, what, at)
                    elif what == "wo":
                        add_attention(at)
                    elif what == "x2":
                        finish_x2(at)
                    elif what == "x2T":
                        low(x2T[1][:], x2T[0][:], C, what, at)
                    elif what == "v":
                        value_out(at)
                    elif what == "vT":
                        low(vT[1][:], vT[0][:], C, what, at)
                    elif what == "gate":
                        gate_out(at)
                    elif what == "moments":
                        gate_moments()
                    elif what == "ranks":
                        gate_ranks()
                    elif what == "weigh":
                        weigh_hidden()
                    elif what == "hT":
                        low(hT[at % 2][1][:], hT[at % 2][0][:], 3, what, at)
                    elif what == "w2":
                        add_mixture(at)
                    elif what == "y":
                        finish_y(at)
                    elif what == "x1T":
                        low(x1T[1][:, :, at * P:(at + 1) * P], x1T[0][:, :, at * P:(at + 1) * P], C, what, at)
                if a is not None:
                    assert chain_a.n == chain_a.per_pass, chain_a.n
                if m is not None:
                    assert chain_m.n == chain_m.per_pass, chain_m.n
                if f is not None:
                    assert chain_f.n == chain_f.per_pass, chain_f.n

            dve.sem_inc(x2_ready, FROM_ONE)
            iterations(dve, body)


def build(nc, a):
    def scratch(name, shape, dt=F32):
        return nc.dram_tensor(name, shape, dt, kind="Internal").ap()

    kT = scratch("ctx_kT", [B, P, C * CTX])
    vm = scratch("ctx_vm", [B, P, HEADS * VB])
    vr = scratch("ctx_vr", [B, P, 4 * 4 * VB])
    mask = scratch("ctx_mask", [B, CTX])
    x1 = scratch("x1", [B * NT, P, D])
    ctx = {"ctxT": a["ctxT"], "wkT": a["xattn_wkT"], "wvT": a["xattn_wvT"], "mask": a["mask"],
           "kT_d": kT, "vm_d": vm, "vr_d": vr, "mask_d": mask}
    with ExitStack() as scope:
        ident = scope.enter_context(nc.sbuf_tensor("ident", [P, P], F32))
        with ExitStack() as first:
            xT = [first.enter_context(nc.sbuf_tensor(f"attn_xT_{part}", [P, C, S], F32R)) for part in ("hi", "lo")]
        ready = [Weight(nc, scope, name, a[key]) for name, key in
                 (("wq", "xattn_wqT"), ("wo", "xattn_woT"), ("wv", "ffn_wvT"), ("w2", "w2T"))]
        rest = 2 * C * S - sum(2 * weight.chunks * D for weight in ready)
        attention_part(nc, xT, rest, ident, ready, ctx, a["x_rows"], a["xT_tiles"], a["attn_wqk"], a["attn_wvT"],
                       a["slope"], x1)
        post_part(nc, ident, ready, a["gate_wT"], x1, kT, vm, vr, mask, a["ffn_bv"], a["gate_b"], a["alpha"],
                  a["gains"], a["shifts"], a["out"])


def kernel(**inputs):
    import numpy as np
    import concourse.bacc as bacc
    from concourse.bass_utils import run_bass_kernel_spmd

    g = {k: np.asarray(v) for k, v in inputs.items()}
    f = {k[len("L0_ffn_"):]: v for k, v in g.items() if k.startswith("L0_ffn_")}
    x = g["x"].reshape(B * NT, P, D)
    experts = E * INNER
    arrays = {
        "x_rows": x,
        "xT_tiles": x.reshape(B * NT, P, C, P).transpose(0, 3, 2, 1).reshape(B * NT, P, D),
        "ctxT": g["ctx_1024"].reshape(B * CTX, D).T,
        "mask": g["mask_Bx1x1xS2_ik0"].reshape(B, CTX),
        "attn_wqk": g["L0_attn_W_qk"],
        "attn_wvT": g["L0_attn_W_v"].T,
        "slope": g["L0_attn_alibi_slope"].reshape(1, 1),
        "xattn_wkT": g["L0_xattn_Wk"].T,
        "xattn_wvT": g["L0_xattn_Wv"].T,
        "xattn_wqT": g["L0_xattn_Wq"].T,
        "xattn_woT": g["L0_xattn_Wo"].T,
        "ffn_wvT": f["Wv"].T,
        "ffn_bv": f["bv"].reshape(1, D),
        "gate_wT": np.concatenate([f["Wg"], f["Wp"].reshape(E * PV, D), f["W1"].reshape(experts, D)]).T,
        "gate_b": np.concatenate([f["bg"], np.zeros(E * PV, np.float32), f["b1"].reshape(experts)]).reshape(1, GW),
        "w2T": np.concatenate([f["W2"].transpose(0, 2, 1).reshape(experts, D), f["b2"],
                               np.zeros((HP - experts - E, D), np.float32)]),
        "alpha": f["alpha"].reshape(1, 1),
        "gains": np.concatenate([f["g_r"], f["g_c"]]).reshape(1, 2 * E),
        "shifts": np.concatenate([f["b_r"], f["b_c"]]).reshape(1, 2 * E),
    }
    arrays = {k: np.ascontiguousarray(v) for k, v in arrays.items()}
    nc = bacc.Bacc("TRN2", target_bir_lowering=False, num_devices=1)
    aps = {k: nc.dram_tensor(k + "_in", v.shape, mybir.dt.from_np(v.dtype), kind="ExternalInput").ap()
           for k, v in arrays.items()}
    aps["out"] = nc.dram_tensor("result", [B * NT, P, D], F32, kind="ExternalOutput").ap()
    build(nc, aps)
    r = run_bass_kernel_spmd(nc, [{k + "_in": v for k, v in arrays.items()}], core_ids=[0])
    return r.results[0]["result"].reshape(B, S, D)
```
